# Optimizing a Trainium2 kernel written in Bass

```python
import numpy as np
import jax
import jax.numpy as jnp

def _softmax(x, axis=-1):
    return jax.nn.softmax(x, axis=axis)

def _gelu(x):
    return jax.nn.gelu(x, approximate=True)

def _silu(x):
    return jax.nn.silu(x)

def _sigmoid(x):
    return jax.nn.sigmoid(x)

def _layernorm(x, axis=-1, eps=1e-05):
    m = jnp.mean(x, axis=axis, keepdims=True)
    v = jnp.var(x, axis=axis, keepdims=True)
    return (x - m) / jnp.sqrt(v + eps)

def _scatter_add(tgt, idx, src, axis=0):
    return tgt.at[idx].add(src)

def _segment_sum(src, seg, n):
    return jax.ops.segment_sum(src, seg, n)
kernel_name = 'mk_decoder_postln_d1_seqx_r4_be45d5'

def setup_inputs(seed: int=0):
    np.random.seed(seed)
    _w = jnp.asarray

    def _rec_inputs():
        import jax
        import jax.numpy as jnp
        _rk = jax.random.key(seed)
        x = 0.002226 + 0.9996 * jax.random.normal(jax.random.fold_in(_rk, 1), (16, 256, 256), jnp.float32)
        _lenS = 256 - jax.random.randint(jax.random.fold_in(_rk, 7), (16,), 0, max(1, 256 // 4) + 1, jnp.int32)
        _lenS2 = 256 - jax.random.randint(jax.random.fold_in(_rk, 8), (16,), 0, max(1, 256 // 4) + 1, jnp.int32)
        _ctx_1024P = jax.random.normal(jax.random.fold_in(_rk, 11), (16, 16, 256), jnp.float32)
        _ctx_1024c = jax.random.dirichlet(jax.random.fold_in(_rk, 511), 0.3 * jnp.ones((16,), jnp.float32), (16, 256))
        _ctx_1024t = jnp.einsum('bsk,bkd->bsd', _ctx_1024c, _ctx_1024P)
        _ctx_1024t = _ctx_1024t * jax.lax.rsqrt(jnp.mean(jnp.square(_ctx_1024t)) + 1e-12) * 0.953939
        ctx_1024 = -0.000125008 + 0.999885 * (_ctx_1024t + 0.3 * jax.random.normal(jax.random.fold_in(_rk, 611), (16, 256, 256), jnp.float32))
        _validS = jnp.arange(256)[None, :] < _lenS[:, None]
        _validS2 = jnp.arange(256)[None, :] < _lenS2[:, None]
        _causal = jnp.tril(jnp.ones((256, 256), dtype=bool))
        mask_BxS2_bk0 = jnp.logical_not(jnp.broadcast_to(_validS2[:, :], (16, 256)))
        return (x, ctx_1024, mask_BxS2_bk0)
    x, ctx_1024, mask_BxS2_bk0 = _rec_inputs()

    def _L0_attn_setup():
        import jax, jax.numpy as jnp
        import numpy as np
        HEADS = 16
        D_MODEL = 256
        EXPANSION = 2
        D_EXP = D_MODEL * EXPANSION
        D_HEAD = D_EXP // HEADS
        B, SEQ = (1, 512)
        LN_EPS = 1e-05
        NEG_BIG = -10000000000.0

        def layer_norm(x, w, b):
            mu = jnp.mean(x, axis=-1, keepdims=True)
            var = jnp.var(x, axis=-1, keepdims=True)
            return (x - mu) * jax.lax.rsqrt(var + LN_EPS) * w + b
        key = jax.random.key(seed)
        ks = jax.random.split(key, 8)
        d_out = 4 * D_EXP + HEADS
        x = jax.random.normal(ks[0], (B, SEQ, D_MODEL), dtype=jnp.float32)
        W_in = 0.02 * jax.random.normal(ks[1], (d_out, D_MODEL), dtype=jnp.float32)
        b_in = jnp.zeros((d_out,), dtype=jnp.float32)
        W_in = W_in.at[4 * D_EXP:].set(0.0)
        b_in = b_in.at[4 * D_EXP:].set(jnp.linspace(-8.0, 8.0, HEADS))
        W_out = 0.02 * (2 * 12) ** (-0.5) * jax.random.normal(ks[2], (D_MODEL, D_EXP), dtype=jnp.float32)
        in_ln_w = jnp.ones((D_MODEL,), dtype=jnp.float32)
        in_ln_b = jnp.zeros((D_MODEL,), dtype=jnp.float32)
        out_ln_w = jnp.ones((D_MODEL,), dtype=jnp.float32)
        out_ln_b = jnp.zeros((D_MODEL,), dtype=jnp.float32)
        smear_factor = jnp.linspace(-6.0, 6.0, HEADS)
        log_scale = jnp.zeros((HEADS,), dtype=jnp.float32)
        return {'x': x, 'W_in': W_in, 'b_in': b_in, 'in_ln_w': in_ln_w, 'in_ln_b': in_ln_b, 'W_out': W_out, 'out_ln_w': out_ln_w, 'out_ln_b': out_ln_b, 'smear_factor': smear_factor, 'log_scale': log_scale}
    _L0_attn_all = _L0_attn_setup()
    _L0_attn_in = {k: v for k, v in _L0_attn_all.items() if k in ('W_in', 'b_in', 'in_ln_w', 'in_ln_b', 'W_out', 'out_ln_w', 'out_ln_b', 'smear_factor', 'log_scale')}
    del _L0_attn_all

    def _L0_xattn_setup():
        import jax, jax.numpy as jnp
        import numpy as np
        EPS = 1e-05

        def layer_norm(x, g, b):
            mu = jnp.mean(x, axis=-1, keepdims=True)
            var = jnp.mean((x - mu) ** 2, axis=-1, keepdims=True)
            return (x - mu) * jax.lax.rsqrt(var + EPS) * g + b
        key = jax.random.key(seed)
        ks = jax.random.split(key, 8)
        b, n, l, D = (8, 1024, 64, 256)
        heads, dim_head = (16, 64)
        inner = heads * dim_head
        x = jax.random.normal(ks[0], (b, n, D), dtype=jnp.float32)
        latents = jax.random.normal(ks[1], (b, l, D), dtype=jnp.float32)
        mask = jax.random.randint(ks[2], (b, n), 0, 2) > 0
        Wq = jax.random.normal(ks[3], (D, inner), dtype=jnp.float32) * D ** (-0.5)
        Wkv = jax.random.normal(ks[4], (D, 2 * inner), dtype=jnp.float32) * D ** (-0.5)
        Wout = jax.random.normal(ks[5], (inner, D), dtype=jnp.float32) * inner ** (-0.5)
        g1 = jnp.ones((D,), jnp.float32)
        b1 = jnp.zeros((D,), jnp.float32)
        g2 = jnp.ones((D,), jnp.float32)
        b2 = jnp.zeros((D,), jnp.float32)
        return {'x': x, 'latents': latents, 'mask': mask, 'g1': g1, 'b1': b1, 'g2': g2, 'b2': b2, 'Wq': Wq, 'Wkv': Wkv, 'Wout': Wout}
    _L0_xattn_all = _L0_xattn_setup()
    _L0_xattn_in = {k: v for k, v in _L0_xattn_all.items() if k in ('g1', 'b1', 'g2', 'b2', 'Wq', 'Wkv', 'Wout')}
    del _L0_xattn_all

    def _L0_ffn_setup():
        import jax, jax.numpy as jnp
        import numpy as np
        D_MODEL, D_FF, N_EXP, TOP_K = (256, 1024, 8, 2)

        def _moe(x, Wr, br, W1, b1, W2, b2):
            B, S, D = x.shape
            xf = x.reshape(-1, D)
            logits = xf @ Wr + br
            probs = jax.nn.softmax(logits, axis=-1)
            top_vals, top_idx = jax.lax.top_k(probs, TOP_K)
            gates = top_vals / jnp.sum(top_vals, axis=-1, keepdims=True)
            h = jax.nn.gelu(jnp.einsum('td,edf->etf', xf, W1) + b1[:, None, :], approximate=False)
            y = jnp.einsum('etf,efd->etd', h, W2) + b2[:, None, :]
            w_te = jnp.sum(jax.nn.one_hot(top_idx, N_EXP, dtype=x.dtype) * gates[..., None], axis=1)
            out = jnp.einsum('te,etd->td', w_te, y)
            return out.reshape(B, S, D)
        key = jax.random.key(seed)
        ks = jax.random.split(key, 8)
        s = 1.0 / np.sqrt(D_MODEL)
        sf = 1.0 / np.sqrt(D_FF)
        return {'x': jax.random.normal(ks[0], (2, 512, D_MODEL), dtype=jnp.float32), 'Wr': jax.random.uniform(ks[1], (D_MODEL, N_EXP), minval=-s, maxval=s, dtype=jnp.float32), 'br': jnp.zeros((N_EXP,), jnp.float32), 'W1': jax.random.uniform(ks[2], (N_EXP, D_MODEL, D_FF), minval=-s, maxval=s, dtype=jnp.float32), 'b1': jnp.zeros((N_EXP, D_FF), jnp.float32), 'W2': jax.random.uniform(ks[3], (N_EXP, D_FF, D_MODEL), minval=-sf, maxval=sf, dtype=jnp.float32), 'b2': jnp.zeros((N_EXP, D_MODEL), jnp.float32)}
    _L0_ffn_all = _L0_ffn_setup()
    _L0_ffn_in = {k: v for k, v in _L0_ffn_all.items() if k in ('Wr', 'br', 'W1', 'b1', 'W2', 'b2')}
    del _L0_ffn_all
    return {'x': x, 'ctx_1024': ctx_1024, 'mask_BxS2_bk0': mask_BxS2_bk0, 'L0_attn_W_in': _L0_attn_in['W_in'], 'L0_attn_b_in': _L0_attn_in['b_in'], 'L0_attn_in_ln_w': _L0_attn_in['in_ln_w'], 'L0_attn_in_ln_b': _L0_attn_in['in_ln_b'], 'L0_attn_W_out': _L0_attn_in['W_out'], 'L0_attn_out_ln_w': _L0_attn_in['out_ln_w'], 'L0_attn_out_ln_b': _L0_attn_in['out_ln_b'], 'L0_attn_smear_factor': _L0_attn_in['smear_factor'], 'L0_attn_log_scale': _L0_attn_in['log_scale'], 'L0_xattn_g1': _L0_xattn_in['g1'], 'L0_xattn_b1': _L0_xattn_in['b1'], 'L0_xattn_g2': _L0_xattn_in['g2'], 'L0_xattn_b2': _L0_xattn_in['b2'], 'L0_xattn_Wq': _L0_xattn_in['Wq'], 'L0_xattn_Wkv': _L0_xattn_in['Wkv'], 'L0_xattn_Wout': _L0_xattn_in['Wout'], 'L0_ffn_Wr': _L0_ffn_in['Wr'], 'L0_ffn_br': _L0_ffn_in['br'], 'L0_ffn_W1': _L0_ffn_in['W1'], 'L0_ffn_b1': _L0_ffn_in['b1'], 'L0_ffn_W2': _L0_ffn_in['W2'], 'L0_ffn_b2': _L0_ffn_in['b2']}

def reference(x, ctx_1024, mask_BxS2_bk0, L0_attn_W_in, L0_attn_b_in, L0_attn_in_ln_w, L0_attn_in_ln_b, L0_attn_W_out, L0_attn_out_ln_w, L0_attn_out_ln_b, L0_attn_smear_factor, L0_attn_log_scale, L0_xattn_g1, L0_xattn_b1, L0_xattn_g2, L0_xattn_b2, L0_xattn_Wq, L0_xattn_Wkv, L0_xattn_Wout, L0_ffn_Wr, L0_ffn_br, L0_ffn_W1, L0_ffn_b1, L0_ffn_W2, L0_ffn_b2):
    import jax
    import jax.numpy as jnp

    def _L0_attn_ref(x, W_in, b_in, in_ln_w, in_ln_b, W_out, out_ln_w, out_ln_b, smear_factor, log_scale):
        import jax, jax.numpy as jnp
        import numpy as np
        HEADS = 16
        D_MODEL = 256
        EXPANSION = 2
        D_EXP = D_MODEL * EXPANSION
        D_HEAD = D_EXP // HEADS
        B, SEQ = (1, 512)
        LN_EPS = 1e-05
        NEG_BIG = -10000000000.0

        def layer_norm(x, w, b):
            mu = jnp.mean(x, axis=-1, keepdims=True)
            var = jnp.var(x, axis=-1, keepdims=True)
            return (x - mu) * jax.lax.rsqrt(var + LN_EPS) * w + b
        b, i, d = x.shape
        xn = layer_norm(x, in_ln_w, in_ln_b)
        proj = xn @ W_in.T + b_in
        q, k, v, p, y = jnp.split(proj, [D_EXP, 2 * D_EXP, 3 * D_EXP, 4 * D_EXP], axis=-1)
        to_heads = lambda t: t.reshape(b, i, HEADS, D_HEAD).transpose(0, 2, 1, 3)
        q, k, v = (to_heads(q), to_heads(k), to_heads(v))
        smear = jax.nn.sigmoid(smear_factor)[None, :, None, None]
        k_prev = jnp.pad(k, ((0, 0), (0, 0), (1, 0), (0, 0)))[:, :, :-1, :]
        k = (1 - smear) * k + smear * k_prev
        s = jnp.exp(log_scale)[None, :, None, None]
        pos = jnp.cumsum(jax.nn.sigmoid(y).transpose(0, 2, 1), axis=-1)
        relpos = pos[..., :, None] - pos[..., None, :]
        causal = jnp.triu(jnp.full((i, i), NEG_BIG, dtype=x.dtype), k=1)
        mask = causal - relpos
        scores = jnp.einsum('bhid,bhjd->bhij', q / s, k / s) / np.sqrt(D_HEAD) + mask
        attn = jax.nn.softmax(scores, axis=-1)
        o = jnp.einsum('bhij,bhjd->bhid', attn, v)
        o = o.transpose(0, 2, 1, 3).reshape(b, i, D_EXP)
        out = jax.nn.silu(p) * o @ W_out.T
        return layer_norm(out, out_ln_w, out_ln_b)

    def _L0_xattn_ref(x, latents, mask, g1, b1, g2, b2, Wq, Wkv, Wout):
        import jax, jax.numpy as jnp
        import numpy as np
        EPS = 1e-05

        def layer_norm(x, g, b):
            mu = jnp.mean(x, axis=-1, keepdims=True)
            var = jnp.mean((x - mu) ** 2, axis=-1, keepdims=True)
            return (x - mu) * jax.lax.rsqrt(var + EPS) * g + b
        heads, dim_head = (16, 64)
        b, n, D = x.shape
        l = latents.shape[1]
        xn = layer_norm(x, g1, b1)
        ln_lat = layer_norm(latents, g2, b2)
        q = ln_lat @ Wq
        kv = jnp.concatenate([xn, ln_lat], axis=1) @ Wkv
        k, v = jnp.split(kv, 2, axis=-1)

        def to_heads(t):
            return t.reshape(t.shape[0], t.shape[1], heads, dim_head).transpose(0, 2, 1, 3)
        q, k, v = (to_heads(q), to_heads(k), to_heads(v))
        scale = 1.0 / np.sqrt(np.sqrt(dim_head)).astype(np.float32)
        weight = jnp.einsum('bhld,bhnd->bhln', q * scale, k * scale)
        full_mask = jnp.concatenate([mask, jnp.ones((b, l), dtype=bool)], axis=1)
        neg = -jnp.finfo(weight.dtype).max
        weight = jnp.where(full_mask[:, None, None, :], weight, neg)
        weight = jax.nn.softmax(weight.astype(jnp.float32), axis=-1).astype(q.dtype)
        out = jnp.einsum('bhln,bhnd->bhld', weight, v)
        out = out.transpose(0, 2, 1, 3).reshape(b, l, heads * dim_head)
        return out @ Wout

    def _L0_ffn_ref(x, Wr, br, W1, b1, W2, b2):
        import jax, jax.numpy as jnp
        import numpy as np
        D_MODEL, D_FF, N_EXP, TOP_K = (256, 1024, 8, 2)

        def _moe(x, Wr, br, W1, b1, W2, b2):
            B, S, D = x.shape
            xf = x.reshape(-1, D)
            logits = xf @ Wr + br
            probs = jax.nn.softmax(logits, axis=-1)
            top_vals, top_idx = jax.lax.top_k(probs, TOP_K)
            gates = top_vals / jnp.sum(top_vals, axis=-1, keepdims=True)
            h = jax.nn.gelu(jnp.einsum('td,edf->etf', xf, W1) + b1[:, None, :], approximate=False)
            y = jnp.einsum('etf,efd->etd', h, W2) + b2[:, None, :]
            w_te = jnp.sum(jax.nn.one_hot(top_idx, N_EXP, dtype=x.dtype) * gates[..., None], axis=1)
            out = jnp.einsum('te,etd->td', w_te, y)
            return out.reshape(B, S, D)
        return _moe(x, Wr, br, W1, b1, W2, b2)
    x = _layernorm(x + _L0_attn_ref(x, L0_attn_W_in, L0_attn_b_in, L0_attn_in_ln_w, L0_attn_in_ln_b, L0_attn_W_out, L0_attn_out_ln_w, L0_attn_out_ln_b, L0_attn_smear_factor, L0_attn_log_scale), axis=-1)
    x = _layernorm(x + _L0_xattn_ref(ctx_1024, x, mask_BxS2_bk0, L0_xattn_g1, L0_xattn_b1, L0_xattn_g2, L0_xattn_b2, L0_xattn_Wq, L0_xattn_Wkv, L0_xattn_Wout), axis=-1)
    x = _layernorm(x + _L0_ffn_ref(x, L0_ffn_Wr, L0_ffn_br, L0_ffn_W1, L0_ffn_b1, L0_ffn_W2, L0_ffn_b2), axis=-1)
    return x

_drawn_inputs = setup_inputs


def setup_inputs(seed=0):
    import zlib

    import numpy as np

    out = dict(_drawn_inputs(seed))
    spreads = {'L0_attn_in_ln_w': (1.0, 0.2),
     'L0_attn_in_ln_b': (0.0, 0.1),
     'L0_attn_out_ln_w': (1.0, 0.2),
     'L0_attn_out_ln_b': (0.0, 0.1),
     'L0_attn_log_scale': (0.0, 0.604),
     'L0_xattn_g1': (1.0, 0.6),
     'L0_xattn_b1': (0.0, 0.407),
     'L0_xattn_g2': (1.0, 0.2),
     'L0_xattn_b2': (0.0, 0.1),
     'L0_ffn_br': (0.0, 0.1),
     'L0_ffn_b1': (0.0, 0.306),
     'L0_ffn_b2': (0.0, 0.1)}
    factors = {}
    for name, (base, spread) in spreads.items():
        noise = np.random.default_rng([zlib.crc32(name.encode()), seed]).standard_normal(out[name].shape)
        drawn = base * np.exp(spread * noise) if base else spread * noise
        out[name] = jnp.asarray(drawn.astype(out[name].dtype))
    for name, factor in factors.items():
        out[name] = (out[name] * factor).astype(out[name].dtype)
    return out
```

```python
from contextlib import ExitStack

import numpy as np

import concourse.bass as bass
from concourse import mybir

F32 = mybir.dt.float32
F32R = mybir.dt.float32r
U8 = mybir.dt.uint8
I32 = mybir.dt.int32
U32 = mybir.dt.uint32
ALU = mybir.AluOpType
ACT = mybir.ActivationFunctionType
AX_X = mybir.AxisListType.X

P = 128
B, S, D = 16, 256, 256
TC = S // P
KC = D // P
EPS = 1e-5

HEADS = 16
DH_A = 32
D_EXP = HEADS * DH_A
EC = D_EXP // P
HPC = P // DH_A
W_COLS = 4 * D_EXP + HEADS
NEG_BIG = -1.0e10

DH_X = 64
INNER = HEADS * DH_X
XC = INNER // P
N_KEYS = 2 * S
NC = N_KEYS // P
X_SCALE = 1.0 / float(np.sqrt(DH_X))
MASKED = -1.0e30

E, F, TOP = 8, 1024, 2
T = B * S
FC = F // P
SLOTS = 256
N_TILES = (T * TOP + E * (SLOTS - 1)) // SLOTS
REGION = T
SPARE = E * REGION
JUNK = SPARE + (N_TILES + 1) * SLOTS
LIST = JUNK + E * REGION + S
SC = SLOTS // P
MAX_TILES = REGION // SLOTS
RING = 3
ROUNDS = N_TILES // RING
assert N_TILES % RING == 0

FILLS = 40
UNITS = HEADS + 2 * HEADS
PROB_RING, PT_RING = 6, 4

(XT, CTXT, YP, QP, KP, VP, PP, X2T, LOGITS, PREFIX, KCTX, WO, VCTX, LNT, QX, KLAT, VLAT, WOX) = (
    0, 1, 2, 3, 5, 7, 9, 11, 12, 13, 14, 18, 20, 24, 26, 30, 34, 38)
LN_OUT, LN_RES, LN_LAT, LN_X, LN_CTX, LN_X2 = 1, 2, 3, 4, 5, 6
LNS = 6
PREFETCH_STEP = 6
ROUTE_A, ROUTE_B, ROUTE_C = 5, 7, 10
LOGIT_STEP, PREFIX_STEP = 3, 8


class Signal:

    def __init__(self, sem, per, start=None):
        self.sem, self.per = sem, per
        self.start = per if start is None else start

    def at(self, b, n):
        return b * self.per + (self.start + n)


def decoder_layer(nc, x, ctx_in, mask, w_in_t, w_out_t, wq, wkv, wout, cols, rows, heads_rows, y_bias, wr,
                  w1, b1, w2, b2, out):
    x2_dram = nc.dram_tensor("x2_rows", (T, D), F32).ap()
    list_dram = nc.dram_tensor("expert_list", (LIST, 1), I32).ap()
    stack = ExitStack()
    with stack:
        def sem(name):
            return stack.enter_context(nc.semaphore(name))

        def sig(name, per, start=None):
            return Signal(sem(name), per, start)

        def keep(name, shape, dt=F32):
            return stack.enter_context(nc.sbuf_tensor(name, shape, dt))

        ident = keep("ident", [P, P])
        gates = keep("gates", [P, B + 1, TC, TOP])
        slots = keep("slots", [P, B + 1, TC, TOP])
        counts = keep("counts", [P, E])
        attention_phase(nc, sem, sig, x, ctx_in, mask, w_in_t, w_out_t, wq, wkv, wout, cols, rows,
                        heads_rows, y_bias, wr, x2_dram, list_dram, ident, gates, slots, counts)
        expert_phase(nc, sem, w1, b1, w2, b2, x2_dram, list_dram, out, ident, gates, slots, counts)


def attention_phase(nc, sem, sig, x, ctx_in, mask, w_in_t, w_out_t, wq, wkv, wout, cols, rows,
                    heads_rows, y_bias, wr, x2_dram, list_dram, ident, gates, slots, counts):
    with ExitStack() as stack:
        def sb(name, shape, dt=F32):
            return stack.enter_context(nc.sbuf_tensor(name, shape, dt))

        def bank(name):
            return stack.enter_context(nc.psum_tensor(name, [P, 512], F32))

        win = sb("win", [P, KC, W_COLS])
        wo = sb("wo", [P, EC, D])
        wq_s = sb("wq_s", [P, KC, INNER])
        wkv_s = sb("wkv_s", [P, KC, 2 * INNER])
        wox = sb("wox", [P, XC, D])
        wr_s = sb("wr_s", [P, KC, E])
        col = sb("col", [P, 24])
        row = sb("row", [P, D_EXP + 2 * D + E])
        smls = sb("smls", [P, 2 * EC])
        by = sb("by", [HEADS, 1])
        inw, inb, bq, bk, bp, g1, be1, g2, be2 = (
            col[:, a:z] for a, z in ((0, 2), (2, 4), (4, 8), (8, 12), (12, 16), (16, 18), (18, 20), (20, 22), (22, 24)))
        bv_row, onw, onb, br_row = (
            row[:, a:z] for a, z in ((0, 512), (512, 768), (768, 1024), (1024, 1032)))
        smear = sb("smear", [P, EC])
        unsmear = sb("unsmear", [P, EC])
        q_scale = sb("q_scale", [P, EC])
        q_bias = sb("q_bias", [P, EC])
        half_bp = sb("half_bp", [P, EC])
        half_by = sb("half_by", [HEADS, 1])
        causal = sb("causal", [P, S])
        before = sb("before", [P, P])
        ones = sb("ones", [P, P])
        head_rows = sb("head_rows", [64, HEADS])
        head_pick = sb("head_pick", [64, HEADS], F32R)
        minus_half = sb("minus_half", [P, TC])
        expert_no = sb("expert_no", [P, E])
        expert_i = sb("expert_i", [P, E], I32)
        expert_base = sb("expert_base", [P, E])
        zero_list = sb("zero_list", [P, JUNK // P], I32)
        x_raw = sb("x_raw", [P, TC, D])
        ctx_raw = sb("ctx_raw", [P, TC, D])
        mask_raw = sb("mask_raw", [P, S // 4], I32)
        mask_add = sb("mask_add", [P, N_KEYS])
        x_res = sb("x_res", [P, TC, D])
        zx = sb("zx", [P, TC, D])
        zctx = sb("zctx", [P, TC, D])
        xn_t = sb("xn_t", [P, KC, S])
        keys_t = sb("keys_t", [P, KC, N_KEYS])
        gate_tanh = sb("gate_tanh", [HEADS, S])
        one_keep = sb("one_keep", [HEADS, S])
        gate_sig = sb("gate_sig", [HEADS, S])
        pos = sb("pos", [HEADS, S])
        pos_parts = sb("pos_parts", [64, S], F32R)
        q_t = sb("q_t", [P, EC, S])
        k_t = sb("k_t", [P, EC, S])
        k_prev = sb("k_prev", [P, EC, S + 1])
        v_a = sb("v_a", [P, TC, D_EXP])
        p_tanh = sb("p_tanh", [P, EC, S])
        p_half = sb("p_half", [P, EC, S])
        silu_p = sb("silu_p", [P, EC, S])
        gated_t = sb("gated_t", [P, EC, S])
        prob = sb("prob", [P, PROB_RING, N_KEYS])
        low = sb("low", [P, UNITS, TC])
        den = sb("den", [P, UNITS, TC])
        rden = sb("rden", [P, UNITS, TC])
        pt = sb("pt", [P, PT_RING, N_KEYS])
        centred = sb("centred", [P, TC, D])
        res1 = sb("res1", [P, TC, D])
        x1 = sb("x1", [P, TC, D])
        zlat = sb("zlat", [P, TC, D])
        kx_t = sb("kx_t", [P, XC, N_KEYS])
        vx = sb("vx", [P, NC, INNER])
        qx_t = sb("qx_t", [P, XC, S])
        ox_t = sb("ox_t", [P, XC, S])
        res2 = sb("res2", [P, TC, D])
        x2 = sb("x2", [P, TC, D])
        x2_t = sb("x2_t", [P, KC, S])
        stat = sb("stat", [P, LNS, TC, 6])
        mv = sb("mv", [P, LNS, TC, 2])
        var_eps = sb("var_eps", [P, LNS, TC])
        rstd = sb("rstd", [P, LNS, TC])
        logit = sb("logit", [P, TC, E])
        others = sb("others", [P, TC, E])
        best = sb("best", [P, TC, TOP])
        is_best = sb("is_best", [P, TC, E])
        rank = sb("rank", [P, TC, E])
        best_rank = sb("best_rank", [P, TC])
        down = sb("down", [P, E])
        margin = sb("margin", [P, TC])
        margin_tanh = sb("margin_tanh", [P, TC])
        chosen = sb("chosen", [P, TC, TOP, E])
        either = sb("either", [P, TC, E])
        place = sb("place", [P, TC, E])
        own_place = sb("own_place", [P, TC, TOP, E])
        slot_f = sb("slot_f", [P, TC, TOP])
        slot_i = sb("slot_i", [P, TC * TOP], I32)
        next_free = sb("next_free", [P, E])
        real = sb("real", [P, 1])
        junk_off = sb("junk_off", [P, 1])
        token_f = sb("token_f", [P, TC])
        token_i = sb("token_i", [P, TC], I32)

        proj = [bank(f"proj{i}") for i in range(2)]
        score = [bank(f"score{i}") for i in range(2)]
        ptb = [bank(f"ptb{i}") for i in range(2)]
        av = [bank(f"av{i}") for i in range(2)]

        in_weights, late_weights = sem("in_weights"), sem("late_weights")
        consts = sem("consts")
        consts_v = sem("consts_v")
        consts_a = sem("consts_a")
        list_zeroed = sem("list_zeroed")
        passed = {e: sem(f"passed_{e}") for e in ("pool", "dve", "sp")}
        x_loaded, ctx_loaded, mask_loaded = sig("x_loaded", 16), sig("ctx_loaded", 16), sig("mask_loaded", 16)
        x2_stored, scattered = sig("x2_stored", 16), sig("scattered", 16 * TC * TOP, start=0)
        scatter_over = sig("scatter_over", 1)
        zx_ready, zctx_ready = sig("zx_ready", 1), sig("zctx_ready", 1)
        mask_ready, x_res_ready = sig("mask_ready", 1), sig("x_res_ready", 1)
        stats_ready, rstd_ready = sig("stats_ready", LNS), sig("rstd_ready", LNS)
        var_ready = sig("var_ready", LNS)
        ln_steps, prefetch_steps = sig("ln_steps", 6), sig("prefetch_steps", 2)
        zlat_ready, x2_ready = sig("zlat_ready", TC), sig("x2_ready", 1)
        proj_filled = sig("proj_filled", FILLS)
        proj_taken = [sig(f"proj_taken{i}", FILLS // 2) for i in range(2)]
        tanh_ready = sig("tanh_ready", 2)
        k_prev_ready = sig("k_prev_ready", 2)
        pos_steps = sig("pos_steps", 4)
        p_half_ready = sig("p_half_ready", 2)
        score_filled, score_taken = sig("score_filled", UNITS), sig("score_taken", UNITS)
        exp_ready, rden_ready, prob_ready = sig("exp_ready", UNITS), sig("rden_ready", UNITS), sig("prob_ready", UNITS)
        pt_filled = sig("pt_filled", UNITS)
        pt_taken = [sig(f"pt_taken{i}", UNITS // 2) for i in range(2)]
        av_done = sig("av_done", UNITS)
        av_taken = [sig(f"av_taken{i}", 6) for i in range(2)]
        route_steps = sig("route_steps", 14)
        margin_steps = sig("margin_steps", 1)
        margin_ready = sig("margin_ready", 1)
        margin_tanh_ready = sig("margin_tanh_ready", 1)
        either_ready, slot_ready = sig("either_ready", 1), sig("slot_ready", 1)
        token_steps = sig("token_steps", 2)
        counts_ready = sem("counts_ready")

        N_CONSTS, N_VCONSTS, N_IN, N_LATE = 13, 5, 16 * 8, 16 * 5

        def transposed_by(u):
            return u + 1 if u < HEADS else HEADS + 2 * ((u - HEADS) // 2) + 2

        block = stack.enter_context(nc.Block())

        @block.sync
        def _(sp):
            def load_next(b):
                nb = b + 1 if isinstance(b, int) else (b + 1) % B
                if not isinstance(b, int):
                    sp.wait_ge(zx_ready.sem, zx_ready.at(b - 1, 1))
                    sp.sem_inc(passed["sp"], 1)
                    sp.wait_ge(x_res_ready.sem, x_res_ready.at(b - 1, 1))
                    sp.sem_inc(passed["sp"], 1)
                sp.dma_start(x_raw[:], x[nb].rearrange("(c p) d -> p c d", p=P)).then_inc(x_loaded.sem, 16)
                if not isinstance(b, int):
                    sp.wait_ge(zctx_ready.sem, zctx_ready.at(b - 1, 1))
                    sp.sem_inc(passed["sp"], 1)
                sp.dma_start(ctx_raw[:], ctx_in[nb].rearrange("(c p) d -> p c d", p=P)).then_inc(ctx_loaded.sem, 16)
                if not isinstance(b, int):
                    sp.wait_ge(mask_ready.sem, mask_ready.at(b, 1))
                    sp.sem_inc(passed["sp"], 1)
                sp.dma_start(mask_raw[:], mask[nb].broadcast_to([P, S // 4])).then_inc(mask_loaded.sem, 16)

            load_next(-1)
            sp.dma_start(col[:], cols).then_inc(in_weights, 16)
            sp.dma_start(row[:], rows.broadcast_to([P, rows.shape[1]])).then_inc(in_weights, 16)
            sp.dma_start(win[:], w_in_t.rearrange("(k p) n -> p k n", p=P)).then_inc(in_weights, 16)
            sp.dma_start(wkv_s[:], wkv.rearrange("(k p) n -> p k n", p=P)).then_inc(late_weights, 16)
            sp.wait_ge(consts, N_CONSTS)
            sp.dma_start(list_dram[0:JUNK, :].rearrange("(p n) a -> p (n a)", p=P), zero_list[:]).then_inc(list_zeroed, 16)
            with sp.Fori(0, B) as b:
                load_next(b)
                sp.wait_ge(x2_ready.sem, x2_ready.at(b, 1))
                sp.sem_inc(passed["sp"], 1)
                sp.dma_start(x2_dram.rearrange("(b c p) d -> b p c d", b=B, p=P)[b], x2[:]).then_inc(x2_stored.sem, 16)
            sp.wait_ge(x2_stored.sem, x2_stored.at(B, 0))
            sp.wait_ge(mask_loaded.sem, mask_loaded.at(B - 1, 16))
            sp.wait_ge(x_loaded.sem, x_loaded.at(B - 1, 16))
            sp.wait_ge(ctx_loaded.sem, ctx_loaded.at(B - 1, 16))

        @block.gpsimd
        def _(pool):
            pool.memset(ident[:], 0.0).then_inc(consts, 1)
            pool.memset(causal[:], 0.0).then_inc(consts, 1)
            pool.memset(ones[:], 1.0).then_inc(consts, 1)
            pool.memset(head_rows[:], 0.0).then_inc(consts, 1)
            pool.memset(minus_half[:], -0.5).then_inc(consts, 1)
            pool.memset(zero_list[:], 0).then_inc(consts, 1)
            pool.memset(mask_add[:], 0.0).then_inc(consts, 1)
            pool.iota(expert_i[:], pattern=[[1, E]], base=0, channel_multiplier=0).then_inc(consts, 1)
            pool.iota(token_i[:], pattern=[[P, TC]], base=-2 * S, channel_multiplier=1).then_inc(consts, 1)
            pool.wait_ge(consts, 9)
            pool.affine_select(out=ident[:], in_=ident[:], compare_op=ALU.not_equal, fill=1.0, base=0,
                               pattern=[[-1, P]], channel_multiplier=1)
            pool.affine_select(out=causal[:], in_=causal[:], compare_op=ALU.is_ge, fill=NEG_BIG, base=P,
                               pattern=[[-1, S]], channel_multiplier=1)
            pool.affine_select(out=before[:], in_=ones[:], compare_op=ALU.is_ge, fill=0.0, base=-1,
                               pattern=[[1, P]], channel_multiplier=-1)
            pool.affine_select(out=head_rows[:], in_=head_rows[:], compare_op=ALU.not_equal, fill=1.0, base=0,
                               pattern=[[-1, HEADS]], channel_multiplier=1).then_inc(consts, 1)
            pool.tensor_copy(token_f[:], token_i[:]).then_inc(consts, 1)
            pool.tensor_copy(expert_no[:], expert_i[:]).then_inc(consts, 1)
            pool.wait_ge(consts, 12)
            pool.affine_select(out=head_rows[:], in_=head_rows[:], compare_op=ALU.not_equal, fill=1.0, base=-32,
                               pattern=[[-1, HEADS]], channel_multiplier=1).then_inc(consts, 1)
            pool.wait_ge(consts, N_CONSTS)

            def reciprocal_root(b, ln):
                pool.wait_ge(stats_ready.sem, stats_ready.at(b, ln))
                pool.sem_inc(passed["pool"], 1)
                pool.tensor_scalar(var_eps[:, ln - 1, :], mv[:, ln - 1, :, 1], EPS, None, ALU.add).then_inc(var_ready.sem, 1)
                pool.wait_ge(var_ready.sem, var_ready.at(b, ln))
                pool.tensor_tensor(rstd[:, ln - 1, :], var_eps[:, ln - 1, :], minus_half[:], ALU.pow).then_inc(rstd_ready.sem, 1)

            def prefetch(b):
                reciprocal_root(b, LN_X)
                if not isinstance(b, int):
                    pool.wait_ge(stats_ready.sem, stats_ready.at(b, LN_RES))
                pool.wait_ge(x_loaded.sem, x_loaded.at(b, 16))
                pool.wait_ge(in_weights, N_IN)
                for c in range(TC):
                    ins = pool.tensor_tensor(x_res[:, c, :], x_raw[:, c, :], onb, ALU.add)
                ins.then_inc(x_res_ready.sem, 1)
                reciprocal_root(b, LN_CTX)

            def spread_mask(b):
                pool.wait_ge(mask_loaded.sem, mask_loaded.at(b - 1, 16))
                pool.wait_ge(score_taken.sem, score_taken.at(b, 0))
                pool.sem_inc(passed["pool"], 1)
                pool.tensor_scalar(mask_add[:, 0:S], mask_raw[:].bitcast(U8), 1.0, -MASKED, ALU.subtract, ALU.mult).then_inc(mask_ready.sem, 1)

            def scatter(b):
                pool.tensor_scalar(token_f[:], token_f[:], float(S), None, ALU.add).then_inc(token_steps.sem, 1)
                pool.wait_ge(token_steps.sem, token_steps.at(b, 1))
                pool.sem_inc(passed["pool"], 1)
                pool.tensor_copy(token_i[:], token_f[:]).then_inc(token_steps.sem, 1)
                pool.wait_ge(token_steps.sem, token_steps.at(b, 2))
                pool.wait_ge(slot_ready.sem, slot_ready.at(b, 1))
                pool.sem_inc(passed["pool"], 1)
                for c in range(TC):
                    for j in range(TOP):
                        n = c * TOP + j
                        pool.indirect_dma_start(
                            list_dram, bass.IndirectOffsetOnAxis(ap=slot_i[:, n:n + 1].bitcast(U32), axis=0),
                            token_i[:, c:c + 1], None).then_inc(scattered.sem, 16)

            pool.sem_inc(token_steps.sem, token_steps.per)
            def scatter_end(b):
                pool.wait_ge(scattered.sem, scattered.at(b, scattered.per))
                pool.sem_inc(scatter_over.sem, 1)

            pool.sem_inc(mask_ready.sem, mask_ready.per)
            pool.sem_inc(scatter_over.sem, scatter_over.per)
            pool.sem_inc(var_ready.sem, LN_X - 1)
            pool.sem_inc(rstd_ready.sem, LN_X - 1)
            prefetch(-1)
            pool.wait_ge(rstd_ready.sem, rstd_ready.at(-1, LN_CTX))
            pool.sem_inc(var_ready.sem, 1)
            pool.sem_inc(rstd_ready.sem, 1)
            pool.wait_ge(list_zeroed, 16)
            with pool.Fori(0, B) as b:
                spread_mask(b)
                scatter(b)
                for ln in (LN_OUT, LN_RES, LN_LAT):
                    reciprocal_root(b, ln)
                prefetch(b)
                scatter_end(b)
                reciprocal_root(b, LN_X2)
            scatter(B)
            scatter_end(B)

        @block.scalar
        def _(act):
            act.dma_start(by[:], y_bias).then_inc(in_weights, 16)
            for hh in range(HPC):
                act.dma_start(smls[DH_A * hh:DH_A * (hh + 1), :],
                              heads_rows[hh:hh + 1, 0:2 * EC].broadcast_to([DH_A, 2 * EC])).then_inc(in_weights, 16)
            act.dma_start(wo[:], w_out_t.rearrange("(m p) n -> p m n", p=P)).then_inc(late_weights, 16)
            act.dma_start(wr_s[:], wr.rearrange("(k p) n -> p k n", p=P)).then_inc(late_weights, 16)
            act.dma_start(wq_s[:], wq.rearrange("(k p) n -> p k n", p=P)).then_inc(late_weights, 16)
            act.dma_start(wox[:], wout.rearrange("(m p) n -> p m n", p=P)).then_inc(late_weights, 16)
            act.wait_ge(in_weights, N_IN)
            nc.scalar.activation(smear[:], smls[:, 0:EC], ACT.Tanh, scale=0.5).then_inc(consts_a, 1)
            nc.scalar.activation(q_scale[:], smls[:, EC:2 * EC], ACT.Exp, scale=-2.0).then_inc(consts_a, 1)
            act.wait_ge(consts_v, N_VCONSTS)

            def taken(ins, f):
                ins.then_inc(proj_taken[f % 2].sem, 1)

            def filled(b, f):
                act.wait_ge(proj_filled.sem, proj_filled.at(b, f + 1))

            def exps(b, u, half=None):
                act.wait_ge(score_taken.sem, score_taken.at(b, u + 1))
                slot = prob[:, u % PROB_RING, :]
                if u < HEADS:
                    for c in range(TC):
                        s = slot[:, 0:P] if c == 0 else slot[:, P:P + S]
                        ins = nc.scalar.activation(s, s, ACT.Exp, bias=low[:, u, c:c + 1], scale=-1.0,
                                                   accum_out=den[:, u, c:c + 1])
                else:
                    ins = nc.scalar.activation(slot, slot, ACT.Exp, bias=low[:, u, 0:1], scale=-1.0,
                                               accum_out=den[:, u, 0:1])
                ins.then_inc(exp_ready.sem, 1)

            act.sem_inc(tanh_ready.sem, tanh_ready.per)
            act.sem_inc(k_prev_ready.sem, k_prev_ready.per)
            act.sem_inc(exp_ready.sem, exp_ready.per)
            act.sem_inc(margin_tanh_ready.sem, margin_tanh_ready.per)

            def take_x2_t(b):
                filled(b, X2T)
                taken(nc.scalar.copy(x2_t[:].rearrange("p k s -> p (k s)"), proj[X2T % 2][:, :]), X2T)

            def gate_margin(b):
                act.wait_ge(margin_ready.sem, margin_ready.at(b, 1))
                nc.scalar.activation(margin_tanh[:], margin[:], ACT.Tanh, scale=0.5).then_inc(margin_tanh_ready.sem, 1)

            with act.Fori(0, B) as b:
                for f, dst, w, bias in ((XT, xn_t[:, :, :], inw, inb), (CTXT, keys_t[:, :, 0:S], g1, be1)):
                    filled(b, f)
                    for k in range(KC):
                        ins = nc.scalar.activation(dst[:, k, :], proj[f % 2][:, k * S:(k + 1) * S], ACT.Identity,
                                                   bias=bias[:, k:k + 1], scale=w[:, k:k + 1])
                    taken(ins, f)
                filled(b, YP)
                taken(nc.scalar.activation(gate_tanh[:], proj[YP % 2][0:HEADS, 0:S], ACT.Tanh, bias=half_by[:, 0:1], scale=0.5), YP)
                for f in (QP, QP + 1):
                    filled(b, f)
                    for i in range(2):
                        m = 2 * (f - QP) + i
                        ins = nc.scalar.activation(q_t[:, m, :], proj[f % 2][:, i * S:(i + 1) * S], ACT.Identity,
                                                   bias=q_bias[:, m:m + 1], scale=q_scale[:, m:m + 1])
                    taken(ins, f)
                for f in (KP, KP + 1):
                    filled(b, f)
                    for i in range(2):
                        m = 2 * (f - KP) + i
                        ins = nc.scalar.activation(k_prev[:, m, 1:S + 1], proj[f % 2][:, i * S:(i + 1) * S], ACT.Identity,
                                                   bias=bk[:, m:m + 1], scale=smear[:, m:m + 1])
                    ins.then_inc(k_prev_ready.sem, 1)
                for f in (PP, PP + 1):
                    act.wait_ge(p_half_ready.sem, p_half_ready.at(b, f - PP + 1))
                    for i in range(2):
                        m = 2 * (f - PP) + i
                        ins = nc.scalar.activation(p_tanh[:, m, :], proj[f % 2][:, i * S:(i + 1) * S], ACT.Tanh,
                                                   bias=half_bp[:, m:m + 1], scale=0.5)
                    ins.then_inc(tanh_ready.sem, 1)
                take_x2_t(b)
                for i in range(HEADS + 3):
                    if i < HEADS:
                        exps(b, i)
                    if i == ROUTE_B:
                        gate_margin(b)
                    if i >= HEADS - 1:
                        f = KCTX + i - (HEADS - 1)
                        filled(b, f)
                        m = 2 * (f - KCTX)
                        taken(nc.scalar.copy(kx_t[:, m:m + 2, 0:S], proj[f % 2][:, :].rearrange("p (i s) -> p i s", i=2)), f)
                for f in range(VCTX, VCTX + 4):
                    filled(b, f)
                    n, h = divmod(f - VCTX, 2)
                    taken(nc.scalar.copy(vx[:, n, 512 * h:512 * (h + 1)], proj[f % 2][:, :]), f)
                for c in range(TC):
                    filled(b, LNT + c)
                    for k in range(KC):
                        ins = nc.scalar.activation(keys_t[:, k, S + c * P:S + (c + 1) * P],
                                                   proj[(LNT + c) % 2][:, k * P:(k + 1) * P], ACT.Identity,
                                                   bias=be2[:, k:k + 1], scale=g2[:, k:k + 1])
                    taken(ins, LNT + c)
                for f in range(KLAT, KLAT + 4):
                    filled(b, f)
                    m = 2 * (f - KLAT)
                    taken(nc.scalar.copy(kx_t[:, m:m + 2, S:N_KEYS], proj[f % 2][:, :].rearrange("p (i s) -> p i s", i=2)), f)
                for i in range(HEADS + 4):
                    if i < HEADS:
                        for c in range(TC):
                            exps(b, HEADS + 2 * i + c)
                    if 2 <= i < HEADS + 2:
                        w = HEADS + 2 * (i - 2)
                        act.wait_ge(pt_filled.sem, pt_filled.at(b, w + 1))
                        act.wait_ge(av_done.sem, av_done.at(b, w - PT_RING + 1))
                        nc.scalar.copy(pt[:, w % PT_RING, :], ptb[w % 2][:, :]).then_inc(pt_taken[w % 2].sem, 1)
                    if i >= 5 and i % 2 == 1:
                        pair = (i - 5) // 2
                        f = EC + pair
                        act.wait_ge(av_done.sem, av_done.at(b, HEADS + 4 * pair + 4))
                        nc.scalar.copy(ox_t[:, pair, :], av[f % 2][:, 0:S]).then_inc(av_taken[f % 2].sem, 1)
            take_x2_t(B)
            gate_margin(B)

        @block.vector
        def _(dve):
            def apart(signal, value):
                dve.wait_ge(signal.sem, value)
                dve.sem_inc(passed["dve"], 1)

            def filled(b, f):
                dve.wait_ge(proj_filled.sem, proj_filled.at(b, f + 1))

            def taken(ins, f):
                ins.then_inc(proj_taken[f % 2].sem, 1)

            dve.memset(pos_parts[:].bitcast(F32), 0.0)
            dve.memset(x2[:], 0.0)
            dve.memset(real[:], 0.0)
            dve.memset(one_keep[:], 1.0)
            dve.memset(junk_off[:], float(JUNK)).then_inc(consts_v, 1)
            dve.wait_ge(consts, N_CONSTS)
            dve.tensor_copy(head_pick[:], head_rows[:])
            dve.tensor_scalar(down[:], expert_no[:], -1.0, float(E), ALU.mult, ALU.add)
            dve.tensor_scalar(expert_base[:], expert_no[:], float(REGION), None, ALU.mult)
            dve.tensor_scalar(next_free[:], expert_no[:], float(REGION), float(JUNK), ALU.mult, ALU.add).then_inc(consts_v, 1)
            dve.wait_ge(consts_a, 2)
            dve.wait_ge(in_weights, N_IN)
            dve.tensor_scalar(unsmear[:], smear[:], -0.5, 0.5, ALU.mult, ALU.add).then_inc(consts_v, 1)
            dve.tensor_scalar(q_scale[:], q_scale[:], 1.0 / float(np.sqrt(DH_A)), None, ALU.mult).then_inc(consts_v, 1)
            dve.tensor_scalar(half_bp[:], bp, 0.5, None, ALU.mult)
            dve.tensor_scalar(half_by[:], by[:], 0.5, None, ALU.mult)
            dve.wait_ge(consts_v, 4)
            dve.tensor_scalar(smear[:], smear[:], 0.5, 0.5, ALU.mult, ALU.add)
            dve.tensor_tensor(q_bias[:], bq, q_scale[:], ALU.mult)
            dve.tensor_tensor(k_prev[:, :, 0], unsmear[:], bk, ALU.mult).then_inc(consts_v, 1)
            dve.sem_inc(stats_ready.sem, LN_X - 1)
            for s in (ln_steps, zlat_ready, x2_ready, x2_stored, pos_steps, p_half_ready, score_taken, rden_ready,
                      prob_ready, route_steps, margin_ready, margin_steps, either_ready, slot_ready):
                dve.sem_inc(s.sem, s.per)

            def stats(b, ln, sources, steps, n):
                for c in range(TC):
                    ins = dve.bn_stats(stat[:, ln - 1, c, :], sources[c])
                ins.then_inc(steps.sem, 1)
                apart(steps, steps.at(b, n))
                for c in range(TC):
                    ins = dve.bn_aggr(mv[:, ln - 1, c, :], stat[:, ln - 1, c, :])
                ins.then_inc(stats_ready.sem, 1)

            def normalise(b, ln, out, src, c):
                return dve.tensor_scalar(out, src, mv[:, ln - 1, c, 0:1], rstd[:, ln - 1, c:c + 1], ALU.subtract, ALU.mult)

            def prefetch(b):
                for n, (ln, loaded, raw, z, ready, f) in enumerate((
                        (LN_X, x_loaded, x_raw, zx, zx_ready, XT), (LN_CTX, ctx_loaded, ctx_raw, zctx, zctx_ready, CTXT))):
                    dve.wait_ge(loaded.sem, loaded.at(b, 16))
                    stats(b, ln, [raw[:, c, :] for c in range(TC)], prefetch_steps, n + 1)
                    dve.wait_ge(rstd_ready.sem, rstd_ready.at(b, ln))
                    if not isinstance(b, int):
                        filled(b, f)
                    for c in range(TC):
                        ins = normalise(b, ln, z[:, c, :], raw[:, c, :], c)
                    ins.then_inc(ready.sem, 1)

            prefetch(-1)
            dve.wait_ge(stats_ready.sem, stats_ready.at(-1, LN_CTX))
            dve.sem_inc(stats_ready.sem, 1)

            def forget_gates(b):
                dve.wait_ge(proj_taken[YP % 2].sem, proj_taken[YP % 2].at(b, YP // 2 + 1))
                dve.tensor_scalar(gate_sig[:], gate_tanh[:], 0.5, 0.5, ALU.mult, ALU.add).then_inc(pos_steps.sem, 1)
                dve.wait_ge(pos_steps.sem, pos_steps.at(b, 1))
                dve.tensor_tensor_scan(pos[:], one_keep[:], gate_sig[:], 0.0, ALU.mult, ALU.add).then_inc(pos_steps.sem, 1)
                dve.wait_ge(pos_steps.sem, pos_steps.at(b, 2))
                dve.tensor_copy(pos_parts[0:HEADS, :], pos[:]).then_inc(pos_steps.sem, 1)
                dve.wait_ge(pos_steps.sem, pos_steps.at(b, 3))
                dve.tensor_tensor(pos_parts[32:32 + HEADS, :], pos[:], pos_parts[0:HEADS, :].bitcast(F32),
                                  ALU.subtract).then_inc(pos_steps.sem, 1)

            def take_projections(b):
                for f in (KP, KP + 1):
                    dve.wait_ge(k_prev_ready.sem, k_prev_ready.at(b, f - KP + 1))
                    for i in range(2):
                        m = 2 * (f - KP) + i
                        ins = dve.scalar_tensor_tensor(out=k_t[:, m, :], in0=proj[f % 2][:, i * S:(i + 1) * S],
                                                       scalar=unsmear[:, m:m + 1], in1=k_prev[:, m, 0:S],
                                                       op0=ALU.mult, op1=ALU.add)
                    taken(ins, f)
                for f in (VP, VP + 1):
                    filled(b, f)
                    taken(dve.tensor_tensor(v_a[:, f - VP, :], proj[f % 2][:, :], bv_row, ALU.add), f)
                for f in (PP, PP + 1):
                    filled(b, f)
                    m = 2 * (f - PP)
                    for i in range(2):
                        ins = dve.tensor_scalar(p_half[:, m + i, :], proj[f % 2][:, i * S:(i + 1) * S],
                                                bp[:, m + i:m + i + 1], 0.5, ALU.add, ALU.mult)
                    ins.then_inc(p_half_ready.sem, 1)
                    dve.wait_ge(tanh_ready.sem, tanh_ready.at(b, f - PP + 1))
                    taken(dve.scalar_tensor_tensor(out=silu_p[:, m:m + 2, :], in0=p_tanh[:, m:m + 2, :], scalar=1.0,
                                                   in1=p_half[:, m:m + 2, :], op0=ALU.add, op1=ALU.mult), f)

            def masked_scores(b, u):
                v = u - PROB_RING
                at = pt_filled.at(b, transposed_by(v)) if v >= 0 else pt_filled.at(b, transposed_by(v + UNITS) - UNITS)
                apart(pt_filled, at)
                apart(score_filled, score_filled.at(b, u + 1))
                slot, bank = prob[:, u % PROB_RING, :], score[u % 2]
                if u < HEADS:
                    dve.tensor_tensor_reduce(slot[:, 0:P], bank[:, 0:P], causal[:, P:S], -1.0, 3.0e38,
                                             ALU.add, ALU.min, low[:, u, 0:1])
                    ins = dve.tensor_tensor_reduce(slot[:, P:P + S], bank[:, S:2 * S], causal[:, :], -1.0, 3.0e38,
                                                   ALU.add, ALU.min, low[:, u, 1:2])
                else:
                    ins = dve.tensor_tensor_reduce(slot, bank[:, :], mask_add[:, :], -X_SCALE, 3.0e38,
                                                   ALU.add, ALU.min, low[:, u, 0:1])
                ins.then_inc(score_taken.sem, 1)

            def one_over_sum(b, u):
                dve.wait_ge(exp_ready.sem, exp_ready.at(b, u + 1))
                n = TC if u < HEADS else 1
                dve.reciprocal(rden[:, u, 0:n], den[:, u, 0:n]).then_inc(rden_ready.sem, 1)

            def probabilities(b, u):
                dve.wait_ge(rden_ready.sem, rden_ready.at(b, u + 1))
                slot = prob[:, u % PROB_RING, :]
                for c in range(TC if u < HEADS else 1):
                    s = slot if u >= HEADS else slot[:, 0:P] if c == 0 else slot[:, P:P + S]
                    ins = dve.tensor_scalar(s, s, rden[:, u, c:c + 1], None, ALU.mult)
                ins.then_inc(prob_ready.sem, 1)

            def take_transposed(b, w, n):
                dve.wait_ge(pt_filled.sem, pt_filled.at(b, w + 1))
                dve.wait_ge(av_done.sem, av_done.at(b, w - PT_RING + 1))
                dve.tensor_copy(pt[:, w % PT_RING, 0:n], ptb[w % 2][:, 0:n]).then_inc(pt_taken[w % 2].sem, 1)

            def best_two(b):
                filled(b, LOGITS)
                taken(dve.tensor_tensor(logit[:], proj[LOGITS % 2][:, 0:TC * E].rearrange("p (c e) -> p c e", c=TC),
                                        br_row.unsqueeze(1).broadcast_to([P, TC, E]), ALU.add), LOGITS)
                apart(proj_taken[LOGITS % 2], proj_taken[LOGITS % 2].at(b, LOGITS // 2 + 1))
                every = [P, TC, E]
                rest = logit
                for j in range(TOP):
                    n = 5 * j
                    dve.tensor_reduce(best[:, :, j], rest[:], AX_X, ALU.max).then_inc(route_steps.sem, 1)
                    dve.wait_ge(route_steps.sem, route_steps.at(b, n + 1))
                    dve.tensor_tensor(is_best[:], rest[:], best[:, :, j].unsqueeze(2).broadcast_to(every), ALU.is_equal).then_inc(route_steps.sem, 1)
                    dve.wait_ge(route_steps.sem, route_steps.at(b, n + 2))
                    dve.tensor_tensor(rank[:], is_best[:], down[:].unsqueeze(1).broadcast_to(every), ALU.mult).then_inc(route_steps.sem, 1)
                    dve.wait_ge(route_steps.sem, route_steps.at(b, n + 3))
                    dve.tensor_reduce(best_rank[:], rank[:], AX_X, ALU.max).then_inc(route_steps.sem, 1)
                    dve.wait_ge(route_steps.sem, route_steps.at(b, n + 4))
                    dve.tensor_tensor(chosen[:, :, j, :], down[:].unsqueeze(1).broadcast_to(every),
                                      best_rank[:].unsqueeze(2).broadcast_to(every), ALU.is_equal).then_inc(route_steps.sem, 1)
                    dve.wait_ge(route_steps.sem, route_steps.at(b, n + 5))
                    if j == 0:
                        dve.scalar_tensor_tensor(out=others[:], in0=chosen[:, :, 0, :], scalar=MASKED, in1=logit[:],
                                                 op0=ALU.mult, op1=ALU.add).then_inc(margin_steps.sem, 1)
                        dve.wait_ge(margin_steps.sem, margin_steps.at(b, 1))
                        rest = others
                dve.tensor_tensor(margin[:], best[:, :, 0], best[:, :, 1], ALU.subtract).then_inc(margin_ready.sem, 1)
                dve.tensor_tensor(either[:], chosen[:, :, 0, :], chosen[:, :, 1, :], ALU.add).then_inc(either_ready.sem, 1)

            def list_places(b):
                dve.wait_ge(margin_tanh_ready.sem, margin_tanh_ready.at(b, 1))
                dve.tensor_scalar(gates[:, b, :, 0], margin_tanh[:], 0.5, 0.5, ALU.mult, ALU.add)
                dve.tensor_scalar(gates[:, b, :, 1], margin_tanh[:], -0.5, 0.5, ALU.mult, ALU.add)
                filled(b, PREFIX)
                dve.tensor_tensor(place[:], proj[PREFIX % 2][:, 0:TC * E].rearrange("p (c e) -> p c e", c=TC),
                                  next_free[:].unsqueeze(1).broadcast_to([P, TC, E]), ALU.add).then_inc(route_steps.sem, 1)
                dve.wait_ge(route_steps.sem, route_steps.at(b, 11))
                taken(dve.scalar_tensor_tensor(out=next_free[:], in0=proj[PREFIX % 2][:, TC * E:(TC + 1) * E],
                                               scalar=real[:, 0:1], in1=next_free[:], op0=ALU.mult, op1=ALU.add), PREFIX)
                dve.tensor_tensor(own_place[:], chosen[:], place[:].unsqueeze(2).broadcast_to([P, TC, TOP, E]),
                                  ALU.mult).then_inc(route_steps.sem, 1)
                dve.wait_ge(route_steps.sem, route_steps.at(b, 12))
                dve.tensor_scalar(next_free[:], next_free[:], junk_off[:, 0:1], None, ALU.subtract)
                dve.tensor_reduce(slot_f[:], own_place[:], AX_X, ALU.add).then_inc(route_steps.sem, 1)
                dve.wait_ge(route_steps.sem, route_steps.at(b, 13))
                dve.wait_ge(scatter_over.sem, scatter_over.at(b, 0))
                dve.tensor_copy(slots[:, b, :, :], slot_f[:])
                dve.tensor_copy(slot_i[:], slot_f[:].rearrange("p c j -> p (c j)")).then_inc(slot_ready.sem, 1)
                dve.memset(real[:], 1.0)
                dve.memset(junk_off[:], 0.0).then_inc(route_steps.sem, 1)

            with dve.Fori(0, B) as b:
                forget_gates(b)
                take_projections(b)
                for i in range(HEADS + 4):
                    if 1 <= i <= HEADS:
                        one_over_sum(b, i - 1)
                    if i < HEADS:
                        masked_scores(b, i)
                    if 1 <= i <= HEADS:
                        probabilities(b, i - 1)
                    if 2 <= i < HEADS + 2:
                        take_transposed(b, i - 2, P + S)
                    if i == ROUTE_A:
                        best_two(b)
                    if i == ROUTE_C:
                        list_places(b)
                    if i >= 7 and (i - 7) % HPC == 0:
                        f = (i - 7) // HPC
                        dve.wait_ge(av_done.sem, av_done.at(b, HPC * f + HPC))
                        dve.tensor_tensor(gated_t[:, f, :], av[f % 2][:, 0:S], silu_p[:, f, :], ALU.mult).then_inc(av_taken[f % 2].sem, 1)
                filled(b, WO + 1)
                stats(b, LN_OUT, [proj[(WO + c) % 2][:, 0:D] for c in range(TC)], ln_steps, 1)
                dve.wait_ge(rstd_ready.sem, rstd_ready.at(b, LN_OUT))
                for c in range(TC):
                    taken(dve.scalar_tensor_tensor(out=centred[:, c, :], in0=proj[(WO + c) % 2][:, 0:D],
                                                   scalar=mv[:, LN_OUT - 1, c, 0:1], in1=onw,
                                                   op0=ALU.subtract, op1=ALU.mult), WO + c)
                for c in range(TC):
                    f = WO + c
                    dve.wait_ge(proj_taken[f % 2].sem, proj_taken[f % 2].at(b, f // 2 + 1))
                    ins = dve.scalar_tensor_tensor(out=res1[:, c, :], in0=centred[:, c, :], scalar=rstd[:, LN_OUT - 1, c:c + 1],
                                                   in1=x_res[:, c, :], op0=ALU.mult, op1=ALU.add)
                ins.then_inc(ln_steps.sem, 1)
                dve.wait_ge(ln_steps.sem, ln_steps.at(b, 2))
                stats(b, LN_RES, [res1[:, c, :] for c in range(TC)], ln_steps, 3)
                dve.wait_ge(rstd_ready.sem, rstd_ready.at(b, LN_RES))
                for c in range(TC):
                    ins = normalise(b, LN_RES, x1[:, c, :], res1[:, c, :], c)
                ins.then_inc(ln_steps.sem, 1)
                dve.wait_ge(ln_steps.sem, ln_steps.at(b, 4))
                stats(b, LN_LAT, [x1[:, c, :] for c in range(TC)], ln_steps, 5)
                dve.wait_ge(rstd_ready.sem, rstd_ready.at(b, LN_LAT))
                for c in range(TC):
                    normalise(b, LN_LAT, zlat[:, c, :], x1[:, c, :], c).then_inc(zlat_ready.sem, 1)
                for f in range(QX, QX + 4):
                    filled(b, f)
                    m = 2 * (f - QX)
                    taken(dve.tensor_copy(qx_t[:, m:m + 2, :], proj[f % 2][:, :].rearrange("p (i s) -> p i s", i=2)), f)
                for f in range(VLAT, VLAT + 4):
                    filled(b, f)
                    n, h = divmod(f - VLAT, 2)
                    taken(dve.tensor_copy(vx[:, TC + n, 512 * h:512 * (h + 1)], proj[f % 2][:, :]), f)
                dve.wait_ge(mask_ready.sem, mask_ready.at(b, 1))
                for i in range(HEADS + 2):
                    us = [HEADS + 2 * (i - 1) + c for c in range(TC)]
                    if 1 <= i <= HEADS:
                        for u in us:
                            one_over_sum(b, u)
                    if i < HEADS:
                        for u in us:
                            masked_scores(b, u + 2)
                    if 1 <= i <= HEADS:
                        for u in us:
                            probabilities(b, u)
                    if 2 <= i:
                        take_transposed(b, HEADS + 2 * (i - 2) + 1, N_KEYS)
                    if i == PREFETCH_STEP:
                        prefetch(b)
                for c in range(TC):
                    filled(b, WOX + c)
                    taken(dve.tensor_tensor(res2[:, c, :], proj[(WOX + c) % 2][:, 0:D], x1[:, c, :], ALU.add), WOX + c)
                for c in range(TC):
                    f = WOX + c
                    dve.wait_ge(proj_taken[f % 2].sem, proj_taken[f % 2].at(b, f // 2 + 1))
                stats(b, LN_X2, [res2[:, c, :] for c in range(TC)], ln_steps, 6)
                dve.wait_ge(rstd_ready.sem, rstd_ready.at(b, LN_X2))
                dve.wait_ge(x2_stored.sem, x2_stored.at(b, 0))
                for c in range(TC):
                    ins = normalise(b, LN_X2, x2[:, c, :], res2[:, c, :], c)
                ins.then_inc(x2_ready.sem, 1)
            best_two(B)
            list_places(B)
            dve.wait_ge(route_steps.sem, route_steps.at(B, 14))
            dve.tensor_tensor(counts[:], next_free[:], expert_base[:], ALU.subtract).then_inc(counts_ready, 1)

        @block.tensor
        def _(pe):
            pe.wait_ge(consts, N_CONSTS)
            pe.wait_ge(consts_v, N_VCONSTS)
            pe.wait_ge(in_weights, N_IN)
            for s in (proj_filled, *proj_taken, score_filled, pt_filled, *pt_taken, av_done, *av_taken):
                pe.sem_inc(s.sem, s.per)
            matmul, transpose = nc.tensor.matmul, nc.tensor.transpose

            def free(b, f):
                pe.wait_ge(proj_taken[f % 2].sem, proj_taken[f % 2].at(b, f // 2))
                return proj[f % 2]

            def in_sbuf(b, f):
                pe.wait_ge(proj_taken[f % 2].sem, proj_taken[f % 2].at(b, f // 2 + 1))

            def full(ins):
                ins.then_inc(proj_filled.sem, 1)

            def project(out, lhs, rhs, chunks):
                for k in range(chunks):
                    ins = matmul(out, lhs(k), rhs(k), start=(k == 0), stop=(k == chunks - 1))
                return ins

            def transposed(b, f, z, ready, value):
                bk_ = free(b, f)
                pe.wait_ge(ready.sem, value)
                for k in range(KC):
                    for c in range(TC):
                        ins = transpose(bk_[:, k * S + c * P:k * S + (c + 1) * P], z[:, c, k * P:(k + 1) * P], ident[:])
                full(ins)

            def chunk_pairs(b, f0, n, weights, col0, rhs):
                for f in range(f0, f0 + n):
                    bk_ = free(b, f)
                    for i in range(2):
                        m0 = col0 + (2 * (f - f0) + i) * P
                        ins = project(bk_[:, i * S:(i + 1) * S], lambda k: weights[:, k, m0:m0 + P], rhs, KC)
                    full(ins)

            def scores_a(b, u):
                pe.wait_ge(score_taken.sem, score_taken.at(b, u - 1))
                if u == 0:
                    pe.wait_ge(pos_steps.sem, pos_steps.at(b, 4))
                m, hh = divmod(u, HPC)
                if u % (2 * HPC) == 0:
                    in_sbuf(b, KP + m // 2)
                r = slice(DH_A * hh, DH_A * (hh + 1))
                pick = head_pick[0:48, u:u + 1].broadcast_to([48, P])
                for c in range(TC):
                    keys = (c + 1) * P
                    matmul(score[u % 2][:, c * S:(c + 1) * S], pick, pos_parts[0:48, :], start=True, stop=False)
                    ins = matmul(score[u % 2][:, c * S:c * S + keys], q_t[r, m, c * P:(c + 1) * P], k_t[r, m, 0:keys],
                                 start=False, stop=True)
                ins.then_inc(score_filled.sem, 1)

            def transposes_a(b, u):
                pe.wait_ge(pt_taken[u % 2].sem, pt_taken[u % 2].at(b, u // 2))
                pe.wait_ge(prob_ready.sem, prob_ready.at(b, u + 1))
                for i in range(3):
                    ins = transpose(ptb[u % 2][:, i * P:(i + 1) * P], prob[:, u % PROB_RING, i * P:(i + 1) * P], ident[:])
                ins.then_inc(pt_filled.sem, 1)

            def values_a(b, u):
                f, hh = divmod(u, HPC)
                if u == 0:
                    in_sbuf(b, VP)
                    in_sbuf(b, VP + 1)
                if hh == 0:
                    pe.wait_ge(av_taken[f % 2].sem, av_taken[f % 2].at(b, f // 2))
                pe.wait_ge(pt_taken[u % 2].sem, pt_taken[u % 2].at(b, u // 2 + 1))
                o = av[f % 2][DH_A * hh:DH_A * (hh + 1), 0:S]
                dims = slice(DH_A * u, DH_A * (u + 1))
                matmul(o, v_a[:, 0, dims], pt[:, u % PT_RING, 0:S], start=True, stop=False)
                matmul(o[:, P:S], v_a[:, 1, dims], pt[:, u % PT_RING, S:S + P], start=False, stop=True).then_inc(av_done.sem, 1)

            def scores_x(b, h, c):
                u = HEADS + 2 * h + c
                m, r = h // 2, slice(DH_X * (h % 2), DH_X * (h % 2 + 1))
                pe.wait_ge(score_taken.sem, score_taken.at(b, u - 1))
                if h % 4 == 0 and c == 0:
                    in_sbuf(b, KLAT + m // 2)
                matmul(score[u % 2][:, :], qx_t[r, m, c * P:(c + 1) * P], kx_t[r, m, :], start=True, stop=True).then_inc(score_filled.sem, 1)

            def transposes_x(b, h):
                for half in range(2):
                    w = HEADS + 2 * h + half
                    pe.wait_ge(pt_taken[w % 2].sem, pt_taken[w % 2].at(b, w // 2))
                    if half == 0:
                        pe.wait_ge(prob_ready.sem, prob_ready.at(b, HEADS + 2 * h + TC))
                    for nn in range(2):
                        n = 2 * half + nn
                        for c in range(TC):
                            ins = transpose(ptb[w % 2][:, nn * S + c * P:nn * S + (c + 1) * P],
                                            prob[:, (HEADS + 2 * h + c) % PROB_RING, n * P:(n + 1) * P], ident[:])
                    ins.then_inc(pt_filled.sem, 1)

            def values_x(b, h):
                f, r = EC + h // 2, slice(DH_X * (h % 2), DH_X * (h % 2 + 1))
                if h == 0:
                    in_sbuf(b, VLAT + 2)
                    in_sbuf(b, VLAT + 3)
                if h % 2 == 0:
                    pe.wait_ge(av_taken[f % 2].sem, av_taken[f % 2].at(b, f // 2))
                for half in range(2):
                    w = HEADS + 2 * h + half
                    pe.wait_ge(pt_taken[w % 2].sem, pt_taken[w % 2].at(b, w // 2 + 1))
                    for nn in range(2):
                        n = 2 * half + nn
                        ins = matmul(av[f % 2][r, 0:S], vx[:, n, DH_X * h:DH_X * (h + 1)],
                                     pt[:, w % PT_RING, nn * S:(nn + 1) * S], start=(n == 0), stop=(n == NC - 1))
                    ins.then_inc(av_done.sem, 1)

            def x2_transposed(b):
                transposed(b, X2T, x2, x2_ready, x2_ready.at(b, 0))

            def logits(b):
                bk_ = free(b, LOGITS)
                in_sbuf(b, X2T)
                for c in range(TC):
                    ins = project(bk_[:, c * E:(c + 1) * E], lambda k: x2_t[:, k, c * P:(c + 1) * P],
                                  lambda k: wr_s[:, k, :], KC)
                full(ins)

            def prefixes(b):
                bk_ = free(b, PREFIX)
                pe.wait_ge(either_ready.sem, either_ready.at(b, 1))
                matmul(bk_[:, 0:E], before[:], either[:, 0, :], start=True, stop=True)
                matmul(bk_[:, E:2 * E], ones[:], either[:, 0, :], start=True, stop=False)
                matmul(bk_[:, E:2 * E], before[:], either[:, 1, :], start=False, stop=True)
                matmul(bk_[:, 2 * E:3 * E], ones[:], either[:, 0, :], start=True, stop=False)
                full(matmul(bk_[:, 2 * E:3 * E], ones[:], either[:, 1, :], start=False, stop=True))

            def ctx_keys(k):
                return keys_t[:, k, 0:S]

            def lat_keys(k):
                return keys_t[:, k, S:N_KEYS]

            def values_of(b, f0, n0):
                for f in range(f0, f0 + 4):
                    n, h = divmod(f - f0, 2)
                    n += n0
                    bk_ = free(b, f)
                    full(project(bk_[:, :], lambda k: keys_t[:, k, n * P:(n + 1) * P],
                                 lambda k: wkv_s[:, k, INNER + 512 * h:INNER + 512 * (h + 1)], KC))

            with pe.Fori(0, B) as b:
                transposed(b, XT, zx, zx_ready, zx_ready.at(b - 1, 1))
                transposed(b, CTXT, zctx, zctx_ready, zctx_ready.at(b - 1, 1))
                bk_ = free(b, YP)
                in_sbuf(b, XT)
                full(project(bk_[0:HEADS, 0:S], lambda k: win[:, k, 4 * D_EXP:W_COLS], lambda k: xn_t[:, k, :], KC))
                chunk_pairs(b, QP, 2, win, 0, lambda k: xn_t[:, k, :])
                chunk_pairs(b, KP, 2, win, D_EXP, lambda k: xn_t[:, k, :])
                for f in (VP, VP + 1):
                    bk_ = free(b, f)
                    full(project(bk_[:, :], lambda k: xn_t[:, k, (f - VP) * P:(f - VP + 1) * P],
                                 lambda k: win[:, k, 2 * D_EXP:3 * D_EXP], KC))
                chunk_pairs(b, PP, 2, win, 3 * D_EXP, lambda k: xn_t[:, k, :])
                pe.wait_ge(late_weights, N_LATE)
                x2_transposed(b)
                for i in range(HEADS + 3):
                    if i == LOGIT_STEP:
                        logits(b)
                    if i == PREFIX_STEP:
                        prefixes(b)
                    if i < HEADS:
                        scores_a(b, i)
                    if 2 <= i < HEADS + 2:
                        transposes_a(b, i - 2)
                    if i >= HEADS - 1:
                        if i == HEADS - 1:
                            in_sbuf(b, CTXT)
                        n = i - (HEADS - 1)
                        chunk_pairs(b, KCTX + n, 1, wkv_s, 2 * n * P, ctx_keys)
                    if i >= 3:
                        values_a(b, i - 3)
                for f in range(EC):
                    pe.wait_ge(av_taken[f % 2].sem, av_taken[f % 2].at(b, f // 2 + 1))
                for c in range(TC):
                    bk_ = free(b, WO + c)
                    full(project(bk_[:, 0:D], lambda k: gated_t[:, k, c * P:(c + 1) * P], lambda k: wo[:, k, :], EC))
                values_of(b, VCTX, 0)
                for c in range(TC):
                    bk_ = free(b, LNT + c)
                    pe.wait_ge(zlat_ready.sem, zlat_ready.at(b, c + 1))
                    for k in range(KC):
                        ins = transpose(bk_[:, k * P:(k + 1) * P], zlat[:, c, k * P:(k + 1) * P], ident[:])
                    full(ins)
                for c in range(TC):
                    in_sbuf(b, LNT + c)
                chunk_pairs(b, QX, 4, wq_s, 0, lat_keys)
                chunk_pairs(b, KLAT, 4, wkv_s, 0, lat_keys)
                values_of(b, VLAT, TC)
                for i in range(HEADS + 3):
                    if i < HEADS:
                        for c in range(TC):
                            scores_x(b, i, c)
                    if 2 <= i < HEADS + 2:
                        transposes_x(b, i - 2)
                    if i >= 3:
                        values_x(b, i - 3)
                for f in range(EC, EC + XC):
                    if f >= EC + XC - 2:
                        pe.wait_ge(av_taken[f % 2].sem, av_taken[f % 2].at(b, f // 2 + 1))
                for c in range(TC):
                    bk_ = free(b, WOX + c)
                    full(project(bk_[:, 0:D], lambda k: ox_t[:, k, c * P:(c + 1) * P], lambda k: wox[:, k, :], XC))
            for i in range(2):
                pe.wait_ge(proj_taken[i].sem, proj_taken[i].at(B, 0))
                pe.sem_inc(proj_taken[i].sem, (X2T + 1 - i) // 2)
            pe.sem_inc(proj_filled.sem, X2T)
            x2_transposed(B)
            logits(B)
            prefixes(B)


def expert_phase(nc, sem, w1, b1, w2, b2, x2_dram, list_dram, out, ident, gates, slots, counts):
    y_dram = nc.dram_tensor("expert_rows", (N_TILES * SLOTS, D), F32).ap()
    with ExitStack() as stack:
        def sb(name, shape, dt=F32):
            return stack.enter_context(nc.sbuf_tensor(name, shape, dt))

        def bank(name):
            return stack.enter_context(nc.psum_tensor(name, [P, 512], F32))

        def sig(name, per, start=None):
            return Signal(sem(name), per, RING * per if start is None else start)

        tile_i = sb("tile_i", [P, N_TILES], I32)
        tile_no = sb("tile_no", [P, N_TILES])
        bound_i = sb("bound_i", [P, MAX_TILES], I32)
        bound = sb("bound", [P, MAX_TILES])
        has_tile = sb("has_tile", [P, E, MAX_TILES])
        tiles_of = sb("tiles_of", [P, E])
        one_e = sb("one_e", [P, E])
        last_tile = sb("last_tile", [P, E])
        is_past = sb("is_past", [P, N_TILES, E])
        past_tiles = sb("past_tiles", [P, N_TILES, E])
        expert_f = sb("expert_f", [P, N_TILES])
        first_f = sb("first_f", [P, N_TILES])
        expert_rows_f = sb("expert_rows_f", [P, N_TILES])
        tile_base = sb("tile_base", [P, N_TILES], I32)
        tile_expert = sb("tile_expert", [P, N_TILES], I32)
        half_e = sb("half_e", [P, TC])
        region_i = sb("region_i", [P, E], I32)
        region = sb("region", [P, E])
        closing = sb("closing", [P, E])
        in_region = sb("in_region", [P, B * TC * TOP, E])
        gaps = sb("gaps", [P, B * TC * TOP, E])
        gap = sb("gap", [P, B * TC * TOP])
        row_no = sb("row_no", [P, B, TC, TOP], I32)
        w1_s = [sb(f"w1_s{i}", [P, KC, F]) for i in range(RING)]
        w2_s = [sb(f"w2_s{i}", [P, FC, D]) for i in range(RING)]
        b1_s = [sb(f"b1_s{i}", [P, FC]) for i in range(RING)]
        b2_s = [sb(f"b2_s{i}", [P, D]) for i in range(RING)]
        tokens = [sb(f"tokens{i}", [P, SC], I32) for i in range(RING)]
        xg = [sb(f"xg{i}", [P, SC, D]) for i in range(RING)]
        xg_t = [sb(f"xg_t{i}", [P, KC, SLOTS]) for i in range(RING)]
        h_t = [sb(f"h_t{i}", [P, FC, SLOTS]) for i in range(RING)]
        y_s = [sb(f"y_s{i}", [P, SC, D]) for i in range(RING)]
        own_slots = [sb(f"own_slots{q}", [P, TC, TOP], I32) for q in range(2)]
        yb = [sb(f"yb{q}", [P, TC, TOP, D]) for q in range(2)]
        xb = [sb(f"xb{q}", [P, TC, D]) for q in range(2)]
        half_sum = sb("half_sum", [P, TC, D])
        res3 = sb("res3", [P, TC, D])
        stat3 = sb("stat3", [P, TC, 6])
        mv3 = sb("mv3", [P, TC, 2])
        var3 = sb("var3", [P, TC])
        rstd3 = sb("rstd3", [P, TC])
        ob = [sb(f"ob{q}", [P, TC, D]) for q in range(2)]
        xt_bank = bank("xt_bank")
        h_bank = [bank(f"h_bank{i}") for i in range(FC // 2)]
        y_bank = [bank(f"y_bank{i}") for i in range(RING)]

        consts = sem("tile_consts")
        plan = sem("tile_plan")
        passed = {e: sem(f"passed3_{e}") for e in ("pool", "dve", "sp")}
        w1_loaded = [sig(f"w1_loaded{i}", 32, 0) for i in range(RING)]
        w2_loaded = [sig(f"w2_loaded{i}", 32, 0) for i in range(RING)]
        tokens_loaded = [sig(f"tokens_loaded{i}", 16, 0) for i in range(RING)]
        gathered = [sig(f"gathered{i}", 16 * SC, 0) for i in range(RING)]
        y_stored = [Signal(sem(f"y_stored{i}"), 16, 16) for i in range(RING)]
        xt_filled, xt_taken = sig("xt_filled", 1), sig("xt_taken", 1)
        h_filled, h_taken = sig("h_filled", FC // 2), sig("h_taken", FC // 2)
        y_filled, y_taken = sig("y_filled", 1), sig("y_taken", 1)
        slots_ready = Signal(sem("slots_ready"), 1, 2)
        rows_back = [sig(f"rows_back{q}", 16 * TC * TOP, 0) for q in range(2)]
        xb_loaded = [sig(f"xb_loaded{q}", 16, 0) for q in range(2)]
        out_stored = [Signal(sem(f"out_stored{q}"), 16, 16) for q in range(2)]
        sum_steps = Signal(sem("sum_steps"), 3, 6)
        stats3 = Signal(sem("stats3"), 1, 2)
        var3_ready, rstd3_ready = Signal(sem("var3_ready"), 1, 2), Signal(sem("rstd3_ready"), 1, 2)
        ob_ready = Signal(sem("ob_ready"), 1, 2)
        N_PLAN = 10

        block = stack.enter_context(nc.Block())

        @block.sync
        def _(sp):
            def pass_wait(s, value):
                if not (isinstance(value, int) and value <= 0):
                    sp.wait_ge(s.sem, value)
                    sp.sem_inc(passed["sp"], 1)

            def load(r, i):
                t = r * RING + i
                base = sp.value_load(tile_base[0:1, bass.ds(t, 1)], min_val=0, max_val=JUNK - SLOTS)
                e = sp.value_load(tile_expert[0:1, bass.ds(t, 1)], min_val=0, max_val=E - 1)
                pass_wait(gathered[i], gathered[i].at(r, 0))
                sp.dma_start(tokens[i][:], list_dram[bass.ds(base, SLOTS), :].rearrange("(p c) a -> p (c a)", p=P)).then_inc(tokens_loaded[i].sem, 16)
                pass_wait(y_taken, y_taken.at(t - RING, 1) if not isinstance(r, int) else 0)
                sp.dma_start(w1_s[i][:], w1[e].rearrange("(k p) f -> p k f", p=P)).then_inc(w1_loaded[i].sem, 16)
                sp.dma_start(b1_s[i][:], b1[e]).then_inc(w1_loaded[i].sem, 16)
                sp.dma_start(w2_s[i][:], w2[e].rearrange("(k p) d -> p k d", p=P)).then_inc(w2_loaded[i].sem, 16)
                sp.dma_start(b2_s[i][:], b2[e].broadcast_to([P, D])).then_inc(w2_loaded[i].sem, 16)

            def store(r, i):
                t = r * RING + i
                pass_wait(y_taken, y_taken.at(t, 1))
                sp.dma_start(y_dram.rearrange("(t p c) d -> t p c d", p=P, c=SC)[t], y_s[i][:]).then_inc(y_stored[i].sem, 16)

            sp.wait_ge(plan, N_PLAN)
            for i in range(RING):
                load(0, i)
            store(0, 0)
            with sp.Fori(1, ROUNDS) as r:
                for i in range(RING):
                    load(r, i)
                    if i == RING - 1:
                        store(r, 0)
                    else:
                        store(r - 1, i + 1)
            for i in range(1, RING):
                store(ROUNDS - 1, i)

            x2_rows, out_rows = (a.rearrange("(b c p) d -> b p c d", b=B, p=P) for a in (x2_dram, out))

            def load_x2(r, q):
                b = 2 * r + q
                if not isinstance(r, int):
                    pass_wait(sum_steps, sum_steps.at(b - 2, 2))
                sp.dma_start(xb[q][:], x2_rows[b]).then_inc(xb_loaded[q].sem, 16)

            def store_out(r, q):
                b = 2 * r + q
                pass_wait(ob_ready, ob_ready.at(b, 1))
                sp.dma_start(out_rows[b], ob[q][:]).then_inc(out_stored[q].sem, 16)

            load_x2(0, 0)
            load_x2(0, 1)
            with sp.Fori(1, B // 2) as r:
                for q in range(2):
                    store_out(r - 1, q)
                    load_x2(r, q)
            for q in range(2):
                store_out(B // 2 - 1, q)
            for q in range(2):
                sp.wait_ge(out_stored[q].sem, out_stored[q].at(B // 2, 0))

        @block.gpsimd
        def _(pool):
            pool.iota(tile_i[:], pattern=[[1, N_TILES]], base=0, channel_multiplier=0).then_inc(consts, 1)
            pool.iota(bound_i[:], pattern=[[SLOTS, MAX_TILES]], base=0, channel_multiplier=0).then_inc(consts, 1)
            pool.memset(half_e[:], -0.5).then_inc(consts, 1)
            pool.iota(region_i[:], pattern=[[REGION, E]], base=0, channel_multiplier=0).then_inc(consts, 1)
            pool.wait_ge(consts, 4)
            pool.tensor_copy(region[:], region_i[:]).then_inc(consts, 1)
            pool.tensor_copy(tile_no[:], tile_i[:]).then_inc(consts, 1)
            pool.tensor_copy(bound[:], bound_i[:]).then_inc(consts, 1)
            pool.sem_inc(var3_ready.sem, var3_ready.start)
            pool.sem_inc(rstd3_ready.sem, rstd3_ready.start)

            def gather(r, i):
                t = r * RING + i
                pool.wait_ge(tokens_loaded[i].sem, tokens_loaded[i].at(r, 16))
                pool.sem_inc(passed["pool"], 1)
                pool.wait_ge(xt_filled.sem, xt_filled.at(t - RING, 1))
                pool.sem_inc(passed["pool"], 1)
                for c in range(SC):
                    pool.indirect_dma_start(xg[i][:, c, :], None, x2_dram, bass.IndirectOffsetOnAxis(
                        ap=tokens[i][:, c:c + 1].bitcast(U32), axis=0)).then_inc(gathered[i].sem, 16)

            with pool.Fori(0, ROUNDS) as r:
                for i in range(RING):
                    gather(r, i)
            for i in range(RING):
                pool.wait_ge(y_stored[i].sem, y_stored[i].at(ROUNDS, 0))

            def rows(r, q):
                b = 2 * r + q
                pool.wait_ge(slots_ready.sem, slots_ready.at(b, 1))
                pool.sem_inc(passed["pool"], 1)
                pool.wait_ge(sum_steps.sem, sum_steps.at(b - 2, 2))
                pool.sem_inc(passed["pool"], 1)
                for c in range(TC):
                    for j in range(TOP):
                        pool.indirect_dma_start(yb[q][:, c, j, :], None, y_dram, bass.IndirectOffsetOnAxis(
                            ap=own_slots[q][:, c, j:j + 1].bitcast(U32), axis=0)).then_inc(rows_back[q].sem, 16)

            def reciprocal_root(b):
                pool.wait_ge(stats3.sem, stats3.at(b, 1))
                pool.sem_inc(passed["pool"], 1)
                pool.tensor_scalar(var3[:], mv3[:, :, 1], EPS, None, ALU.add).then_inc(var3_ready.sem, 1)
                pool.wait_ge(var3_ready.sem, var3_ready.at(b, 1))
                pool.tensor_tensor(rstd3[:], var3[:], half_e[:], ALU.pow).then_inc(rstd3_ready.sem, 1)

            rows(0, 0)
            with pool.Fori(0, B // 2 - 1) as r:
                rows(r, 1)
                reciprocal_root(2 * r)
                rows(r + 1, 0)
                reciprocal_root(2 * r + 1)
            rows(B // 2 - 1, 1)
            reciprocal_root(B - 2)
            reciprocal_root(B - 1)

        @block.scalar
        def _(act):
            act.sem_inc(h_taken.sem, h_taken.start)

            def gelus(r, i):
                t = r * RING + i
                act.wait_ge(w1_loaded[i].sem, w1_loaded[i].at(r, 32))
                act.wait_ge(y_filled.sem, y_filled.at(t - RING, 1))
                for m in range(FC // 2):
                    act.wait_ge(h_filled.sem, h_filled.at(t, m + 1))
                    for n in range(2):
                        f = 2 * m + n
                        ins = nc.scalar.activation(h_t[i][:, f, :], h_bank[m][:, n * SLOTS:(n + 1) * SLOTS], ACT.Gelu,
                                                   bias=b1_s[i][:, f:f + 1])
                    ins.then_inc(h_taken.sem, 1)

            with act.Fori(0, ROUNDS) as r:
                for i in range(RING):
                    gelus(r, i)

        @block.vector
        def _(dve):
            def apart(s, value):
                dve.wait_ge(s.sem, value)
                dve.sem_inc(passed["dve"], 1)

            def step(ins, n):
                ins.then_inc(plan, 1)
                dve.wait_ge(plan, n)

            dve.wait_ge(consts, 7)
            dve.memset(one_e[:], 1.0)
            step(dve.tensor_tensor(has_tile[:], counts[:].unsqueeze(2).broadcast_to([P, E, MAX_TILES]),
                                   bound[:].unsqueeze(1).broadcast_to([P, E, MAX_TILES]), ALU.is_gt), 1)
            step(dve.tensor_reduce(tiles_of[:], has_tile[:], AX_X, ALU.add), 2)
            step(dve.tensor_tensor_scan(last_tile[:], one_e[:], tiles_of[:], 0.0, ALU.mult, ALU.add), 3)
            step(dve.tensor_tensor(is_past[:], tile_no[:].unsqueeze(2).broadcast_to([P, N_TILES, E]),
                                   last_tile[:].unsqueeze(1).broadcast_to([P, N_TILES, E]), ALU.is_ge), 4)
            step(dve.tensor_tensor(past_tiles[:], is_past[:], tiles_of[:].unsqueeze(1).broadcast_to([P, N_TILES, E]),
                                   ALU.mult), 5)
            step(dve.tensor_reduce(expert_f[:], is_past[:], AX_X, ALU.add), 6)
            step(dve.tensor_reduce(first_f[:], past_tiles[:], AX_X, ALU.add), 7)
            dve.tensor_scalar(expert_rows_f[:], expert_f[:], float(REGION), None, ALU.mult)
            step(dve.tensor_tensor(first_f[:], tile_no[:], first_f[:], ALU.subtract), 8)
            dve.tensor_scalar(tile_expert[:], expert_f[:], float(E - 1), None, ALU.min)
            step(dve.scalar_tensor_tensor(out=expert_rows_f[:], in0=first_f[:], scalar=float(SLOTS), in1=expert_rows_f[:],
                                          op0=ALU.mult, op1=ALU.add), 9)
            dve.tensor_copy(tile_base[:], expert_rows_f[:]).then_inc(plan, 1)
            own = slots[:, 1:B + 1, :, :].rearrange("p b c j -> p (b c j)")
            dve.memset(closing[:, 0:1], 0.0)
            dve.tensor_scalar(closing[:, 1:E], tiles_of[:, 0:E - 1], float(SLOTS), float(REGION), ALU.mult, ALU.subtract)
            step(dve.tensor_tensor(in_region[:], own.unsqueeze(2).broadcast_to([P, B * TC * TOP, E]),
                                   region[:].unsqueeze(1).broadcast_to([P, B * TC * TOP, E]), ALU.is_ge), 11)
            step(dve.tensor_tensor(gaps[:], in_region[:], closing[:].unsqueeze(1).broadcast_to([P, B * TC * TOP, E]),
                                   ALU.mult), 12)
            step(dve.tensor_reduce(gap[:], gaps[:], AX_X, ALU.add), 13)
            step(dve.tensor_tensor(row_no[:].rearrange("p b c j -> p (b c j)"), own, gap[:], ALU.add), 14)
            for s in (xt_taken, y_taken, slots_ready, sum_steps, stats3, ob_ready, *y_stored, *out_stored):
                dve.sem_inc(s.sem, s.start)

            def take_xt(r, i):
                t = r * RING + i
                dve.wait_ge(xt_filled.sem, xt_filled.at(t, 1))
                dve.wait_ge(h_filled.sem, h_filled.at(t - RING, FC // 2))
                dve.tensor_copy(xg_t[i][:].rearrange("p k s -> p (k s)"), xt_bank[:, :]).then_inc(xt_taken.sem, 1)

            def take_y(r, i):
                t = r * RING + i
                dve.wait_ge(w2_loaded[i].sem, w2_loaded[i].at(r, 32))
                dve.wait_ge(y_stored[i].sem, y_stored[i].at(r, 0))
                dve.wait_ge(y_filled.sem, y_filled.at(t, 1))
                dve.tensor_tensor(y_s[i][:], y_bank[i][:, :].rearrange("p (c d) -> p c d", c=SC),
                                  b2_s[i][:].unsqueeze(1).broadcast_to([P, SC, D]), ALU.add).then_inc(y_taken.sem, 1)

            take_xt(0, 0)
            with dve.Fori(0, ROUNDS - 1) as r:
                for i in range(RING):
                    take_xt(r + (i + 1) // RING, (i + 1) % RING)
                    take_y(r, i)
            for i in range(RING):
                if i + 1 < RING:
                    take_xt(ROUNDS - 1, i + 1)
                take_y(ROUNDS - 1, i)

            def places(r, q):
                b = 2 * r + q
                dve.tensor_copy(own_slots[q][:], row_no[:, b, :, :] if isinstance(b, int) else
                                row_no[:, bass.ds(b, 1), :, :].rearrange("p o c j -> p (o c) j")).then_inc(slots_ready.sem, 1)

            def combine(r, q):
                b = 2 * r + q
                g = gates[:, b + 1, :, :] if isinstance(b, int) else gates[:, bass.ds(b + 1, 1), :, :].rearrange("p o c j -> p (o c) j")
                dve.wait_ge(xb_loaded[q].sem, xb_loaded[q].at(r, 16))
                dve.wait_ge(rows_back[q].sem, rows_back[q].at(r, rows_back[q].per))
                for c in range(TC):
                    ins = dve.scalar_tensor_tensor(out=half_sum[:, c, :], in0=yb[q][:, c, 0, :], scalar=g[:, c, 0:1],
                                                   in1=xb[q][:, c, :], op0=ALU.mult, op1=ALU.add)
                ins.then_inc(sum_steps.sem, 1)
                dve.wait_ge(sum_steps.sem, sum_steps.at(b, 1))
                for c in range(TC):
                    ins = dve.scalar_tensor_tensor(out=res3[:, c, :], in0=yb[q][:, c, 1, :], scalar=g[:, c, 1:2],
                                                   in1=half_sum[:, c, :], op0=ALU.mult, op1=ALU.add)
                ins.then_inc(sum_steps.sem, 1)
                dve.wait_ge(sum_steps.sem, sum_steps.at(b, 2))
                for c in range(TC):
                    ins = dve.bn_stats(stat3[:, c, :], res3[:, c, :])
                ins.then_inc(sum_steps.sem, 1)
                apart(sum_steps, sum_steps.at(b, 3))
                for c in range(TC):
                    ins = dve.bn_aggr(mv3[:, c, :], stat3[:, c, :])
                ins.then_inc(stats3.sem, 1)
                dve.wait_ge(out_stored[q].sem, out_stored[q].at(r, 0))
                dve.wait_ge(rstd3_ready.sem, rstd3_ready.at(b, 1))
                for c in range(TC):
                    ins = dve.tensor_scalar(ob[q][:, c, :], res3[:, c, :], mv3[:, c, 0:1], rstd3[:, c:c + 1],
                                            ALU.subtract, ALU.mult)
                ins.then_inc(ob_ready.sem, 1)

            places(0, 0)
            with dve.Fori(0, B // 2 - 1) as r:
                places(r, 1)
                combine(r, 0)
                places(r + 1, 0)
                combine(r, 1)
            places(B // 2 - 1, 1)
            combine(B // 2 - 1, 0)
            combine(B // 2 - 1, 1)

        @block.tensor
        def _(pe):
            for s in (xt_filled, h_filled, y_filled):
                pe.sem_inc(s.sem, s.start)
            matmul, transpose = nc.tensor.matmul, nc.tensor.transpose

            def rows_transposed(r, i):
                t = r * RING + i
                pe.wait_ge(gathered[i].sem, gathered[i].at(r, gathered[i].per))
                pe.wait_ge(xt_taken.sem, xt_taken.at(t - 1, 1))
                for k in range(KC):
                    for c in range(SC):
                        ins = transpose(xt_bank[:, k * SLOTS + c * P:k * SLOTS + (c + 1) * P],
                                        xg[i][:, c, k * P:(k + 1) * P], ident[:])
                ins.then_inc(xt_filled.sem, 1)

            def first_product(r, i):
                t = r * RING + i
                pe.wait_ge(w1_loaded[i].sem, w1_loaded[i].at(r, 32))
                pe.wait_ge(xt_taken.sem, xt_taken.at(t, 1))
                for m in range(FC // 2):
                    pe.wait_ge(h_taken.sem, h_taken.at(t - 1, m + 1))
                    for n in range(2):
                        f = 2 * m + n
                        for k in range(KC):
                            ins = matmul(h_bank[m][:, n * SLOTS:(n + 1) * SLOTS], w1_s[i][:, k, f * P:(f + 1) * P],
                                         xg_t[i][:, k, :], start=(k == 0), stop=(k == KC - 1))
                    ins.then_inc(h_filled.sem, 1)

            def second_product(r, i):
                t = r * RING + i
                pe.wait_ge(w2_loaded[i].sem, w2_loaded[i].at(r, 32))
                pe.wait_ge(y_taken.sem, y_taken.at(t - RING, 1))
                for c in range(SC):
                    for f in range(FC):
                        if c == 0 and f % 2 == 0:
                            pe.wait_ge(h_taken.sem, h_taken.at(t, f // 2 + 1))
                        ins = matmul(y_bank[i][:, c * D:(c + 1) * D], h_t[i][:, f, c * P:(c + 1) * P], w2_s[i][:, f, :],
                                     start=(f == 0), stop=(f == FC - 1))
                ins.then_inc(y_filled.sem, 1)

            rows_transposed(0, 0)
            with pe.Fori(0, ROUNDS - 1) as r:
                for i in range(RING):
                    first_product(r, i)
                    rows_transposed(r + (i + 1) // RING, (i + 1) % RING)
                    second_product(r, i)
            for i in range(RING):
                first_product(ROUNDS - 1, i)
                if i + 1 < RING:
                    rows_transposed(ROUNDS - 1, i + 1)
                second_product(ROUNDS - 1, i)


def kernel(**inputs):
    from concourse import bacc
    from concourse.bass_utils import run_bass_kernel_spmd

    def a(name):
        return np.asarray(inputs[name])

    def by_partition(v):
        return np.ascontiguousarray(v.reshape(-1, P).T)

    b_in = a("L0_attn_b_in")
    smear, scale = a("L0_attn_smear_factor"), a("L0_attn_log_scale")
    heads_rows = np.concatenate([smear.reshape(EC, HPC).T, scale.reshape(EC, HPC).T], axis=1)
    arrays = {
        "x": a("x"),
        "ctx": a("ctx_1024"),
        "mask": np.ascontiguousarray(a("mask_BxS2_bk0")).reshape(B, 1, S).view(np.int32),
        "w_in_t": a("L0_attn_W_in").T,
        "w_out_t": a("L0_attn_W_out").T,
        "wq": a("L0_xattn_Wq"),
        "wkv": a("L0_xattn_Wkv"),
        "wout": a("L0_xattn_Wout"),
        "cols": np.concatenate([by_partition(v) for v in (
            a("L0_attn_in_ln_w"), a("L0_attn_in_ln_b"), b_in[0:D_EXP], b_in[D_EXP:2 * D_EXP],
            b_in[3 * D_EXP:4 * D_EXP], a("L0_xattn_g1"), a("L0_xattn_b1"), a("L0_xattn_g2"), a("L0_xattn_b2"))], axis=1),
        "rows": np.concatenate([b_in[2 * D_EXP:3 * D_EXP], a("L0_attn_out_ln_w"), a("L0_attn_out_ln_b"),
                                a("L0_ffn_br")])[None, :],
        "heads_rows": heads_rows,
        "y_bias": b_in[4 * D_EXP:][:, None],
        "wr": a("L0_ffn_Wr"),
        "w1": a("L0_ffn_W1"),
        "b1": a("L0_ffn_b1").reshape(E, FC, P).transpose(0, 2, 1),
        "w2": a("L0_ffn_W2"),
        "b2": a("L0_ffn_b2").reshape(E, 1, D),
    }
    arrays = {k: np.ascontiguousarray(v) for k, v in arrays.items()}
    nc = bacc.Bacc("TRN2", target_bir_lowering=False, num_devices=1)
    args = [nc.dram_tensor(k, v.shape, mybir.dt.from_np(v.dtype), kind="ExternalInput").ap() for k, v in arrays.items()]
    out = nc.dram_tensor("y", (T, D), F32, kind="ExternalOutput").ap()
    decoder_layer(nc, *args, out)
    r = run_bass_kernel_spmd(nc, [arrays], core_ids=[0])
    return r.results[0]["y"].reshape(B, S, D)
```

```python
from contextlib import ExitStack

import numpy as np

import concourse.bass as bass
from concourse import mybir

F32 = mybir.dt.float32
F32R = mybir.dt.float32r
U8 = mybir.dt.uint8
I32 = mybir.dt.int32
U32 = mybir.dt.uint32
ALU = mybir.AluOpType
ACT = mybir.ActivationFunctionType
AX_X = mybir.AxisListType.X

P = 128
B, S, D = 16, 256, 256
TC = S // P
KC = D // P
EPS = 1e-5

HEADS = 16
DH_A = 32
D_EXP = HEADS * DH_A
EC = D_EXP // P
HPC = P // DH_A
W_COLS = 4 * D_EXP + HEADS
NEG_BIG = -1.0e10

DH_X = 64
INNER = HEADS * DH_X
XC = INNER // P
N_KEYS = 2 * S
NC = N_KEYS // P
PX_RING = KC * INNER // N_KEYS
X_SCALE = 1.0 / float(np.sqrt(DH_X))
MASKED = -1.0e30

E, F, TOP = 8, 1024, 2
T = B * S
FC = F // P
SLOTS = 256
N_TILES = (T * TOP + E * (SLOTS - 1)) // SLOTS
REGION = T
SPARE = E * REGION
JUNK = SPARE + (N_TILES + 1) * SLOTS
LIST = JUNK + E * REGION + S
SC = SLOTS // P
MAX_TILES = REGION // SLOTS
RING = 3
ROUNDS = N_TILES // RING
assert N_TILES % RING == 0



class Signal:

    def __init__(self, sem, per, start=None):
        self.sem, self.per = sem, per
        self.start = per if start is None else start

    def at(self, b, n):
        return b * self.per + (self.start + n)


def decoder_layer(nc, x, ctx_in, mask, w_in_t, w_out_t, wq, wkv, wout, cols, rows, heads_rows, y_bias, wr,
                  w1, b1, w2, b2, out):
    x1_dram = nc.dram_tensor("x1_rows", (T + S, D), F32).ap()
    x2_dram = nc.dram_tensor("x2_rows", (T + S, D), F32).ap()
    list_dram = nc.dram_tensor("expert_list", (LIST, 1), I32).ap()
    stack = ExitStack()
    with stack:
        def sem(name):
            return stack.enter_context(nc.semaphore(name))

        def sig(name, per, start=None):
            return Signal(sem(name), per, start)

        def keep(name, shape, dt=F32):
            return stack.enter_context(nc.sbuf_tensor(name, shape, dt))

        ident = keep("ident", [P, P])
        gates = keep("gates", [P, B + 1, TC, TOP])
        slots = keep("slots", [P, B + 1, TC, TOP])
        counts = keep("counts", [P, E])
        with ExitStack() as inner:
            def half(name, shape):
                return inner.enter_context(nc.sbuf_tensor(name, shape, F32))

            vx = half("x_vx", [P, NC, INNER])
            pt = half("x_pt", [P, PX_RING, N_KEYS])
            wkv_s = vx[:].rearrange("p (k h) n -> p k (h n)", k=KC)
            wq_s = pt[:].rearrange("p (k h) n -> p k (h n)", k=KC)
            wox = half("wox", [P, XC, D])
            wr_s = half("wr_s", [P, KC, E])
            col = half("col", [P, 28])
            row = half("row", [P, 2 * D + E])
            self_phase(nc, sem, sig, x, w_in_t, w_out_t, wq, wkv, wout, wr, cols, rows, heads_rows, y_bias, x1_dram,
                       list_dram, ident, wq_s, wkv_s, wox, wr_s, col, row)
            cross_phase(nc, sem, sig, ctx_in, mask, x1_dram, x2_dram, list_dram, ident, vx, pt, wq_s, wkv_s, wox, wr_s, col,
                        row, gates, slots, counts)
        expert_phase(nc, sem, w1, b1, w2, b2, x2_dram, list_dram, out, ident, gates, slots, counts)


def self_phase(nc, sem, sig, x, w_in_t, w_out_t, wq, wkv, wout, wr, cols, rows, heads_rows, y_bias, x1_dram, list_dram,
               ident, wq_s, wkv_s, wox, wr_s, col, row):
    FILLS = 12
    WO, XT, YP, QP, KP, PP, VP = 0, 2, 3, 4, 6, 8, 10
    LN_X, LN_OUT, LN_RES = 1, 2, 3
    LNS = 3
    PROB_RING, PT_RING = 6, 4
    with ExitStack() as stack:
        def sb(name, shape, dt=F32):
            return stack.enter_context(nc.sbuf_tensor(name, shape, dt))

        def bank(name):
            return stack.enter_context(nc.psum_tensor(name, [P, 512], F32))

        win = sb("win", [P, KC, W_COLS])
        wo = sb("wo", [P, EC, D])
        smls = sb("smls", [P, 2 * EC])
        by = sb("by", [HEADS, 1])
        inw, inb, bq, bk, bp = (col[:, a:z] for a, z in ((0, 2), (2, 4), (4, 8), (8, 12), (12, 16)))
        bv, onw, onb = col[:, 24:28], row[:, 0:256], row[:, 256:512]
        smear = sb("smear", [P, EC])
        unsmear = sb("unsmear", [P, EC])
        q_scale = sb("q_scale", [P, EC])
        q_bias = sb("q_bias", [P, EC])
        half_bp = sb("half_bp", [P, EC])
        half_by = sb("half_by", [HEADS, 1])
        causal = sb("causal", [P, S])
        minus_half = sb("minus_half", [P, TC])
        zero_list = sb("zero_list", [P, JUNK // P], I32)
        zeros = sb("zeros", [P, 512])
        own_rows = sb("own_rows", [P, HPC, EC])
        x_raw = sb("x_raw", [P, TC, D])
        zx = sb("zx", [P, TC, D])
        xn_t = sb("xn_t", [P, KC, S])
        gate_tanh = sb("gate_tanh", [HEADS, S])
        one_keep = sb("one_keep", [HEADS, S])
        gate_sig = sb("gate_sig", [HEADS, S])
        pos = sb("pos", [HEADS, S])
        pos_parts = sb("pos_parts", [64, S], F32R)
        q_t = sb("q_t", [P, EC, S])
        k_t = sb("k_t", [P, EC, S])
        k_prev = sb("k_prev", [P, EC, S + 1])
        q_hi = sb("q_hi", [P, EC, S], F32R)
        q_lo = sb("q_lo", [P, EC, S], F32R)
        k_hi = sb("k_hi", [P, EC, S], F32R)
        k_lo = sb("k_lo", [P, EC, S], F32R)
        q_parts = sb("q_parts", [P, HPC, EC, S], F32R)
        k_parts = sb("k_parts", [P, HPC, EC, S], F32R)
        v_a = sb("v_a", [P, TC, D_EXP])
        p_tanh = sb("p_tanh", [P, EC, S])
        p_half = sb("p_half", [P, EC, S])
        silu_p = sb("silu_p", [P, EC, S])
        gated_t = sb("gated_t", [P, EC, S])
        prob = sb("prob", [P, PROB_RING, 3 * P])
        low = sb("low", [P, HEADS, TC])
        den = sb("den", [P, HEADS, TC])
        rden = sb("rden", [P, HEADS, TC])
        pt = sb("pt", [P, PT_RING, 3 * P])
        x_again = sb("x_again", [P, TC, D])
        x_res = sb("x_res", [P, TC, D])
        out_s = sb("out_s", [P, TC, D])
        centred = sb("centred", [P, TC, D])
        res1 = sb("res1", [P, TC, D])
        x1 = sb("x1", [P, TC, D])
        stat = sb("stat", [P, LNS, TC, 6])
        mv = sb("mv", [P, LNS, TC, 2])
        var_eps = sb("var_eps", [P, LNS, TC])
        rstd = sb("rstd", [P, LNS, TC])
        proj = [bank(f"proj{i}") for i in range(2)]
        score = [bank(f"score{i}") for i in range(2)]
        ptb = [bank(f"ptb{i}") for i in range(2)]
        av = [bank(f"av{i}") for i in range(2)]

        in_weights, late_weights = sem("in_weights"), sem("late_weights")
        consts, consts_v, consts_a = sem("consts"), sem("consts_v"), sem("consts_a")
        list_zeroed = sem("list_zeroed")
        passed = {e: sem(f"passed_{e}") for e in ("pool", "dve", "sp")}
        x_loaded, again_loaded = sig("x_loaded", 16), sig("again_loaded", 16, 0)
        parts_loaded = [sig(f"parts_loaded{g}", 16 * 8) for g in range(HPC)]
        x1_stored = sig("x1_stored", 16)
        ln_steps, stats_ready = sig("ln_steps", 4), sig("stats_ready", LNS)
        var_ready, rstd_ready = sig("var_ready", LNS), sig("rstd_ready", LNS)
        zx_ready, x_res_ready, x1_ready = sig("zx_ready", 1), sig("x_res_ready", 1), sig("x1_ready", 1)
        proj_filled = sig("proj_filled", FILLS)
        proj_taken = [sig(f"proj_taken{i}", FILLS // 2) for i in range(2)]
        k_prev_ready, k_hi_ready = sig("k_prev_ready", 2), sig("k_hi_ready", 2)
        pos_steps, p_half_ready = sig("pos_steps", 4), sig("p_half_ready", 2)
        q_split, k_split = sig("q_split", 2), sig("k_split", 2)
        out_used = sig("out_used", 1)
        silu_ready = sig("silu_ready", 1, 0)
        score_filled, score_taken = sig("score_filled", HEADS), sig("score_taken", HEADS)
        exp_ready, rden_ready, prob_ready = sig("exp_ready", HEADS), sig("rden_ready", HEADS), sig("prob_ready", HEADS)
        pt_filled = sig("pt_filled", HEADS)
        pt_taken = [sig(f"pt_taken{i}", HEADS // 2) for i in range(2)]
        av_done, gated = sig("av_done", HEADS), sig("gated", 2, 0)
        N_CONSTS, N_VCONSTS, N_IN, N_LATE = 10, 6, 16 * 9, 16 * 4

        block = stack.enter_context(nc.Block())

        @block.sync
        def _(sp):
            def rows_of(nb):
                return x[nb].rearrange("(c p) d -> p c d", p=P)

            def pass_wait(s, value):
                sp.wait_ge(s.sem, value)
                sp.sem_inc(passed["sp"], 1)

            def spread_parts(b):
                sp.wait_ge(k_split.sem, k_split.at(b, 2))
                for g in range(HPC):
                    r = slice(DH_A * g, DH_A * (g + 1))
                    if g == 0:
                        sp.wait_ge(pos_steps.sem, pos_steps.at(b, 4))
                    sp.wait_ge(score_filled.sem, score_filled.at(b, EC * g + EC))
                    for dst, src, place in ((q_parts, q_hi, 0), (q_parts, q_lo, 1), (q_parts, q_hi, 2),
                                            (k_parts, k_hi, 0), (k_parts, k_hi, 1), (k_parts, k_lo, 2)):
                        sp.dma_start(dst[DH_A * place:DH_A * (place + 1), g, :, :].bitcast(F32), src[r, :, :].bitcast(F32)).then_inc(parts_loaded[g].sem, 16)
                    for n in range(2):
                        sp.dma_start(k_parts[3 * DH_A + n * HEADS:3 * DH_A + (n + 1) * HEADS, g, :, :].bitcast(F32),
                                     pos_parts[32 * n:32 * n + HEADS, :].bitcast(F32).unsqueeze(1).broadcast_to([HEADS, EC, S])).then_inc(parts_loaded[g].sem, 16)

            sp.dma_start(x_raw[:], rows_of(0)).then_inc(x_loaded.sem, 16)
            sp.dma_start(col[:], cols).then_inc(in_weights, 16)
            sp.dma_start(row[:], rows.broadcast_to([P, rows.shape[1]])).then_inc(in_weights, 16)
            sp.dma_start(win[:], w_in_t.rearrange("(k p) n -> p k n", p=P)).then_inc(in_weights, 16)
            sp.dma_start(x_again[:], rows_of(0)).then_inc(again_loaded.sem, 16)
            sp.wait_ge(consts, N_CONSTS)
            sp.dma_start(list_dram[0:JUNK, :].rearrange("(p n) a -> p (n a)", p=P), zero_list[:]).then_inc(list_zeroed, 16)
            sp.wait_ge(zx_ready.sem, zx_ready.at(-1, 1))
            sp.dma_start(x_raw[:], rows_of(1)).then_inc(x_loaded.sem, 16)
            sp.wait_ge(consts_v, N_VCONSTS)
            spread_parts(-1)
            sp.dma_start(wkv_s, wkv.rearrange("(k p) n -> p k n", p=P)).then_inc(late_weights, 16)
            sp.dma_start(wq_s, wq.rearrange("(k p) n -> p k n", p=P)).then_inc(late_weights, 16)
            sp.dma_start(wox[:], wout.rearrange("(m p) n -> p m n", p=P)).then_inc(late_weights, 16)
            sp.dma_start(wr_s[:], wr.rearrange("(k p) n -> p k n", p=P)).then_inc(late_weights, 16)
            with sp.Fori(0, B) as b:
                pass_wait(zx_ready, zx_ready.at(b, 1))
                sp.dma_start(x_raw[:], rows_of((b + 2) % B)).then_inc(x_loaded.sem, 16)
                pass_wait(x_res_ready, x_res_ready.at(b, 1))
                sp.dma_start(x_again[:], rows_of(b)).then_inc(again_loaded.sem, 16)
                pass_wait(x1_ready, x1_ready.at(b, 1))
                sp.dma_start(x1_dram.rearrange("(b c p) d -> b p c d", c=TC, p=P)[b], x1[:]).then_inc(x1_stored.sem, 16)
                spread_parts(b)
            sp.wait_ge(x1_ready.sem, x1_ready.at(B, 1))
            sp.dma_start(x1_dram.rearrange("(b c p) d -> b p c d", c=TC, p=P)[B], x1[:]).then_inc(x1_stored.sem, 16)
            sp.wait_ge(x1_stored.sem, x1_stored.at(B, 16))
            sp.wait_ge(list_zeroed, 16)
            sp.wait_ge(late_weights, N_LATE)
            sp.wait_ge(x_loaded.sem, x_loaded.at(B, 16))
            for g in range(HPC):
                sp.wait_ge(parts_loaded[g].sem, parts_loaded[g].at(B - 1, parts_loaded[g].per))

        @block.gpsimd
        def _(pool):
            pool.memset(ident[:], 0.0).then_inc(consts, 1)
            pool.memset(causal[:], 0.0).then_inc(consts, 1)
            pool.memset(minus_half[:], -0.5).then_inc(consts, 1)
            pool.memset(zero_list[:], 0).then_inc(consts, 1)
            pool.memset(zeros[:], 0.0).then_inc(consts, 1)
            pool.memset(own_rows[:], 0.0).then_inc(consts, 1)
            pool.wait_ge(consts, 6)
            pool.affine_select(out=own_rows[:], in_=own_rows[:], compare_op=ALU.not_equal, fill=1.0, base=-3 * DH_A,
                               pattern=[[-1, HPC], [-HPC, EC]], channel_multiplier=1).then_inc(consts, 1)
            pool.wait_ge(consts, 7)
            pool.affine_select(out=own_rows[:], in_=own_rows[:], compare_op=ALU.not_equal, fill=1.0, base=-3 * DH_A - HEADS,
                               pattern=[[-1, HPC], [-HPC, EC]], channel_multiplier=1).then_inc(consts, 1)
            pool.affine_select(out=ident[:], in_=ident[:], compare_op=ALU.not_equal, fill=1.0, base=0,
                               pattern=[[-1, P]], channel_multiplier=1).then_inc(consts, 1)
            pool.affine_select(out=causal[:], in_=causal[:], compare_op=ALU.is_ge, fill=NEG_BIG, base=P,
                               pattern=[[-1, S]], channel_multiplier=1).then_inc(consts, 1)
            pool.wait_ge(consts, N_CONSTS)

            def reciprocal_root(b, ln):
                pool.wait_ge(stats_ready.sem, stats_ready.at(b, ln))
                pool.sem_inc(passed["pool"], 1)
                pool.tensor_scalar(var_eps[:, ln - 1, :], mv[:, ln - 1, :, 1], EPS, None, ALU.add).then_inc(var_ready.sem, 1)
                pool.wait_ge(var_ready.sem, var_ready.at(b, ln))
                pool.tensor_tensor(rstd[:, ln - 1, :], var_eps[:, ln - 1, :], minus_half[:], ALU.pow).then_inc(rstd_ready.sem, 1)

            def low_parts(b):
                for n in range(2):
                    m = slice(2 * n, 2 * n + 2)
                    f = QP + n
                    pool.wait_ge(proj_taken[f % 2].sem, proj_taken[f % 2].at(b, f // 2 + 1))
                    pool.tensor_tensor(q_lo[:, m, :], q_t[:, m, :], q_hi[:, m, :].bitcast(F32), ALU.subtract).then_inc(q_split.sem, 1)
                for n in range(2):
                    m = slice(2 * n, 2 * n + 2)
                    pool.wait_ge(k_hi_ready.sem, k_hi_ready.at(b, n + 1))
                    pool.tensor_tensor(k_lo[:, m, :], k_t[:, m, :], k_hi[:, m, :].bitcast(F32), ALU.subtract).then_inc(k_split.sem, 1)

            def residual(b):
                pool.wait_ge(again_loaded.sem, again_loaded.at(b, 16))
                pool.wait_ge(ln_steps.sem, ln_steps.at(b - 1, 3))
                pool.tensor_tensor(x_res[:], x_again[:], onb.unsqueeze(1).broadcast_to([P, TC, D]), ALU.add).then_inc(x_res_ready.sem, 1)

            pool.sem_inc(x_res_ready.sem, 1)
            reciprocal_root(-1, LN_X)
            pool.wait_ge(rstd_ready.sem, rstd_ready.at(-1, LN_X))
            for s in (var_ready, rstd_ready):
                pool.sem_inc(s.sem, LNS - 1)
            pool.wait_ge(in_weights, N_IN)
            low_parts(-1)
            with pool.Fori(0, B) as b:
                reciprocal_root(b, LN_X)
                residual(b)
                for ln in (LN_OUT, LN_RES):
                    reciprocal_root(b, ln)
                low_parts(b)
            pool.wait_ge(rstd_ready.sem, rstd_ready.at(B - 1, LNS))
            for s in (var_ready, rstd_ready):
                pool.sem_inc(s.sem, 1)
            residual(B)
            for ln in (LN_OUT, LN_RES):
                reciprocal_root(B, ln)

        @block.scalar
        def _(act):
            act.dma_start(by[:], y_bias).then_inc(in_weights, 16)
            for hh in range(HPC):
                act.dma_start(smls[DH_A * hh:DH_A * (hh + 1), :],
                              heads_rows[hh:hh + 1, 0:2 * EC].broadcast_to([DH_A, 2 * EC])).then_inc(in_weights, 16)
            act.dma_start(wo[:], w_out_t.rearrange("(m p) n -> p m n", p=P)).then_inc(in_weights, 16)
            act.wait_ge(in_weights, N_IN)
            nc.scalar.activation(smear[:], smls[:, 0:EC], ACT.Tanh, scale=0.5).then_inc(consts_a, 1)
            nc.scalar.activation(q_scale[:], smls[:, EC:2 * EC], ACT.Exp, scale=-2.0).then_inc(consts_a, 1)
            act.wait_ge(consts_v, N_VCONSTS)

            def taken(ins, f):
                ins.then_inc(proj_taken[f % 2].sem, 1)

            def filled(b, f):
                act.wait_ge(proj_filled.sem, proj_filled.at(b, f + 1))

            def exps(b, u):
                act.wait_ge(score_taken.sem, score_taken.at(b, u + 1))
                slot = prob[:, u % PROB_RING, :]
                for c in range(TC):
                    s = slot[:, 0:P] if c == 0 else slot[:, P:P + S]
                    ins = nc.scalar.activation(s, s, ACT.Exp, bias=low[:, u, c:c + 1], scale=-1.0, accum_out=den[:, u, c:c + 1])
                ins.then_inc(exp_ready.sem, 1)

            def take_transposed(b, u):
                act.wait_ge(pt_filled.sem, pt_filled.at(b, u + 1))
                act.wait_ge(av_done.sem, av_done.at(b, u - PT_RING + 1))
                nc.scalar.copy(pt[:, u % PT_RING, :], ptb[u % 2][:, 0:3 * P]).then_inc(pt_taken[u % 2].sem, 1)

            def take_xt(b):
                filled(b, XT)
                for k in range(KC):
                    ins = nc.scalar.activation(xn_t[:, k, :], proj[XT % 2][:, k * S:(k + 1) * S], ACT.Identity,
                                               bias=inb[:, k:k + 1], scale=inw[:, k:k + 1])
                taken(ins, XT)

            def take_y(b):
                filled(b, YP)
                taken(nc.scalar.activation(gate_tanh[:], proj[YP % 2][0:HEADS, 0:S], ACT.Tanh, bias=half_by[:, 0:1], scale=0.5), YP)

            def take_q(b, n):
                f = QP + n
                if n == 0:
                    act.wait_ge(q_split.sem, q_split.at(b - 1, 2))
                    for g in range(HPC):
                        act.wait_ge(parts_loaded[g].sem, parts_loaded[g].at(b - 1, parts_loaded[g].per))
                filled(b, f)
                for dst in (q_t, q_hi):
                    for i in range(2):
                        m = 2 * n + i
                        ins = nc.scalar.activation(dst[:, m, :], proj[f % 2][:, i * S:(i + 1) * S], ACT.Identity,
                                                   bias=q_bias[:, m:m + 1], scale=q_scale[:, m:m + 1])
                taken(ins, f)

            def smear_k(b, n):
                f = KP + n
                filled(b, f)
                for i in range(2):
                    m = 2 * n + i
                    ins = nc.scalar.activation(k_prev[:, m, 1:S + 1], proj[f % 2][:, i * S:(i + 1) * S], ACT.Identity,
                                               bias=bk[:, m:m + 1], scale=smear[:, m:m + 1])
                ins.then_inc(k_prev_ready.sem, 1)

            def high_k(b, n):
                f = KP + n
                act.wait_ge(proj_taken[f % 2].sem, proj_taken[f % 2].at(b, f // 2 + 1))
                nc.scalar.copy(k_hi[:, 2 * n:2 * n + 2, :], k_t[:, 2 * n:2 * n + 2, :]).then_inc(k_hi_ready.sem, 1)

            def tanh_p(b, n):
                f = PP + n
                act.wait_ge(p_half_ready.sem, p_half_ready.at(b, n + 1))
                act.wait_ge(silu_ready.sem, silu_ready.at(b, 1))
                for i in range(2):
                    m = 2 * n + i
                    ins = nc.scalar.activation(p_tanh[:, m, :], proj[f % 2][:, i * S:(i + 1) * S], ACT.Tanh,
                                               bias=half_bp[:, m:m + 1], scale=0.5)
                taken(ins, f)

            def take_v(b):
                act.wait_ge(av_done.sem, av_done.at(b - 1, HEADS))
                for f in (VP, VP + 1):
                    filled(b - 1, f)
                    taken(nc.scalar.copy(v_a[:, f - VP, :], proj[f % 2][:, :]), f)

            def take_output(c):
                def part(b):
                    filled(b, WO + c)
                    act.wait_ge(out_used.sem, out_used.at(b - 1, 1))
                    taken(nc.scalar.copy(out_s[:, c, :], proj[(WO + c) % 2][:, 0:D]), WO + c)
                return part

            def projections(b):
                take_xt(b)
                take_y(b)
                for n in range(2):
                    take_q(b, n)
                for n in range(2):
                    smear_k(b, n)
                    high_k(b, n)
                for n in range(2):
                    tanh_p(b, n)

            for s in (exp_ready, *pt_taken):
                act.sem_inc(s.sem, s.per)
            projections(-1)
            steps = {1: [take_v], 5: [take_xt], 6: [take_y], 7: [lambda b: take_q(b, 0)], 8: [lambda b: take_q(b, 1)],
                     9: [lambda b: smear_k(b, 0)], 10: [lambda b: high_k(b, 0), lambda b: smear_k(b, 1)],
                     11: [lambda b: high_k(b, 1), lambda b: tanh_p(b, 0)], 12: [lambda b: tanh_p(b, 1)],
                     3: [take_output(0)], 4: [take_output(1)]}
            with act.Fori(0, B) as b:
                for i in range(HEADS + 3):
                    if i < HEADS:
                        exps(b, i)
                    if i >= 3:
                        take_transposed(b, i - 3)
                    for part in steps.get(i, ()):
                        part(b)
            take_v(B)
            for c in range(TC):
                take_output(c)(B)

        @block.vector
        def _(dve):
            def apart(signal, value):
                dve.wait_ge(signal.sem, value)
                dve.sem_inc(passed["dve"], 1)

            def filled(b, f):
                dve.wait_ge(proj_filled.sem, proj_filled.at(b, f + 1))

            def taken(ins, f):
                ins.then_inc(proj_taken[f % 2].sem, 1)

            dve.memset(silu_p[:], 0.0)
            dve.memset(one_keep[:], 1.0).then_inc(consts_v, 1)
            dve.wait_ge(consts, N_CONSTS)
            for g in range(HPC):
                ins = dve.tensor_copy(q_parts[3 * DH_A:P, g, :, :],
                                      own_rows[3 * DH_A:P, g, :].unsqueeze(2).broadcast_to([P - 3 * DH_A, EC, S]))
            ins.then_inc(consts_v, 1)
            dve.wait_ge(consts_a, 2)
            dve.wait_ge(in_weights, N_IN)
            dve.tensor_scalar(unsmear[:], smear[:], -0.5, 0.5, ALU.mult, ALU.add).then_inc(consts_v, 1)
            dve.tensor_scalar(q_scale[:], q_scale[:], 1.0 / float(np.sqrt(DH_A)), None, ALU.mult).then_inc(consts_v, 1)
            dve.tensor_scalar(half_bp[:], bp, 0.5, None, ALU.mult)
            dve.tensor_scalar(half_by[:], by[:], 0.5, None, ALU.mult).then_inc(consts_v, 1)
            dve.wait_ge(consts_v, 5)
            dve.tensor_scalar(smear[:], smear[:], 0.5, 0.5, ALU.mult, ALU.add)
            dve.tensor_tensor(q_bias[:], bq, q_scale[:], ALU.mult)
            dve.tensor_tensor(k_prev[:, :, 0], unsmear[:], bk, ALU.mult).then_inc(consts_v, 1)
            for s in (x1_ready, x1_stored, out_used, score_taken, rden_ready, prob_ready):
                dve.sem_inc(s.sem, s.per)

            def stats(b, ln, sources, n):
                for c in range(TC):
                    ins = dve.bn_stats(stat[:, ln - 1, c, :], sources[c])
                ins.then_inc(ln_steps.sem, 1)
                apart(ln_steps, ln_steps.at(b, n))
                for c in range(TC):
                    ins = dve.bn_aggr(mv[:, ln - 1, c, :], stat[:, ln - 1, c, :])
                ins.then_inc(stats_ready.sem, 1)

            def normalise(ln, out, src, c):
                return dve.tensor_scalar(out, src, mv[:, ln - 1, c, 0:1], rstd[:, ln - 1, c:c + 1], ALU.subtract, ALU.mult)

            def x_stats(b):
                dve.wait_ge(x_loaded.sem, x_loaded.at(b, 16))
                stats(b, LN_X, [x_raw[:, c, :] for c in range(TC)], 1)

            def x_normalised(b):
                dve.wait_ge(rstd_ready.sem, rstd_ready.at(b, LN_X))
                for c in range(TC):
                    ins = normalise(LN_X, zx[:, c, :], x_raw[:, c, :], c)
                ins.then_inc(zx_ready.sem, 1)

            def forget_gates(b):
                dve.wait_ge(proj_taken[YP % 2].sem, proj_taken[YP % 2].at(b, YP // 2 + 1))
                dve.tensor_scalar(gate_sig[:], gate_tanh[:], 0.5, 0.5, ALU.mult, ALU.add).then_inc(pos_steps.sem, 1)
                dve.wait_ge(pos_steps.sem, pos_steps.at(b, 1))
                dve.tensor_tensor_scan(pos[:], one_keep[:], gate_sig[:], 0.0, ALU.mult, ALU.add).then_inc(pos_steps.sem, 1)
                dve.wait_ge(pos_steps.sem, pos_steps.at(b, 2))
                for g in range(HPC):
                    dve.wait_ge(parts_loaded[g].sem, parts_loaded[g].at(b - 1, parts_loaded[g].per))
                dve.tensor_copy(pos_parts[0:HEADS, :], pos[:]).then_inc(pos_steps.sem, 1)
                dve.wait_ge(pos_steps.sem, pos_steps.at(b, 3))
                dve.tensor_tensor(pos_parts[32:32 + HEADS, :], pos[:], pos_parts[0:HEADS, :].bitcast(F32),
                                  ALU.subtract).then_inc(pos_steps.sem, 1)

            def take_k(b, n):
                f = KP + n
                if n == 0:
                    dve.wait_ge(k_split.sem, k_split.at(b - 1, 2))
                dve.wait_ge(k_prev_ready.sem, k_prev_ready.at(b, n + 1))
                for i in range(2):
                    m = 2 * n + i
                    ins = dve.scalar_tensor_tensor(out=k_t[:, m, :], in0=proj[f % 2][:, i * S:(i + 1) * S],
                                                   scalar=unsmear[:, m:m + 1], in1=k_prev[:, m, 0:S],
                                                   op0=ALU.mult, op1=ALU.add)
                taken(ins, f)

            def half_p(b, n):
                f = PP + n
                filled(b, f)
                for i in range(2):
                    m = 2 * n + i
                    ins = dve.tensor_scalar(p_half[:, m, :], proj[f % 2][:, i * S:(i + 1) * S],
                                            bp[:, m:m + 1], 0.5, ALU.add, ALU.mult)
                ins.then_inc(p_half_ready.sem, 1)

            def gate(b):
                dve.wait_ge(av_done.sem, av_done.at(b - 1, HEADS))
                for m in range(EC):
                    ins = dve.scalar_tensor_tensor(out=gated_t[:, m, :], in0=av[m // 2][:, (m % 2) * S:(m % 2 + 1) * S],
                                                   scalar=bv[:, m:m + 1], in1=silu_p[:, m, :], op0=ALU.add, op1=ALU.mult)
                    if m % 2 == 1:
                        ins.then_inc(gated.sem, 1)

            def silu(b):
                dve.wait_ge(gated.sem, gated.at(b, 2))
                f = PP + 1
                dve.wait_ge(proj_taken[f % 2].sem, proj_taken[f % 2].at(b - 1, f // 2 + 1))
                dve.scalar_tensor_tensor(out=silu_p[:], in0=p_tanh[:], scalar=1.0, in1=p_half[:],
                                         op0=ALU.add, op1=ALU.mult).then_inc(silu_ready.sem, 1)

            def masked_scores(b, u):
                apart(pt_filled, pt_filled.at(b, u - PROB_RING + 1))
                apart(score_filled, score_filled.at(b, u + 1))
                slot, bank = prob[:, u % PROB_RING, :], score[u % 2]
                dve.tensor_tensor_reduce(slot[:, 0:P], bank[:, 0:P], causal[:, P:S], -1.0, 3.0e38,
                                         ALU.add, ALU.min, low[:, u, 0:1])
                dve.tensor_tensor_reduce(slot[:, P:P + S], bank[:, S:2 * S], causal[:, :], -1.0, 3.0e38,
                                         ALU.add, ALU.min, low[:, u, 1:2]).then_inc(score_taken.sem, 1)

            def one_over_sum(b, u):
                dve.wait_ge(exp_ready.sem, exp_ready.at(b, u + 1))
                dve.reciprocal(rden[:, u, :], den[:, u, :]).then_inc(rden_ready.sem, 1)

            def probabilities(b, u):
                dve.wait_ge(rden_ready.sem, rden_ready.at(b, u + 1))
                slot = prob[:, u % PROB_RING, :]
                for c in range(TC):
                    s = slot[:, 0:P] if c == 0 else slot[:, P:P + S]
                    ins = dve.tensor_scalar(s, s, rden[:, u, c:c + 1], None, ALU.mult)
                ins.then_inc(prob_ready.sem, 1)

            def out_stats(b):
                f = WO + 1
                dve.wait_ge(proj_taken[f % 2].sem, proj_taken[f % 2].at(b, f // 2 + 1))
                stats(b, LN_OUT, [out_s[:, c, :] for c in range(TC)], 2)

            def residual_sum(b):
                dve.wait_ge(rstd_ready.sem, rstd_ready.at(b, LN_OUT))
                for c in range(TC):
                    ins = dve.scalar_tensor_tensor(out=centred[:, c, :], in0=out_s[:, c, :],
                                                   scalar=mv[:, LN_OUT - 1, c, 0:1], in1=onw,
                                                   op0=ALU.subtract, op1=ALU.mult)
                ins.then_inc(out_used.sem, 1)
                dve.wait_ge(x_res_ready.sem, x_res_ready.at(b, 1))
                dve.wait_ge(out_used.sem, out_used.at(b, 1))
                for c in range(TC):
                    ins = dve.scalar_tensor_tensor(out=res1[:, c, :], in0=centred[:, c, :], scalar=rstd[:, LN_OUT - 1, c:c + 1],
                                                   in1=x_res[:, c, :], op0=ALU.mult, op1=ALU.add)
                ins.then_inc(ln_steps.sem, 1)
                dve.wait_ge(ln_steps.sem, ln_steps.at(b, 3))
                stats(b, LN_RES, [res1[:, c, :] for c in range(TC)], 4)

            def x1_of(b):
                dve.wait_ge(x1_stored.sem, x1_stored.at(b, 0))
                dve.wait_ge(rstd_ready.sem, rstd_ready.at(b, LN_RES))
                for c in range(TC):
                    ins = normalise(LN_RES, x1[:, c, :], res1[:, c, :], c)
                ins.then_inc(x1_ready.sem, 1)

            def credit(b):
                dve.wait_ge(stats_ready.sem, stats_ready.at(b, LN_X))
                dve.sem_inc(stats_ready.sem, LNS - 1)
                dve.sem_inc(ln_steps.sem, 3)

            x_stats(-1)
            x_normalised(-1)
            credit(-1)
            forget_gates(-1)
            for n in range(2):
                take_k(-1, n)
            for n in range(2):
                half_p(-1, n)
            steps = {1: [gate], 2: [x_stats], 3: [silu], 4: [x_normalised], 7: [forget_gates], 9: [lambda b: take_k(b, 0)],
                     10: [lambda b: take_k(b, 1)], 11: [lambda b: half_p(b, 0)], 12: [lambda b: half_p(b, 1)],
                     5: [out_stats], 6: [residual_sum], 8: [x1_of]}
            with dve.Fori(0, B) as b:
                for i in range(HEADS + 2):
                    if i < HEADS:
                        masked_scores(b, i)
                    if 1 <= i <= HEADS:
                        one_over_sum(b, i - 1)
                    if i >= 2:
                        probabilities(b, i - 2)
                    for part in steps.get(i, ()):
                        part(b)
            gate(B)
            dve.wait_ge(stats_ready.sem, stats_ready.at(B - 1, LNS))
            dve.sem_inc(stats_ready.sem, 1)
            dve.sem_inc(ln_steps.sem, 1)
            for part in (out_stats, residual_sum, x1_of):
                part(B)

        @block.tensor
        def _(pe):
            pe.wait_ge(consts, N_CONSTS)
            pe.wait_ge(in_weights, N_IN)
            for s, n in ((proj_filled, XT), (proj_taken[0], 1), (proj_taken[1], 1), (score_filled, HEADS), (pt_filled, HEADS),
                         (av_done, HEADS - 1)):
                pe.sem_inc(s.sem, n)
            matmul, transpose = nc.tensor.matmul, nc.tensor.transpose

            def free(b, f):
                pe.wait_ge(proj_taken[f % 2].sem, proj_taken[f % 2].at(b, f // 2))
                return proj[f % 2]

            def in_sbuf(b, f):
                pe.wait_ge(proj_taken[f % 2].sem, proj_taken[f % 2].at(b, f // 2 + 1))

            def full(ins):
                ins.then_inc(proj_filled.sem, 1)

            def project(out, lhs, rhs, chunks):
                for k in range(chunks):
                    ins = matmul(out, lhs(k), rhs(k), start=(k == 0), stop=(k == chunks - 1))
                return ins

            def x_transposed(b):
                bk_ = free(b, XT)
                pe.wait_ge(zx_ready.sem, zx_ready.at(b, 1))
                for k in range(KC):
                    for c in range(TC):
                        ins = transpose(bk_[:, k * S + c * P:k * S + (c + 1) * P], zx[:, c, k * P:(k + 1) * P], ident[:])
                full(ins)

            def project_y(b):
                bk_ = free(b, YP)
                in_sbuf(b, XT)
                full(project(bk_[0:HEADS, 0:S], lambda k: win[:, k, 4 * D_EXP:W_COLS], lambda k: xn_t[:, k, :], KC))

            def chunk(b, f, i, col0):
                bk_ = free(b, f) if i == 0 else proj[f % 2]
                ins = project(bk_[:, i * S:(i + 1) * S], lambda k: win[:, k, col0:col0 + P], lambda k: xn_t[:, k, :], KC)
                if i == 1:
                    full(ins)

            def chunks_of(f0, col0):
                return [lambda b, m=m: chunk(b, f0 + m // 2, m % 2, col0 + m * P) for m in range(EC)]

            def project_v(b, c):
                bk_ = free(b, VP + c)
                full(project(bk_[:, :], lambda k: xn_t[:, k, c * P:(c + 1) * P], lambda k: win[:, k, 2 * D_EXP:3 * D_EXP], KC))

            def scores(b, u):
                g, m = divmod(u, EC)
                pe.wait_ge(score_taken.sem, score_taken.at(b, u - 1))
                if m == 0:
                    pe.wait_ge(parts_loaded[g].sem, parts_loaded[g].at(b - 1, parts_loaded[g].per))
                for c in range(TC):
                    ins = matmul(score[u % 2][:, c * S:(c + 1) * S], q_parts[:, g, m, c * P:(c + 1) * P], k_parts[:, g, m, :],
                                 start=True, stop=True)
                ins.then_inc(score_filled.sem, 1)

            def transposes(b, u):
                pe.wait_ge(pt_taken[u % 2].sem, pt_taken[u % 2].at(b, u // 2))
                pe.wait_ge(prob_ready.sem, prob_ready.at(b, u + 1))
                for i in range(3):
                    ins = transpose(ptb[u % 2][:, i * P:(i + 1) * P], prob[:, u % PROB_RING, i * P:(i + 1) * P], ident[:])
                ins.then_inc(pt_filled.sem, 1)

            def values(b, u):
                g, m = divmod(u, EC)
                h = HPC * m + g
                if u == 0:
                    in_sbuf(b - 1, VP)
                    in_sbuf(b - 1, VP + 1)
                if u in (0, 2):
                    pe.wait_ge(gated.sem, gated.at(b, u // 2 + 1))
                pe.wait_ge(pt_taken[u % 2].sem, pt_taken[u % 2].at(b, u // 2 + 1))
                o = av[m // 2][DH_A * g:DH_A * (g + 1), (m % 2) * S:(m % 2 + 1) * S]
                dims = slice(DH_A * h, DH_A * (h + 1))
                matmul(o, v_a[:, 0, dims], pt[:, u % PT_RING, 0:S], start=True, stop=False)
                matmul(o[:, P:S], v_a[:, 1, dims], pt[:, u % PT_RING, S:S + P], start=False, stop=True).then_inc(av_done.sem, 1)

            def output(c):
                def part(b):
                    pe.wait_ge(gated.sem, gated.at(b, 2))
                    bk_ = free(b, WO + c)
                    full(project(bk_[:, 0:D], lambda k: gated_t[:, k, c * P:(c + 1) * P], lambda k: wo[:, k, :], EC))
                return part

            for j in range(2):
                ins = matmul(av[j][:, :], zeros[:, 0:P], zeros[:, :], start=True, stop=True)
            ins.then_inc(av_done.sem, 1)
            pe.wait_ge(consts_v, N_VCONSTS)
            outputs = [output(c) for c in range(TC)]
            inputs = [x_transposed, project_y, *chunks_of(QP, 0), *chunks_of(KP, D_EXP), *chunks_of(PP, 3 * D_EXP),
                      lambda b: project_v(b, 0), lambda b: project_v(b, 1)]

            for part in inputs:
                part(-1)
            before_ = {3: outputs[0], 4: outputs[1], 5: inputs[0], 16: inputs[14], 17: inputs[15]}
            after_ = {6: inputs[1]}
            for n, part in enumerate(inputs[2:14]):
                (after_ if n % 2 else before_)[7 + n // 2] = part
            with pe.Fori(0, B) as b:
                scores(b, 0)
                for i in range(HEADS + 4):
                    if i in before_:
                        before_[i](b)
                    if 3 <= i < HEADS + 3:
                        transposes(b, i - 3)
                    if i + 1 < HEADS:
                        scores(b, i + 1)
                    if i >= 4:
                        values(b, i - 4)
                    if i in after_:
                        after_[i](b)
            for part in outputs:
                part(B)


def cross_phase(nc, sem, sig, ctx_in, mask, x1_dram, x2_dram, list_dram, ident, vx, pt, wq_s, wkv_s, wox, wr_s, col, row,
                gates, slots, counts):
    FILLS = 26
    V1 = (0, 2, 3, 6)
    WOX, X2T, LOGITS, PREFIX, CT, LT = 1, 4, 5, 7, 8, 9
    KQ = (10, 13, 16, 21)
    V0 = (19, 20, 24, 25)
    LN_X2, LN_LAT, LN_CTX = 1, 2, 3
    LNS = 3
    UNITS = 2 * HEADS
    PROB_RING = 6
    QUADS = HEADS // 4
    with ExitStack() as stack:
        def sb(name, shape, dt=F32):
            return stack.enter_context(nc.sbuf_tensor("x_" + name, shape, dt))

        def bank(name):
            return stack.enter_context(nc.psum_tensor("x_" + name, [P, 512], F32))

        def signal(name, per, start=None):
            return sig("x_" + name, per, start)

        g1, be1, g2, be2 = (col[:, a:z] for a, z in ((16, 18), (18, 20), (20, 22), (22, 24)))
        br_row = row[:, 2 * D:2 * D + E]
        before = sb("before", [P, P])
        ones = sb("ones", [P, P])
        minus_half = sb("minus_half", [P, TC])
        expert_no = sb("expert_no", [P, E])
        expert_i = sb("expert_i", [P, E], I32)
        expert_base = sb("expert_base", [P, E])
        down = sb("down", [P, E])
        ctx_raw = sb("ctx_raw", [P, TC, D])
        x1_raw = sb("x1_raw", [P, TC, D])
        mask_raw = sb("mask_raw", [P, S // 4], I32)
        mask_add = sb("mask_add", [P, N_KEYS])
        zctx = sb("zctx", [P, TC, D])
        zlat = sb("zlat", [P, TC, D])
        keys_hi = sb("keys_hi", [P, KC, N_KEYS], F32R)
        keys_lo = sb("keys_lo", [P, KC, N_KEYS], F32R)
        keys_t = [z[:].rearrange("p c d -> p (c d)").rearrange("p (k s) -> p k s", k=KC) for z in (zctx, zlat)]
        wkv_hi = sb("wkv_hi", [P, KC, 2 * INNER], F32R)
        wkv_lo = sb("wkv_lo", [P, KC, 2 * INNER], F32R)
        wq_hi = sb("wq_hi", [P, KC, INNER], F32R)
        wq_lo = sb("wq_lo", [P, KC, INNER], F32R)
        q_parts = sb("q_parts", [P, HEADS, S], F32R)
        q_lo = sb("q_lo", [P, XC, S], F32R)
        k_twice = sb("k_twice", [P, HEADS, N_KEYS], F32R)
        k_lo = sb("k_lo", [P, XC, N_KEYS], F32R)
        prob = sb("prob", [P, PROB_RING, N_KEYS])
        low = sb("low", [P, UNITS])
        den = sb("den", [P, UNITS])
        rden = sb("rden", [P, UNITS])
        ox_t = sb("ox_t", [P, XC, S])
        x1_again = sb("x1_again", [P, TC, D])
        res2 = sb("res2", [P, TC, D])
        x2 = sb("x2", [P, TC, D])
        x2_t = sb("x2_t", [P, KC, S])
        stat = sb("stat", [P, LNS, TC, 6])
        mv = sb("mv", [P, LNS, TC, 2])
        var_eps = sb("var_eps", [P, LNS, TC])
        rstd = sb("rstd", [P, LNS, TC])
        logit = sb("logit", [P, TC, E])
        others = sb("others", [P, TC, E])
        best = sb("best", [P, TC, TOP])
        is_best = sb("is_best", [P, TC, E])
        rank = sb("rank", [P, TC, E])
        best_rank = sb("best_rank", [P, TC])
        margin = sb("margin", [P, TC])
        margin_tanh = sb("margin_tanh", [P, TC])
        chosen = sb("chosen", [P, TC, TOP, E])
        either = sb("either", [P, TC, E])
        place = sb("place", [P, TC, E])
        own_place = sb("own_place", [P, TC, TOP, E])
        slot_f = sb("slot_f", [P, TC, TOP])
        slot_i = sb("slot_i", [P, TC * TOP], I32)
        next_free = sb("next_free", [P, E])
        real = sb("real", [P, 1])
        junk_off = sb("junk_off", [P, 1])
        token_f = sb("token_f", [P, TC])
        token_i = sb("token_i", [P, TC], I32)
        proj = [bank(f"proj{i}") for i in range(2)]
        score = [bank(f"score{i}") for i in range(2)]
        ptb = [bank(f"ptb{i}") for i in range(2)]
        av = [bank(f"av{i}") for i in range(2)]

        consts, consts_v = sem("x_consts"), sem("x_consts_v")
        passed = {e: sem(f"x_passed_{e}") for e in ("pool", "dve", "sp")}
        x1_loaded, ctx_loaded, mask_loaded = signal("x1_loaded", 16), signal("ctx_loaded", 16), signal("mask_loaded", 16)
        again_loaded, x2_stored = signal("again_loaded", 16, 0), signal("x2_stored", 16)
        spread = [signal(f"spread{f}", 16 * 6) for f in range(QUADS)]
        scattered, scatter_over = signal("scattered", 16 * TC * TOP, 0), signal("scatter_over", 1)
        mask_ready = signal("mask_ready", 1)
        ln_steps, stats_ready = signal("ln_steps", 4), signal("stats_ready", LNS)
        var_ready, rstd_ready = signal("var_ready", LNS), signal("rstd_ready", LNS)
        zlat_ready, zctx_ready, x2_ready = signal("zlat_ready", 1), signal("zctx_ready", 1), signal("x2_ready", 1)
        proj_filled = signal("proj_filled", FILLS)
        proj_taken = [signal(f"proj_taken{i}", FILLS // 2) for i in range(2)]
        keys_hi_ready, keys_split = signal("keys_hi_ready", 2), signal("keys_split", 2)
        weights_hi, weights_split = sem("x_weights_hi"), sem("x_weights_split")
        k_hi_ready, q_hi_ready, q_lo_ready = signal("k_hi_ready", 2 * QUADS), signal("q_hi_ready", QUADS), signal("q_lo_ready", QUADS)
        score_filled, score_taken = signal("score_filled", UNITS), signal("score_taken", UNITS)
        exp_ready, prob_ready = signal("exp_ready", UNITS), signal("prob_ready", HEADS)
        rden_ready = signal("rden_ready", HEADS)
        pt_filled = signal("pt_filled", UNITS)
        pt_taken = [signal(f"pt_taken{i}", HEADS) for i in range(2)]
        av_done = signal("av_done", UNITS)
        av_taken = [signal(f"av_taken{i}", XC // 2) for i in range(2)]
        route_steps, margin_steps = signal("route_steps", 14), signal("margin_steps", 1)
        margin_ready, margin_tanh_ready = signal("margin_ready", 1), signal("margin_tanh_ready", 1)
        either_ready, slot_ready = signal("either_ready", 1), signal("slot_ready", 1)
        token_steps = signal("token_steps", 2)
        counts_ready = sem("counts_ready")
        N_CONSTS, N_VCONSTS = 9, 3

        weights = [(wkv_hi[:, k, :], wkv_s[:, k, :]) for k in range(KC)] + [(wq_hi[:], wq_s)]
        weights_lo = [wkv_lo[:, k, :] for k in range(KC)] + [wq_lo[:]]

        def halves(f):
            return [(slice(DH_X * o, DH_X * (o + 1)), slice(4 * f + o, 4 * f + 4, 2)) for o in range(2)]

        block = stack.enter_context(nc.Block())

        @block.sync
        def _(sp):
            x1_rows, x2_rows = (a.rearrange("(b c p) d -> b p c d", c=TC, p=P) for a in (x1_dram, x2_dram))

            def pass_wait(s, value):
                sp.wait_ge(s.sem, value)
                sp.sem_inc(passed["sp"], 1)

            def context_of(nb):
                return ctx_in[nb].rearrange("(c p) d -> p c d", p=P)

            def spread_heads(b):
                for f in range(QUADS):
                    (lo_rows, even), (hi_rows, odd) = halves(f)
                    for n in range(2):
                        keys = slice(n * S, (n + 1) * S)
                        sp.wait_ge(k_hi_ready.sem, k_hi_ready.at(b, 2 * f + n + 1))
                        for dst, src, heads in ((hi_rows, lo_rows, even), (lo_rows, hi_rows, odd)):
                            sp.dma_start(k_twice[dst, heads, keys].bitcast(F32),
                                         k_twice[src, heads, keys].bitcast(F32)).then_inc(spread[f].sem, 16)
                    sp.wait_ge(q_lo_ready.sem, q_lo_ready.at(b, f + 1))
                    for dst, src, heads in ((hi_rows, lo_rows, even), (lo_rows, hi_rows, odd)):
                        sp.dma_start(q_parts[dst, heads, :].bitcast(F32),
                                     q_lo[src, 2 * f:2 * f + 2, :].bitcast(F32)).then_inc(spread[f].sem, 16)

            sp.dma_start(x1_raw[:], x1_rows[1]).then_inc(x1_loaded.sem, 16)
            sp.dma_start(ctx_raw[:], context_of(0)).then_inc(ctx_loaded.sem, 16)
            sp.dma_start(mask_raw[:], mask[0].broadcast_to([P, S // 4])).then_inc(mask_loaded.sem, 16)
            sp.dma_start(x1_again[:], x1_rows[0]).then_inc(again_loaded.sem, 16)
            sp.wait_ge(zlat_ready.sem, zlat_ready.at(-1, 1))
            sp.dma_start(x1_raw[:], x1_rows[2]).then_inc(x1_loaded.sem, 16)
            sp.wait_ge(zctx_ready.sem, zctx_ready.at(-1, 1))
            sp.dma_start(ctx_raw[:], context_of(1)).then_inc(ctx_loaded.sem, 16)
            spread_heads(-1)
            with sp.Fori(0, B) as b:
                pass_wait(mask_ready, mask_ready.at(b - 1, 1))
                sp.dma_start(mask_raw[:], mask[(b + 1) % B].broadcast_to([P, S // 4])).then_inc(mask_loaded.sem, 16)
                pass_wait(ln_steps, ln_steps.at(b, 1))
                sp.dma_start(x1_again[:], x1_rows[b + 1]).then_inc(again_loaded.sem, 16)
                pass_wait(x2_ready, x2_ready.at(b, 1))
                sp.dma_start(x2_rows[b], x2[:]).then_inc(x2_stored.sem, 16)
                pass_wait(zlat_ready, zlat_ready.at(b, 1))
                sp.dma_start(x1_raw[:], x1_rows[(b + 3) % (B + 1)]).then_inc(x1_loaded.sem, 16)
                pass_wait(zctx_ready, zctx_ready.at(b, 1))
                sp.dma_start(ctx_raw[:], context_of((b + 2) % B)).then_inc(ctx_loaded.sem, 16)
                spread_heads(b)
            sp.wait_ge(x2_ready.sem, x2_ready.at(B, 1))
            sp.dma_start(x2_rows[B], x2[:]).then_inc(x2_stored.sem, 16)
            sp.wait_ge(x2_stored.sem, x2_stored.at(B, 16))
            sp.wait_ge(mask_loaded.sem, mask_loaded.at(B - 1, 16))
            sp.wait_ge(x1_loaded.sem, x1_loaded.at(B, 16))
            sp.wait_ge(ctx_loaded.sem, ctx_loaded.at(B, 16))
            for f in range(QUADS):
                sp.wait_ge(spread[f].sem, spread[f].at(B - 1, spread[f].per))

        @block.gpsimd
        def _(pool):
            pool.memset(ones[:], 1.0).then_inc(consts, 1)
            pool.memset(minus_half[:], -0.5).then_inc(consts, 1)
            pool.memset(mask_add[:], 0.0).then_inc(consts, 1)
            pool.memset(ox_t[:], 0.0).then_inc(consts, 1)
            pool.iota(expert_i[:], pattern=[[1, E]], base=0, channel_multiplier=0).then_inc(consts, 1)
            pool.iota(token_i[:], pattern=[[P, TC]], base=-S, channel_multiplier=1).then_inc(consts, 1)
            pool.wait_ge(consts, 6)
            pool.affine_select(out=before[:], in_=ones[:], compare_op=ALU.is_ge, fill=0.0, base=-1,
                               pattern=[[1, P]], channel_multiplier=-1).then_inc(consts, 1)
            pool.tensor_copy(token_f[:], token_i[:]).then_inc(consts, 1)
            pool.tensor_copy(expert_no[:], expert_i[:]).then_inc(consts, 1)
            pool.wait_ge(consts, N_CONSTS)

            def reciprocal_root(b, ln):
                pool.wait_ge(stats_ready.sem, stats_ready.at(b, ln))
                pool.sem_inc(passed["pool"], 1)
                pool.tensor_scalar(var_eps[:, ln - 1, :], mv[:, ln - 1, :, 1], EPS, None, ALU.add).then_inc(var_ready.sem, 1)
                pool.wait_ge(var_ready.sem, var_ready.at(b, ln))
                pool.tensor_tensor(rstd[:, ln - 1, :], var_eps[:, ln - 1, :], minus_half[:], ALU.pow).then_inc(rstd_ready.sem, 1)

            def low_keys(b):
                for n in range(2):
                    keys = slice(n * S, (n + 1) * S)
                    pool.wait_ge(keys_hi_ready.sem, keys_hi_ready.at(b, n + 1))
                    pool.tensor_tensor(keys_lo[:, :, keys], keys_t[n], keys_hi[:, :, keys].bitcast(F32),
                                       ALU.subtract).then_inc(keys_split.sem, 1)

            def scatter(b):
                pool.tensor_scalar(token_f[:], token_f[:], float(S), None, ALU.add).then_inc(token_steps.sem, 1)
                pool.wait_ge(token_steps.sem, token_steps.at(b, 1))
                pool.sem_inc(passed["pool"], 1)
                pool.tensor_copy(token_i[:], token_f[:]).then_inc(token_steps.sem, 1)
                pool.wait_ge(token_steps.sem, token_steps.at(b, 2))
                pool.wait_ge(slot_ready.sem, slot_ready.at(b, 1))
                pool.sem_inc(passed["pool"], 1)
                for c in range(TC):
                    for j in range(TOP):
                        n = c * TOP + j
                        pool.indirect_dma_start(
                            list_dram, bass.IndirectOffsetOnAxis(ap=slot_i[:, n:n + 1].bitcast(U32), axis=0),
                            token_i[:, c:c + 1], None).then_inc(scattered.sem, 16)
                pool.wait_ge(scattered.sem, scattered.at(b, scattered.per))
                pool.sem_inc(scatter_over.sem, 1)

            for s in (scatter_over, token_steps):
                pool.sem_inc(s.sem, s.per)
            for s in (var_ready, rstd_ready):
                pool.sem_inc(s.sem, LN_X2)
            for ln in (LN_LAT, LN_CTX):
                reciprocal_root(-1, ln)
            low_keys(-1)
            with pool.Fori(0, B) as b:
                for ln in (LN_X2, LN_LAT, LN_CTX):
                    reciprocal_root(b, ln)
                low_keys(b)
                scatter(b)
            reciprocal_root(B, LN_X2)
            scatter(B)

        @block.scalar
        def _(act):
            def taken(ins, f):
                ins.then_inc(proj_taken[f % 2].sem, 1)

            def filled(b, f):
                act.wait_ge(proj_filled.sem, proj_filled.at(b, f + 1))

            def exps(b, u):
                act.wait_ge(score_taken.sem, score_taken.at(b, u + 1))
                slot = prob[:, u % PROB_RING, :]
                nc.scalar.activation(slot, slot, ACT.Exp, bias=low[:, u:u + 1], scale=-1.0,
                                     accum_out=den[:, u:u + 1]).then_inc(exp_ready.sem, 1)

            def take_transposed(b, w):
                act.wait_ge(pt_filled.sem, pt_filled.at(b, w + 1))
                act.wait_ge(av_done.sem, av_done.at(b, w - PX_RING + 1))
                nc.scalar.copy(pt[:, w % PX_RING, :], ptb[w % 2][:, :]).then_inc(pt_taken[w % 2].sem, 1)

            def take_values(b, m):
                if m == 0:
                    filled(b, WOX)
                act.wait_ge(av_done.sem, av_done.at(b, 4 * m + 4))
                nc.scalar.copy(ox_t[:, m, :], av[m % 2][:, 0:S]).then_inc(av_taken[m % 2].sem, 1)

            def take_x2_t(b):
                filled(b, X2T)
                taken(nc.scalar.copy(x2_t[:].rearrange("p k s -> p (k s)"), proj[X2T % 2][:, :]), X2T)

            def gate_margin(b):
                act.wait_ge(margin_ready.sem, margin_ready.at(b, 1))
                nc.scalar.activation(margin_tanh[:], margin[:], ACT.Tanh, scale=0.5).then_inc(margin_tanh_ready.sem, 1)

            def take_keys_t(b, f, w, bias, n):
                keys = slice(n * S, (n + 1) * S)
                filled(b, f)
                for k in range(KC):
                    ins = nc.scalar.activation(keys_t[n][:, k, :], proj[f % 2][:, k * S:(k + 1) * S], ACT.Identity,
                                               bias=bias[:, k:k + 1], scale=w[:, k:k + 1])
                taken(ins, f)
                act.wait_ge(proj_taken[f % 2].sem, proj_taken[f % 2].at(b, f // 2 + 1))
                nc.scalar.copy(keys_hi[:, :, keys], keys_t[n]).then_inc(keys_hi_ready.sem, 1)

            def take_context(b):
                take_keys_t(b, CT, g1, be1, 0)

            def take_latents(b):
                take_keys_t(b, LT, g2, be2, 1)

            def high_part(b, f, fill, dst, ready):
                filled(b, fill)
                act.wait_ge(score_filled.sem, score_filled.at(b, 8 * f + 8))
                for rows, heads in halves(f):
                    ins = nc.scalar.copy(dst(rows, heads), proj[fill % 2][rows, :].rearrange("p (i s) -> p i s", i=2))
                ins.then_inc(ready.sem, 1)

            def high_k(b, f, n):
                high_part(b, f, KQ[f] + n, lambda rows, heads: k_twice[rows, heads, n * S:(n + 1) * S], k_hi_ready)

            def high_q(b, f):
                high_part(b, f, KQ[f] + 2, lambda rows, heads: q_parts[rows, heads, :], q_hi_ready)

            def take_v(b, f, n, half):
                filled(b, f)
                last = (b, 2 * 8) if half == 0 else (b - 1, UNITS)
                act.wait_ge(av_done.sem, av_done.at(*last))
                taken(nc.scalar.copy(vx[:, n, 512 * half:512 * (half + 1)], proj[f % 2][:, :]), f)

            def quad(f):
                return [lambda b: high_k(b, f, 0), lambda b: high_k(b, f, 1), lambda b: high_q(b, f)]

            def v_part(fills, n, half):
                return lambda b: take_v(b, fills[n], n, half)

            for s in (exp_ready, margin_tanh_ready, *pt_taken, *av_taken):
                act.sem_inc(s.sem, s.per)
            act.wait_ge(consts, N_CONSTS)
            for hi, w in weights:
                nc.scalar.copy(hi, w).then_inc(weights_hi, 1)
            for part in (take_context, take_latents, *quad(0), *quad(1), *quad(2), v_part(V0, 0, 0), *quad(3), v_part(V0, 2, 0)):
                part(-1)
            steps = {0: [v_part(V1, 0, 1)], 4: [v_part(V1, 2, 1)], 5: [take_x2_t], 7: [gate_margin], 8: [take_context],
                     9: [take_latents], 10: quad(0)[0:2], 11: [quad(0)[2], quad(1)[0]], 12: quad(1)[1:3], 13: quad(2)[0:2],
                     14: [quad(2)[2], v_part(V0, 0, 0)], 15: quad(3)[0:1], 16: quad(3)[1:3], 17: [v_part(V0, 2, 0)]}
            with act.Fori(0, B) as b:
                for i in range(HEADS + 4):
                    if i < HEADS:
                        for c in range(TC):
                            exps(b, 2 * i + c)
                    if 2 <= i < HEADS + 2:
                        for half in range(2):
                            take_transposed(b, 2 * (i - 2) + half)
                    if i >= 5 and i % 2 == 1:
                        take_values(b, (i - 5) // 2)
                    for part in steps.get(i, ()):
                        part(b)
            take_x2_t(B)
            gate_margin(B)

        @block.vector
        def _(dve):
            def apart(signal, value):
                dve.wait_ge(signal.sem, value)
                dve.sem_inc(passed["dve"], 1)

            def filled(b, f):
                dve.wait_ge(proj_filled.sem, proj_filled.at(b, f + 1))

            def taken(ins, f):
                ins.then_inc(proj_taken[f % 2].sem, 1)

            dve.memset(real[:], 0.0)
            dve.memset(junk_off[:], float(JUNK)).then_inc(consts_v, 1)
            dve.wait_ge(consts, N_CONSTS)
            dve.tensor_scalar(down[:], expert_no[:], -1.0, float(E), ALU.mult, ALU.add)
            dve.tensor_scalar(expert_base[:], expert_no[:], float(REGION), None, ALU.mult).then_inc(consts_v, 1)
            dve.tensor_scalar(next_free[:], expert_no[:], float(REGION), float(JUNK), ALU.mult, ALU.add).then_inc(consts_v, 1)
            dve.wait_ge(consts_v, N_VCONSTS)
            dve.sem_inc(stats_ready.sem, LN_X2)
            dve.sem_inc(ln_steps.sem, 2)
            for s in (x2_ready, x2_stored, score_taken, prob_ready, rden_ready, route_steps, margin_steps,
                      margin_ready, either_ready, slot_ready):
                dve.sem_inc(s.sem, s.per)

            def stats(b, ln, sources, n):
                for c in range(TC):
                    ins = dve.bn_stats(stat[:, ln - 1, c, :], sources[c])
                ins.then_inc(ln_steps.sem, 1)
                apart(ln_steps, ln_steps.at(b, n))
                for c in range(TC):
                    ins = dve.bn_aggr(mv[:, ln - 1, c, :], stat[:, ln - 1, c, :])
                ins.then_inc(stats_ready.sem, 1)

            def normalise(ln, out, src, c):
                return dve.tensor_scalar(out, src, mv[:, ln - 1, c, 0:1], rstd[:, ln - 1, c:c + 1], ALU.subtract, ALU.mult)

            def input_stats(b):
                dve.wait_ge(x1_loaded.sem, x1_loaded.at(b, 16))
                stats(b, LN_LAT, [x1_raw[:, c, :] for c in range(TC)], 3)
                dve.wait_ge(ctx_loaded.sem, ctx_loaded.at(b, 16))
                stats(b, LN_CTX, [ctx_raw[:, c, :] for c in range(TC)], 4)

            def input_normalised(b):
                for ln, n, z, raw, ready in ((LN_LAT, 1, zlat, x1_raw, zlat_ready), (LN_CTX, 0, zctx, ctx_raw, zctx_ready)):
                    dve.wait_ge(rstd_ready.sem, rstd_ready.at(b, ln))
                    if not isinstance(b, int):
                        dve.wait_ge(keys_split.sem, keys_split.at(b - 1, n + 1))
                    for c in range(TC):
                        ins = normalise(ln, z[:, c, :], raw[:, c, :], c)
                    ins.then_inc(ready.sem, 1)

            def residual_sum(b):
                dve.wait_ge(again_loaded.sem, again_loaded.at(b, 16))
                filled(b, WOX)
                ins = dve.tensor_tensor(res2[:], proj[WOX % 2][:, :].rearrange("p (c d) -> p c d", c=TC), x1_again[:], ALU.add)
                ins.then_inc(ln_steps.sem, 1)
                dve.wait_ge(ln_steps.sem, ln_steps.at(b, 1))
                dve.sem_inc(proj_taken[WOX % 2].sem, 1)
                stats(b, LN_X2, [res2[:, c, :] for c in range(TC)], 2)

            def x2_of(b):
                dve.wait_ge(x2_stored.sem, x2_stored.at(b, 0))
                dve.wait_ge(rstd_ready.sem, rstd_ready.at(b, LN_X2))
                for c in range(TC):
                    ins = normalise(LN_X2, x2[:, c, :], res2[:, c, :], c)
                ins.then_inc(x2_ready.sem, 1)

            def low_k(b, f, n):
                fill = KQ[f] + n
                dve.wait_ge(k_hi_ready.sem, k_hi_ready.at(b, 2 * f + n + 1))
                keys = slice(n * S, (n + 1) * S)
                for rows, heads in halves(f):
                    ins = dve.tensor_tensor(k_lo[rows, 2 * f:2 * f + 2, keys], proj[fill % 2][rows, :].rearrange("p (i s) -> p i s", i=2),
                                            k_twice[rows, heads, keys].bitcast(F32), ALU.subtract)
                taken(ins, fill)

            def low_q(b, f):
                fill = KQ[f] + 2
                dve.wait_ge(q_hi_ready.sem, q_hi_ready.at(b, f + 1))
                for rows, heads in halves(f):
                    ins = dve.tensor_tensor(q_lo[rows, 2 * f:2 * f + 2, :], proj[fill % 2][rows, :].rearrange("p (i s) -> p i s", i=2),
                                            q_parts[rows, heads, :].bitcast(F32), ALU.subtract)
                ins.then_inc(q_lo_ready.sem, 1)
                dve.wait_ge(q_lo_ready.sem, q_lo_ready.at(b, f + 1))
                dve.sem_inc(proj_taken[fill % 2].sem, 1)

            def take_v(b, f, n, half):
                filled(b, f)
                last = (b, 2 * 8) if half == 0 else (b - 1, UNITS)
                dve.wait_ge(av_done.sem, av_done.at(*last))
                taken(dve.tensor_copy(vx[:, n, 512 * half:512 * (half + 1)], proj[f % 2][:, :]), f)

            def spread_mask(b):
                dve.wait_ge(mask_loaded.sem, mask_loaded.at(b, 16))
                dve.wait_ge(score_taken.sem, score_taken.at(b, UNITS))
                dve.tensor_scalar(mask_add[:, 0:S], mask_raw[:].bitcast(U8), 1.0, -MASKED, ALU.subtract, ALU.mult).then_inc(mask_ready.sem, 1)

            def masked_scores(b, u):
                if u == 0:
                    apart(mask_ready, mask_ready.at(b - 1, 1))
                apart(pt_filled, pt_filled.at(b, 2 * ((u - PROB_RING) // 2) + 2))
                apart(score_filled, score_filled.at(b, u + 1))
                dve.tensor_tensor_reduce(prob[:, u % PROB_RING, :], score[u % 2][:, :], mask_add[:, :], -X_SCALE, 3.0e38,
                                         ALU.add, ALU.min, low[:, u:u + 1]).then_inc(score_taken.sem, 1)

            def one_over_sum(b, h):
                dve.wait_ge(exp_ready.sem, exp_ready.at(b, 2 * h + 2))
                dve.reciprocal(rden[:, 2 * h:2 * h + 2], den[:, 2 * h:2 * h + 2]).then_inc(rden_ready.sem, 1)

            def probabilities(b, h):
                dve.wait_ge(rden_ready.sem, rden_ready.at(b, h + 1))
                for u in (2 * h, 2 * h + 1):
                    slot = prob[:, u % PROB_RING, :]
                    ins = dve.tensor_scalar(slot, slot, rden[:, u:u + 1], None, ALU.mult)
                ins.then_inc(prob_ready.sem, 1)

            def best_two(b):
                filled(b, LOGITS)
                taken(dve.tensor_tensor(logit[:], proj[LOGITS % 2][:, 0:TC * E].rearrange("p (c e) -> p c e", c=TC),
                                        br_row.unsqueeze(1).broadcast_to([P, TC, E]), ALU.add), LOGITS)
                apart(proj_taken[LOGITS % 2], proj_taken[LOGITS % 2].at(b, LOGITS // 2 + 1))
                every = [P, TC, E]
                rest = logit
                for j in range(TOP):
                    n = 5 * j
                    dve.tensor_reduce(best[:, :, j], rest[:], AX_X, ALU.max).then_inc(route_steps.sem, 1)
                    dve.wait_ge(route_steps.sem, route_steps.at(b, n + 1))
                    dve.tensor_tensor(is_best[:], rest[:], best[:, :, j].unsqueeze(2).broadcast_to(every), ALU.is_equal).then_inc(route_steps.sem, 1)
                    dve.wait_ge(route_steps.sem, route_steps.at(b, n + 2))
                    dve.tensor_tensor(rank[:], is_best[:], down[:].unsqueeze(1).broadcast_to(every), ALU.mult).then_inc(route_steps.sem, 1)
                    dve.wait_ge(route_steps.sem, route_steps.at(b, n + 3))
                    dve.tensor_reduce(best_rank[:], rank[:], AX_X, ALU.max).then_inc(route_steps.sem, 1)
                    dve.wait_ge(route_steps.sem, route_steps.at(b, n + 4))
                    dve.tensor_tensor(chosen[:, :, j, :], down[:].unsqueeze(1).broadcast_to(every),
                                      best_rank[:].unsqueeze(2).broadcast_to(every), ALU.is_equal).then_inc(route_steps.sem, 1)
                    dve.wait_ge(route_steps.sem, route_steps.at(b, n + 5))
                    if j == 0:
                        dve.scalar_tensor_tensor(out=others[:], in0=chosen[:, :, 0, :], scalar=MASKED, in1=logit[:],
                                                 op0=ALU.mult, op1=ALU.add).then_inc(margin_steps.sem, 1)
                        dve.wait_ge(margin_steps.sem, margin_steps.at(b, 1))
                        rest = others
                dve.tensor_tensor(margin[:], best[:, :, 0], best[:, :, 1], ALU.subtract).then_inc(margin_ready.sem, 1)
                dve.tensor_tensor(either[:], chosen[:, :, 0, :], chosen[:, :, 1, :], ALU.add).then_inc(either_ready.sem, 1)

            def list_places(b):
                dve.wait_ge(margin_tanh_ready.sem, margin_tanh_ready.at(b, 1))
                dve.tensor_scalar(gates[:, b, :, 0], margin_tanh[:], 0.5, 0.5, ALU.mult, ALU.add)
                dve.tensor_scalar(gates[:, b, :, 1], margin_tanh[:], -0.5, 0.5, ALU.mult, ALU.add)
                filled(b, PREFIX)
                dve.tensor_tensor(place[:], proj[PREFIX % 2][:, 0:TC * E].rearrange("p (c e) -> p c e", c=TC),
                                  next_free[:].unsqueeze(1).broadcast_to([P, TC, E]), ALU.add).then_inc(route_steps.sem, 1)
                dve.wait_ge(route_steps.sem, route_steps.at(b, 11))
                taken(dve.scalar_tensor_tensor(out=next_free[:], in0=proj[PREFIX % 2][:, TC * E:(TC + 1) * E],
                                               scalar=real[:, 0:1], in1=next_free[:], op0=ALU.mult, op1=ALU.add), PREFIX)
                dve.tensor_tensor(own_place[:], chosen[:], place[:].unsqueeze(2).broadcast_to([P, TC, TOP, E]),
                                  ALU.mult).then_inc(route_steps.sem, 1)
                dve.wait_ge(route_steps.sem, route_steps.at(b, 12))
                dve.tensor_scalar(next_free[:], next_free[:], junk_off[:, 0:1], None, ALU.subtract)
                dve.tensor_reduce(slot_f[:], own_place[:], AX_X, ALU.add).then_inc(route_steps.sem, 1)
                dve.wait_ge(route_steps.sem, route_steps.at(b, 13))
                dve.wait_ge(scatter_over.sem, scatter_over.at(b, 0))
                dve.tensor_copy(slots[:, b, :, :], slot_f[:])
                dve.tensor_copy(slot_i[:], slot_f[:].rearrange("p c j -> p (c j)")).then_inc(slot_ready.sem, 1)
                dve.memset(real[:], 1.0)
                dve.memset(junk_off[:], 0.0).then_inc(route_steps.sem, 1)

            def quad(f):
                return [lambda b: low_k(b, f, 0), lambda b: low_k(b, f, 1), lambda b: low_q(b, f)]

            def v_part(fills, n, half):
                return lambda b: take_v(b, fills[n], n, half)

            spread_mask(-1)
            input_stats(-1)
            input_normalised(-1)
            for n, ((hi, w), lo) in enumerate(zip(weights, weights_lo)):
                dve.wait_ge(weights_hi, n + 1)
                dve.tensor_tensor(lo, w, hi.bitcast(F32), ALU.subtract).then_inc(weights_split, 1)
            for part in (*quad(0), *quad(1), *quad(2), v_part(V0, 1, 0), *quad(3), v_part(V0, 3, 0)):
                part(-1)
            steps = {3: [residual_sum, v_part(V1, 1, 1)], 4: [x2_of], 5: [input_stats], 6: [best_two], 7: [v_part(V1, 3, 1), input_normalised],
                     8: [list_places], 10: quad(0)[0:2], 11: [quad(0)[2], quad(1)[0]], 12: quad(1)[1:3], 13: quad(2)[0:2],
                     14: quad(2)[2:3], 15: [v_part(V0, 1, 0), quad(3)[0]], 16: [spread_mask, *quad(3)[1:3]], 17: [v_part(V0, 3, 0)]}
            with dve.Fori(0, B) as b:
                for i in range(HEADS + 4):
                    if i < HEADS:
                        masked_scores(b, 2 * i)
                    if 1 <= i <= HEADS:
                        one_over_sum(b, i - 1)
                    if i < HEADS:
                        masked_scores(b, 2 * i + 1)
                    if 1 <= i <= HEADS:
                        probabilities(b, i - 1)
                    for part in steps.get(i, ()):
                        part(b)
            for part in (residual_sum, x2_of, best_two, list_places):
                part(B)
            dve.wait_ge(route_steps.sem, route_steps.at(B, 14))
            dve.tensor_tensor(counts[:], next_free[:], expert_base[:], ALU.subtract).then_inc(counts_ready, 1)

        @block.tensor
        def _(pe):
            pe.wait_ge(consts, N_CONSTS)
            for s, n in ((proj_filled, CT), (proj_taken[0], CT // 2), (proj_taken[1], CT // 2), (score_filled, UNITS),
                         (pt_filled, UNITS), (av_done, UNITS)):
                pe.sem_inc(s.sem, n)
            matmul, transpose = nc.tensor.matmul, nc.tensor.transpose

            def free(b, f):
                pe.wait_ge(proj_taken[f % 2].sem, proj_taken[f % 2].at(b, f // 2))
                return proj[f % 2]

            def in_sbuf(b, f):
                pe.wait_ge(proj_taken[f % 2].sem, proj_taken[f % 2].at(b, f // 2 + 1))

            def full(ins):
                ins.then_inc(proj_filled.sem, 1)

            def project(out, lhs, rhs, chunks):
                for k in range(chunks):
                    ins = matmul(out, lhs(k), rhs(k), start=(k == 0), stop=(k == chunks - 1))
                return ins

            def transposed(b, f, z, ready, value):
                bk_ = free(b, f)
                pe.wait_ge(ready.sem, value)
                for k in range(KC):
                    for c in range(TC):
                        ins = transpose(bk_[:, k * S + c * P:k * S + (c + 1) * P], z[:, c, k * P:(k + 1) * P], ident[:])
                full(ins)

            def context_transposed(b):
                transposed(b, CT, zctx, zctx_ready, zctx_ready.at(b, 1))

            def latents_transposed(b):
                transposed(b, LT, zlat, zlat_ready, zlat_ready.at(b, 1))

            def x2_transposed(b):
                transposed(b, X2T, x2, x2_ready, x2_ready.at(b, 1))

            def project_parts(out, lhs, rhs):
                for k in range(KC):
                    for i, j in ((0, 0), (0, 1), (1, 0)):
                        ins = matmul(out, lhs(i, k), rhs(j, k), start=(k == 0 and i + j == 0), stop=(k == KC - 1 and i == 1))
                return ins

            keys_parts = (keys_hi, keys_lo)

            def chunk_pair(b, f, parts, col0, keys):
                bk_ = free(b, f)
                for i in range(2):
                    m0 = col0 + i * P
                    ins = project_parts(bk_[:, i * S:(i + 1) * S], lambda n, k: parts[n][:, k, m0:m0 + P],
                                        lambda n, k: keys_parts[n][:, k, keys])
                full(ins)

            def keys_of(b, f, n):
                if f == 0:
                    pe.wait_ge(keys_split.sem, keys_split.at(b, n + 1))
                chunk_pair(b, KQ[f] + n, (wkv_hi, wkv_lo), 2 * f * P, slice(n * S, (n + 1) * S))

            def queries(b, f):
                chunk_pair(b, KQ[f] + 2, (wq_hi, wq_lo), 2 * f * P, slice(S, N_KEYS))

            def values_of(b, fills, n, half):
                bk_ = free(b, fills[n])
                cols = slice(INNER + 512 * half, INNER + 512 * (half + 1))
                full(project_parts(bk_[:, :], lambda i, k: keys_parts[i][:, k, n * P:(n + 1) * P],
                                   lambda i, k: (wkv_hi, wkv_lo)[i][:, k, cols]))

            def output(b, c):
                if c == 0:
                    free(b, WOX)
                    for i in range(2):
                        pe.wait_ge(av_taken[i].sem, av_taken[i].at(b - 1, XC // 2))
                ins = project(proj[WOX % 2][:, c * D:(c + 1) * D], lambda k: ox_t[:, k, c * P:(c + 1) * P], lambda k: wox[:, k, :], XC)
                if c == TC - 1:
                    full(ins)

            def logits(b):
                bk_ = free(b, LOGITS)
                in_sbuf(b, X2T)
                for c in range(TC):
                    ins = project(bk_[:, c * E:(c + 1) * E], lambda k: x2_t[:, k, c * P:(c + 1) * P],
                                  lambda k: wr_s[:, k, :], KC)
                full(ins)

            def prefixes(b):
                bk_ = free(b, PREFIX)
                pe.wait_ge(either_ready.sem, either_ready.at(b, 1))
                matmul(bk_[:, 0:E], before[:], either[:, 0, :], start=True, stop=True)
                matmul(bk_[:, E:2 * E], ones[:], either[:, 0, :], start=True, stop=False)
                matmul(bk_[:, E:2 * E], before[:], either[:, 1, :], start=False, stop=True)
                matmul(bk_[:, 2 * E:3 * E], ones[:], either[:, 0, :], start=True, stop=False)
                full(matmul(bk_[:, 2 * E:3 * E], ones[:], either[:, 1, :], start=False, stop=True))

            def scores(b, h, c):
                u, m, r = 2 * h + c, h // 2, slice(DH_X * (h % 2), DH_X * (h % 2 + 1))
                pe.wait_ge(score_taken.sem, score_taken.at(b, u - 1))
                if h % 4 == 0 and c == 0:
                    f = h // 4
                    in_sbuf(b - 1, KQ[f] + 1)
                    pe.wait_ge(spread[f].sem, spread[f].at(b - 1, spread[f].per))
                tokens = slice(c * P, (c + 1) * P)
                matmul(score[u % 2][:, :], q_parts[:, h, tokens], k_twice[:, h, :], start=True, stop=False)
                matmul(score[u % 2][:, :], q_parts[r, h, tokens], k_lo[r, m, :], start=False, stop=True).then_inc(score_filled.sem, 1)

            def transposes(b, h):
                for half in range(2):
                    w = 2 * h + half
                    pe.wait_ge(pt_taken[w % 2].sem, pt_taken[w % 2].at(b, w // 2))
                    if half == 0:
                        pe.wait_ge(prob_ready.sem, prob_ready.at(b, h + 1))
                    for nn in range(2):
                        n = 2 * half + nn
                        for c in range(TC):
                            ins = transpose(ptb[w % 2][:, nn * S + c * P:nn * S + (c + 1) * P],
                                            prob[:, (2 * h + c) % PROB_RING, n * P:(n + 1) * P], ident[:])
                    ins.then_inc(pt_filled.sem, 1)

            def values(b, h):
                m, r = h // 2, slice(DH_X * (h % 2), DH_X * (h % 2 + 1))
                if h == 0:
                    in_sbuf(b - 1, V0[2])
                    in_sbuf(b - 1, V0[3])
                if h == HEADS // 2:
                    in_sbuf(b, V1[2])
                    in_sbuf(b, V1[3])
                if h % 2 == 0:
                    pe.wait_ge(av_taken[m % 2].sem, av_taken[m % 2].at(b, m // 2))
                for half in range(2):
                    w = 2 * h + half
                    pe.wait_ge(pt_taken[w % 2].sem, pt_taken[w % 2].at(b, w // 2 + 1))
                    for nn in range(2):
                        n = 2 * half + nn
                        ins = matmul(av[m % 2][r, 0:S], vx[:, n, DH_X * h:DH_X * (h + 1)],
                                     pt[:, w % PX_RING, nn * S:(nn + 1) * S], start=(n == 0), stop=(n == NC - 1))
                    ins.then_inc(av_done.sem, 1)

            def quad(f):
                return [lambda b: keys_of(b, f, 0), lambda b: keys_of(b, f, 1), lambda b: queries(b, f)]

            def v_parts(fills, half):
                return [lambda b, n=n: values_of(b, fills, n, half) for n in range(NC)]

            first, second, outs = v_parts(V0, 0), v_parts(V1, 1), [lambda b, c=c: output(b, c) for c in range(TC)]
            for part in (context_transposed, latents_transposed):
                part(-1)
            pe.wait_ge(weights_split, len(weights))
            for part in (*quad(0), *quad(1), *quad(2), *first[0:2], *quad(3), *first[2:4]):
                part(-1)
            before_, after_ = {}, {}
            before_.update({5: x2_transposed, 6: logits, 8: prefixes, 9: latents_transposed})
            after_.update({0: second[0], 1: outs[0], 2: outs[1], 3: second[1], 4: second[2], 6: second[3], 8: context_transposed})
            for n, part in enumerate((*quad(0), *quad(1), *quad(2), *first[0:2], *quad(3), *first[2:4])):
                (after_ if n % 2 else before_)[10 + n // 2] = part
            with pe.Fori(0, B) as b:
                for c in range(TC):
                    scores(b, 0, c)
                for i in range(HEADS + 3):
                    if i in before_:
                        before_[i](b)
                    if 2 <= i < HEADS + 2:
                        transposes(b, i - 2)
                    if i + 1 < HEADS:
                        for c in range(TC):
                            scores(b, i + 1, c)
                    if i >= 3:
                        values(b, i - 3)
                    if i in after_:
                        after_[i](b)

            def skip(f):
                free(B, f)
                in_sbuf(B, f - 1) if f > 0 else in_sbuf(B - 1, FILLS - 1)
                pe.sem_inc(proj_taken[f % 2].sem, 1)
                pe.sem_inc(proj_filled.sem, 1)

            skip(V1[0])
            for part in outs:
                part(B)
            skip(V1[1])
            skip(V1[2])
            x2_transposed(B)
            logits(B)
            skip(V1[3])
            prefixes(B)


def expert_phase(nc, sem, w1, b1, w2, b2, x2_dram, list_dram, out, ident, gates, slots, counts):
    y_dram = nc.dram_tensor("expert_rows", (N_TILES * SLOTS, D), F32).ap()
    with ExitStack() as stack:
        def sb(name, shape, dt=F32):
            return stack.enter_context(nc.sbuf_tensor(name, shape, dt))

        def bank(name):
            return stack.enter_context(nc.psum_tensor(name, [P, 512], F32))

        def sig(name, per, start=None):
            return Signal(sem(name), per, RING * per if start is None else start)

        tile_i = sb("tile_i", [P, N_TILES], I32)
        tile_no = sb("tile_no", [P, N_TILES])
        bound_i = sb("bound_i", [P, MAX_TILES], I32)
        bound = sb("bound", [P, MAX_TILES])
        has_tile = sb("has_tile", [P, E, MAX_TILES])
        tiles_of = sb("tiles_of", [P, E])
        one_e = sb("one_e", [P, E])
        last_tile = sb("last_tile", [P, E])
        is_past = sb("is_past", [P, N_TILES, E])
        past_tiles = sb("past_tiles", [P, N_TILES, E])
        expert_f = sb("expert_f", [P, N_TILES])
        first_f = sb("first_f", [P, N_TILES])
        expert_rows_f = sb("expert_rows_f", [P, N_TILES])
        tile_base = sb("tile_base", [P, N_TILES], I32)
        tile_expert = sb("tile_expert", [P, N_TILES], I32)
        half_e = sb("half_e", [P, TC])
        region_i = sb("region_i", [P, E], I32)
        region = sb("region", [P, E])
        closing = sb("closing", [P, E])
        in_region = sb("in_region", [P, B * TC * TOP, E])
        gaps = sb("gaps", [P, B * TC * TOP, E])
        gap = sb("gap", [P, B * TC * TOP])
        row_no = sb("row_no", [P, B, TC, TOP], I32)
        w1_s = sb("w1_s", [P, KC, F])
        w2_s = sb("w2_s", [P, FC, D])
        w1_lo = [sb(f"w1_lo{i}", [P, KC, F], F32R) for i in range(RING)]
        w2_lo = [sb(f"w2_lo{i}", [P, FC, D], F32R) for i in range(RING)]
        b1_s = [sb(f"b1_s{i}", [P, FC]) for i in range(RING)]
        b2_s = [sb(f"b2_s{i}", [P, D]) for i in range(RING)]
        w1_hi = [sb(f"w1_hi{i}", [P, KC, F], F32R) for i in range(RING)]
        w2_hi = [sb(f"w2_hi{i}", [P, FC, D], F32R) for i in range(RING)]
        tokens = [sb(f"tokens{i}", [P, SC], I32) for i in range(RING)]
        xg = [sb(f"xg{i}", [P, SC, D]) for i in range(RING)]
        xg_hi = [sb(f"xg_hi{i}", [P, KC, SLOTS], F32R) for i in range(RING)]
        xg_lo = [sb(f"xg_lo{i}", [P, KC, SLOTS], F32R) for i in range(RING)]
        h_lo = sb("h_lo", [P, FC, SLOTS], F32R)
        h_t = sb("h_t", [P, FC, SLOTS])
        h_hi = sb("h_hi", [P, FC, SLOTS], F32R)
        y_s = [sb(f"y_s{i}", [P, SC, D]) for i in range(RING)]
        own_slots = [sb(f"own_slots{q}", [P, TC, TOP], I32) for q in range(2)]
        yb = [sb(f"yb{q}", [P, TC, TOP, D]) for q in range(2)]
        xb = [sb(f"xb{q}", [P, TC, D]) for q in range(2)]
        half_sum = sb("half_sum", [P, TC, D])
        res3 = sb("res3", [P, TC, D])
        stat3 = sb("stat3", [P, TC, 6])
        mv3 = sb("mv3", [P, TC, 2])
        var3 = sb("var3", [P, TC])
        rstd3 = sb("rstd3", [P, TC])
        ob = [sb(f"ob{q}", [P, TC, D]) for q in range(2)]
        xt_bank = bank("xt_bank")
        h_bank = [bank(f"h_bank{i}") for i in range(FC // 2)]
        y_bank = [bank(f"y_bank{i}") for i in range(RING)]

        consts = sem("tile_consts")
        plan = sem("tile_plan")
        passed = {e: sem(f"passed3_{e}") for e in ("pool", "dve", "sp")}
        w1_loaded = [sig(f"w1_loaded{i}", 32, 0) for i in range(RING)]
        w2_loaded = [sig(f"w2_loaded{i}", 32, 0) for i in range(RING)]
        tokens_loaded = [sig(f"tokens_loaded{i}", 16, 0) for i in range(RING)]
        gathered = [sig(f"gathered{i}", 16 * SC, 0) for i in range(RING)]
        y_stored = [Signal(sem(f"y_stored{i}"), 16, 16) for i in range(RING)]
        xt_filled, xt_taken = sig("xt_filled", 1), sig("xt_taken", 1)
        h_filled, h_taken = sig("h_filled", FC // 2), sig("h_taken", FC // 2)
        y_filled, y_taken = sig("y_filled", 1), sig("y_taken", 1)
        xg_hi_ready, w1_hi_ready, w2_hi_ready = sig("xg_hi_ready", 1, 0), sig("w1_hi_ready", 1, 0), sig("w2_hi_ready", 1, 0)
        w1_split, w2_split = sig("w1_split", 1, 0), sig("w2_split", 1, 0)
        h_hi_ready, h_split = sig("h_hi_ready", FC // 2, 0), sig("h_split", FC // 2, 0)
        slots_ready = Signal(sem("slots_ready"), 1, 2)
        rows_back = [sig(f"rows_back{q}", 16 * TC * TOP, 0) for q in range(2)]
        xb_loaded = [sig(f"xb_loaded{q}", 16, 0) for q in range(2)]
        out_stored = [Signal(sem(f"out_stored{q}"), 16, 16) for q in range(2)]
        sum_steps = Signal(sem("sum_steps"), 3, 6)
        stats3 = Signal(sem("stats3"), 1, 2)
        var3_ready, rstd3_ready = Signal(sem("var3_ready"), 1, 2), Signal(sem("rstd3_ready"), 1, 2)
        ob_ready = Signal(sem("ob_ready"), 1, 2)
        N_PLAN = 10

        block = stack.enter_context(nc.Block())

        @block.sync
        def _(sp):
            def pass_wait(s, value):
                if not (isinstance(value, int) and value <= 0):
                    sp.wait_ge(s.sem, value)
                    sp.sem_inc(passed["sp"], 1)

            def load(r, i):
                t = r * RING + i
                base = sp.value_load(tile_base[0:1, bass.ds(t, 1)], min_val=0, max_val=JUNK - SLOTS)
                e = sp.value_load(tile_expert[0:1, bass.ds(t, 1)], min_val=0, max_val=E - 1)
                pass_wait(gathered[i], gathered[i].at(r, 0))
                sp.dma_start(tokens[i][:], list_dram[bass.ds(base, SLOTS), :].rearrange("(p c) a -> p (c a)", p=P)).then_inc(tokens_loaded[i].sem, 16)
                pass_wait(y_taken, y_taken.at(t - RING, 1) if not isinstance(r, int) else 0)
                pass_wait(w1_split, w1_split.at(t - 1, 1))
                sp.dma_start(w1_s[:], w1[e].rearrange("(k p) f -> p k f", p=P)).then_inc(w1_loaded[i].sem, 16)
                sp.dma_start(b1_s[i][:], b1[e]).then_inc(w1_loaded[i].sem, 16)
                pass_wait(w2_split, w2_split.at(t - 1, 1))
                sp.dma_start(w2_s[:], w2[e].rearrange("(k p) d -> p k d", p=P)).then_inc(w2_loaded[i].sem, 16)
                sp.dma_start(b2_s[i][:], b2[e].broadcast_to([P, D])).then_inc(w2_loaded[i].sem, 16)

            def store(r, i):
                t = r * RING + i
                pass_wait(y_taken, y_taken.at(t, 1))
                sp.dma_start(y_dram.rearrange("(t p c) d -> t p c d", p=P, c=SC)[t], y_s[i][:]).then_inc(y_stored[i].sem, 16)

            sp.wait_ge(plan, N_PLAN)
            for i in range(RING):
                load(0, i)
            store(0, 0)
            with sp.Fori(1, ROUNDS) as r:
                for i in range(RING):
                    load(r, i)
                    if i == RING - 1:
                        store(r, 0)
                    else:
                        store(r - 1, i + 1)
            for i in range(1, RING):
                store(ROUNDS - 1, i)

            x2_rows, out_rows = (a.rearrange("(b c p) d -> b p c d", c=TC, p=P) for a in (x2_dram, out))

            def load_x2(r, q):
                b = 2 * r + q
                if not isinstance(r, int):
                    pass_wait(sum_steps, sum_steps.at(b - 2, 2))
                sp.dma_start(xb[q][:], x2_rows[b + 1]).then_inc(xb_loaded[q].sem, 16)

            def store_out(r, q):
                b = 2 * r + q
                pass_wait(ob_ready, ob_ready.at(b, 1))
                sp.dma_start(out_rows[b], ob[q][:]).then_inc(out_stored[q].sem, 16)

            load_x2(0, 0)
            load_x2(0, 1)
            with sp.Fori(1, B // 2) as r:
                for q in range(2):
                    store_out(r - 1, q)
                    load_x2(r, q)
            for q in range(2):
                store_out(B // 2 - 1, q)
            for q in range(2):
                sp.wait_ge(out_stored[q].sem, out_stored[q].at(B // 2, 0))

        @block.gpsimd
        def _(pool):
            pool.iota(tile_i[:], pattern=[[1, N_TILES]], base=0, channel_multiplier=0).then_inc(consts, 1)
            pool.iota(bound_i[:], pattern=[[SLOTS, MAX_TILES]], base=0, channel_multiplier=0).then_inc(consts, 1)
            pool.memset(half_e[:], -0.5).then_inc(consts, 1)
            pool.iota(region_i[:], pattern=[[REGION, E]], base=0, channel_multiplier=0).then_inc(consts, 1)
            pool.wait_ge(consts, 4)
            pool.tensor_copy(region[:], region_i[:]).then_inc(consts, 1)
            pool.tensor_copy(tile_no[:], tile_i[:]).then_inc(consts, 1)
            pool.tensor_copy(bound[:], bound_i[:]).then_inc(consts, 1)
            pool.sem_inc(var3_ready.sem, var3_ready.start)
            pool.sem_inc(rstd3_ready.sem, rstd3_ready.start)

            def gather(r, i):
                t = r * RING + i
                pool.wait_ge(tokens_loaded[i].sem, tokens_loaded[i].at(r, 16))
                pool.sem_inc(passed["pool"], 1)
                pool.wait_ge(xt_filled.sem, xt_filled.at(t - RING, 1))
                pool.sem_inc(passed["pool"], 1)
                for c in range(SC):
                    pool.indirect_dma_start(xg[i][:, c, :], None, x2_dram, bass.IndirectOffsetOnAxis(
                        ap=tokens[i][:, c:c + 1].bitcast(U32), axis=0)).then_inc(gathered[i].sem, 16)

            def low_w2(r, i):
                t = r * RING + i
                pool.wait_ge(w2_hi_ready.sem, w2_hi_ready.at(t, 1))
                pool.tensor_tensor(w2_lo[i][:], w2_s[:], w2_hi[i][:].bitcast(F32), ALU.subtract).then_inc(w2_split.sem, 1)

            def ahead(part, r, i, n):
                part(r + (i + n) // RING, (i + n) % RING)

            gather(0, 0)
            gather(0, 1)
            low_w2(0, 0)
            with pool.Fori(0, ROUNDS - 1) as r:
                for i in range(RING):
                    ahead(gather, r, i, 2)
                    ahead(low_w2, r, i, 1)
            gather(ROUNDS - 1, 2)
            low_w2(ROUNDS - 1, 1)
            low_w2(ROUNDS - 1, 2)
            for i in range(RING):
                pool.wait_ge(y_stored[i].sem, y_stored[i].at(ROUNDS, 0))

            def rows(r, q):
                b = 2 * r + q
                pool.wait_ge(slots_ready.sem, slots_ready.at(b, 1))
                pool.sem_inc(passed["pool"], 1)
                pool.wait_ge(sum_steps.sem, sum_steps.at(b - 2, 2))
                pool.sem_inc(passed["pool"], 1)
                for c in range(TC):
                    for j in range(TOP):
                        pool.indirect_dma_start(yb[q][:, c, j, :], None, y_dram, bass.IndirectOffsetOnAxis(
                            ap=own_slots[q][:, c, j:j + 1].bitcast(U32), axis=0)).then_inc(rows_back[q].sem, 16)

            def reciprocal_root(b):
                pool.wait_ge(stats3.sem, stats3.at(b, 1))
                pool.sem_inc(passed["pool"], 1)
                pool.tensor_scalar(var3[:], mv3[:, :, 1], EPS, None, ALU.add).then_inc(var3_ready.sem, 1)
                pool.wait_ge(var3_ready.sem, var3_ready.at(b, 1))
                pool.tensor_tensor(rstd3[:], var3[:], half_e[:], ALU.pow).then_inc(rstd3_ready.sem, 1)

            rows(0, 0)
            with pool.Fori(0, B // 2 - 1) as r:
                rows(r, 1)
                reciprocal_root(2 * r)
                rows(r + 1, 0)
                reciprocal_root(2 * r + 1)
            rows(B // 2 - 1, 1)
            reciprocal_root(B - 2)
            reciprocal_root(B - 1)

        @block.scalar
        def _(act):
            act.sem_inc(h_taken.sem, h_taken.start)

            def gelus(r, i):
                t = r * RING + i
                act.wait_ge(w1_loaded[i].sem, w1_loaded[i].at(r, 32))
                act.wait_ge(y_filled.sem, y_filled.at(t - 1, 1))
                for m in range(FC // 2):
                    act.wait_ge(h_filled.sem, h_filled.at(t, m + 1))
                    for n in range(2):
                        f = 2 * m + n
                        ins = nc.scalar.activation(h_t[:, f, :], h_bank[m][:, n * SLOTS:(n + 1) * SLOTS], ACT.Gelu,
                                                   bias=b1_s[i][:, f:f + 1])
                    ins.then_inc(h_taken.sem, 1)
                    act.wait_ge(h_taken.sem, h_taken.at(t, m + 1))
                    nc.scalar.copy(h_hi[:, 2 * m:2 * m + 2, :], h_t[:, 2 * m:2 * m + 2, :]).then_inc(h_hi_ready.sem, 1)

            def high_inputs(r, i):
                t = r * RING + i
                act.wait_ge(xt_filled.sem, xt_filled.at(t, 1))
                act.wait_ge(h_filled.sem, h_filled.at(t - RING, FC // 2))
                nc.scalar.copy(xg_hi[i][:].rearrange("p k s -> p (k s)"), xt_bank[:, :]).then_inc(xg_hi_ready.sem, 1)
                act.wait_ge(w1_loaded[i].sem, w1_loaded[i].at(r, 32))
                nc.scalar.copy(w1_hi[i][:], w1_s[:]).then_inc(w1_hi_ready.sem, 1)

            high_inputs(0, 0)
            with act.Fori(0, ROUNDS - 1) as r:
                for i in range(RING):
                    gelus(r, i)
                    high_inputs(r + (i + 1) // RING, (i + 1) % RING)
            for i in range(RING):
                gelus(ROUNDS - 1, i)
                if i + 1 < RING:
                    high_inputs(ROUNDS - 1, i + 1)

        @block.vector
        def _(dve):
            def apart(s, value):
                dve.wait_ge(s.sem, value)
                dve.sem_inc(passed["dve"], 1)

            def step(ins, n):
                ins.then_inc(plan, 1)
                dve.wait_ge(plan, n)

            dve.wait_ge(consts, 7)
            dve.memset(one_e[:], 1.0)
            step(dve.tensor_tensor(has_tile[:], counts[:].unsqueeze(2).broadcast_to([P, E, MAX_TILES]),
                                   bound[:].unsqueeze(1).broadcast_to([P, E, MAX_TILES]), ALU.is_gt), 1)
            step(dve.tensor_reduce(tiles_of[:], has_tile[:], AX_X, ALU.add), 2)
            step(dve.tensor_tensor_scan(last_tile[:], one_e[:], tiles_of[:], 0.0, ALU.mult, ALU.add), 3)
            step(dve.tensor_tensor(is_past[:], tile_no[:].unsqueeze(2).broadcast_to([P, N_TILES, E]),
                                   last_tile[:].unsqueeze(1).broadcast_to([P, N_TILES, E]), ALU.is_ge), 4)
            step(dve.tensor_tensor(past_tiles[:], is_past[:], tiles_of[:].unsqueeze(1).broadcast_to([P, N_TILES, E]),
                                   ALU.mult), 5)
            step(dve.tensor_reduce(expert_f[:], is_past[:], AX_X, ALU.add), 6)
            step(dve.tensor_reduce(first_f[:], past_tiles[:], AX_X, ALU.add), 7)
            dve.tensor_scalar(expert_rows_f[:], expert_f[:], float(REGION), None, ALU.mult)
            step(dve.tensor_tensor(first_f[:], tile_no[:], first_f[:], ALU.subtract), 8)
            dve.tensor_scalar(tile_expert[:], expert_f[:], float(E - 1), None, ALU.min)
            step(dve.scalar_tensor_tensor(out=expert_rows_f[:], in0=first_f[:], scalar=float(SLOTS), in1=expert_rows_f[:],
                                          op0=ALU.mult, op1=ALU.add), 9)
            dve.tensor_copy(tile_base[:], expert_rows_f[:]).then_inc(plan, 1)
            own = slots[:, 1:B + 1, :, :].rearrange("p b c j -> p (b c j)")
            dve.memset(closing[:, 0:1], 0.0)
            dve.tensor_scalar(closing[:, 1:E], tiles_of[:, 0:E - 1], float(SLOTS), float(REGION), ALU.mult, ALU.subtract)
            step(dve.tensor_tensor(in_region[:], own.unsqueeze(2).broadcast_to([P, B * TC * TOP, E]),
                                   region[:].unsqueeze(1).broadcast_to([P, B * TC * TOP, E]), ALU.is_ge), 11)
            step(dve.tensor_tensor(gaps[:], in_region[:], closing[:].unsqueeze(1).broadcast_to([P, B * TC * TOP, E]),
                                   ALU.mult), 12)
            step(dve.tensor_reduce(gap[:], gaps[:], AX_X, ALU.add), 13)
            step(dve.tensor_tensor(row_no[:].rearrange("p b c j -> p (b c j)"), own, gap[:], ALU.add), 14)
            for s in (xt_taken, y_taken, slots_ready, sum_steps, stats3, ob_ready, *y_stored, *out_stored):
                dve.sem_inc(s.sem, s.start)

            def split_inputs(r, i):
                t = r * RING + i
                dve.wait_ge(w2_loaded[i].sem, w2_loaded[i].at(r, 32))
                dve.tensor_copy(w2_hi[i][:], w2_s[:]).then_inc(w2_hi_ready.sem, 1)
                dve.wait_ge(xg_hi_ready.sem, xg_hi_ready.at(t, 1))
                dve.tensor_tensor(xg_lo[i][:].rearrange("p k s -> p (k s)"), xt_bank[:, :],
                                  xg_hi[i][:].bitcast(F32).rearrange("p k s -> p (k s)"), ALU.subtract).then_inc(xt_taken.sem, 1)
                dve.wait_ge(w1_hi_ready.sem, w1_hi_ready.at(t, 1))
                dve.tensor_tensor(w1_lo[i][:], w1_s[:], w1_hi[i][:].bitcast(F32), ALU.subtract).then_inc(w1_split.sem, 1)

            def low_hidden(r, i):
                t = r * RING + i
                for m in range(FC // 2):
                    f = slice(2 * m, 2 * m + 2)
                    dve.wait_ge(h_hi_ready.sem, h_hi_ready.at(t, m + 1))
                    dve.tensor_tensor(h_lo[:, f, :], h_t[:, f, :], h_hi[:, f, :].bitcast(F32), ALU.subtract).then_inc(h_split.sem, 1)

            def take_y(r, i):
                t = r * RING + i
                dve.wait_ge(w2_loaded[i].sem, w2_loaded[i].at(r, 32))
                dve.wait_ge(y_stored[i].sem, y_stored[i].at(r, 0))
                dve.wait_ge(y_filled.sem, y_filled.at(t, 1))
                dve.tensor_tensor(y_s[i][:], y_bank[i][:, :].rearrange("p (c d) -> p c d", c=SC),
                                  b2_s[i][:].unsqueeze(1).broadcast_to([P, SC, D]), ALU.add).then_inc(y_taken.sem, 1)

            split_inputs(0, 0)
            with dve.Fori(0, ROUNDS - 1) as r:
                for i in range(RING):
                    low_hidden(r, i)
                    split_inputs(r + (i + 1) // RING, (i + 1) % RING)
                    take_y(r, i)
            for i in range(RING):
                low_hidden(ROUNDS - 1, i)
                if i + 1 < RING:
                    split_inputs(ROUNDS - 1, i + 1)
                take_y(ROUNDS - 1, i)

            def places(r, q):
                b = 2 * r + q
                dve.tensor_copy(own_slots[q][:], row_no[:, b, :, :] if isinstance(b, int) else
                                row_no[:, bass.ds(b, 1), :, :].rearrange("p o c j -> p (o c) j")).then_inc(slots_ready.sem, 1)

            def combine(r, q):
                b = 2 * r + q
                g = gates[:, b + 1, :, :] if isinstance(b, int) else gates[:, bass.ds(b + 1, 1), :, :].rearrange("p o c j -> p (o c) j")
                dve.wait_ge(xb_loaded[q].sem, xb_loaded[q].at(r, 16))
                dve.wait_ge(rows_back[q].sem, rows_back[q].at(r, rows_back[q].per))
                for c in range(TC):
                    ins = dve.scalar_tensor_tensor(out=half_sum[:, c, :], in0=yb[q][:, c, 0, :], scalar=g[:, c, 0:1],
                                                   in1=xb[q][:, c, :], op0=ALU.mult, op1=ALU.add)
                ins.then_inc(sum_steps.sem, 1)
                dve.wait_ge(sum_steps.sem, sum_steps.at(b, 1))
                for c in range(TC):
                    ins = dve.scalar_tensor_tensor(out=res3[:, c, :], in0=yb[q][:, c, 1, :], scalar=g[:, c, 1:2],
                                                   in1=half_sum[:, c, :], op0=ALU.mult, op1=ALU.add)
                ins.then_inc(sum_steps.sem, 1)
                dve.wait_ge(sum_steps.sem, sum_steps.at(b, 2))
                for c in range(TC):
                    ins = dve.bn_stats(stat3[:, c, :], res3[:, c, :])
                ins.then_inc(sum_steps.sem, 1)
                apart(sum_steps, sum_steps.at(b, 3))
                for c in range(TC):
                    ins = dve.bn_aggr(mv3[:, c, :], stat3[:, c, :])
                ins.then_inc(stats3.sem, 1)
                dve.wait_ge(out_stored[q].sem, out_stored[q].at(r, 0))
                dve.wait_ge(rstd3_ready.sem, rstd3_ready.at(b, 1))
                for c in range(TC):
                    ins = dve.tensor_scalar(ob[q][:, c, :], res3[:, c, :], mv3[:, c, 0:1], rstd3[:, c:c + 1],
                                            ALU.subtract, ALU.mult)
                ins.then_inc(ob_ready.sem, 1)

            places(0, 0)
            with dve.Fori(0, B // 2 - 1) as r:
                places(r, 1)
                combine(r, 0)
                places(r + 1, 0)
                combine(r, 1)
            places(B // 2 - 1, 1)
            combine(B // 2 - 1, 0)
            combine(B // 2 - 1, 1)

        @block.tensor
        def _(pe):
            for s in (xt_filled, h_filled, y_filled):
                pe.sem_inc(s.sem, s.start)
            matmul, transpose = nc.tensor.matmul, nc.tensor.transpose

            def rows_transposed(r, i):
                t = r * RING + i
                pe.wait_ge(gathered[i].sem, gathered[i].at(r, gathered[i].per))
                pe.wait_ge(xt_taken.sem, xt_taken.at(t - 1, 1))
                for k in range(KC):
                    for c in range(SC):
                        ins = transpose(xt_bank[:, k * SLOTS + c * P:k * SLOTS + (c + 1) * P],
                                        xg[i][:, c, k * P:(k + 1) * P], ident[:])
                ins.then_inc(xt_filled.sem, 1)

            part_pairs = ((0, 0), (0, 1), (1, 0))

            def first_product(r, i):
                t = r * RING + i
                w, xs = (w1_hi[i], w1_lo[i]), (xg_hi[i], xg_lo[i])
                pe.wait_ge(w1_split.sem, w1_split.at(t, 1))
                pe.wait_ge(xt_taken.sem, xt_taken.at(t, 1))
                for m in range(FC // 2):
                    pe.wait_ge(h_taken.sem, h_taken.at(t - 1, m + 1))
                    for n in range(2):
                        f = 2 * m + n
                        for k in range(KC):
                            for a, z in part_pairs:
                                ins = matmul(h_bank[m][:, n * SLOTS:(n + 1) * SLOTS], w[a][:, k, f * P:(f + 1) * P],
                                             xs[z][:, k, :], start=(k == 0 and a + z == 0), stop=(k == KC - 1 and a == 1))
                    ins.then_inc(h_filled.sem, 1)

            def second_product(r, i):
                t = r * RING + i
                h, w = (h_hi, h_lo), (w2_hi[i], w2_lo[i])
                pe.wait_ge(w2_split.sem, w2_split.at(t, 1))
                pe.wait_ge(y_taken.sem, y_taken.at(t - RING, 1))
                for c in range(SC):
                    for f in range(FC):
                        if c == 0 and f % 2 == 0:
                            pe.wait_ge(h_split.sem, h_split.at(t, f // 2 + 1))
                        for a, z in part_pairs:
                            ins = matmul(y_bank[i][:, c * D:(c + 1) * D], h[a][:, f, c * P:(c + 1) * P], w[z][:, f, :],
                                         start=(f == 0 and a + z == 0), stop=(f == FC - 1 and a == 1))
                ins.then_inc(y_filled.sem, 1)

            rows_transposed(0, 0)
            with pe.Fori(0, ROUNDS - 1) as r:
                for i in range(RING):
                    first_product(r, i)
                    rows_transposed(r + (i + 1) // RING, (i + 1) % RING)
                    second_product(r, i)
            for i in range(RING):
                first_product(ROUNDS - 1, i)
                if i + 1 < RING:
                    rows_transposed(ROUNDS - 1, i + 1)
                second_product(ROUNDS - 1, i)


def kernel(**inputs):
    from concourse import bacc
    from concourse.bass_utils import run_bass_kernel_spmd

    def a(name):
        return np.asarray(inputs[name])

    def by_partition(v):
        return np.ascontiguousarray(v.reshape(-1, P).T)

    b_in = a("L0_attn_b_in")
    smear, scale = a("L0_attn_smear_factor"), a("L0_attn_log_scale")
    heads_rows = np.concatenate([smear.reshape(EC, HPC).T, scale.reshape(EC, HPC).T], axis=1)
    arrays = {
        "x": a("x"),
        "ctx": a("ctx_1024"),
        "mask": np.ascontiguousarray(a("mask_BxS2_bk0")).reshape(B, 1, S).view(np.int32),
        "w_in_t": a("L0_attn_W_in").T,
        "w_out_t": a("L0_attn_W_out").T,
        "wq": a("L0_xattn_Wq"),
        "wkv": a("L0_xattn_Wkv"),
        "wout": a("L0_xattn_Wout"),
        "cols": np.concatenate([by_partition(v) for v in (
            a("L0_attn_in_ln_w"), a("L0_attn_in_ln_b"), b_in[0:D_EXP], b_in[D_EXP:2 * D_EXP],
            b_in[3 * D_EXP:4 * D_EXP], a("L0_xattn_g1"), a("L0_xattn_b1"), a("L0_xattn_g2"), a("L0_xattn_b2"),
            b_in[2 * D_EXP:3 * D_EXP])], axis=1),
        "rows": np.concatenate([a("L0_attn_out_ln_w"), a("L0_attn_out_ln_b"),
                                a("L0_ffn_br")])[None, :],
        "heads_rows": heads_rows,
        "y_bias": b_in[4 * D_EXP:][:, None],
        "wr": a("L0_ffn_Wr"),
        "w1": a("L0_ffn_W1"),
        "b1": a("L0_ffn_b1").reshape(E, FC, P).transpose(0, 2, 1),
        "w2": a("L0_ffn_W2"),
        "b2": a("L0_ffn_b2").reshape(E, 1, D),
    }
    arrays = {k: np.ascontiguousarray(v) for k, v in arrays.items()}
    nc = bacc.Bacc("TRN2", target_bir_lowering=False, num_devices=1)
    args = [nc.dram_tensor(k, v.shape, mybir.dt.from_np(v.dtype), kind="ExternalInput").ap() for k, v in arrays.items()]
    out = nc.dram_tensor("y", (T, D), F32, kind="ExternalOutput").ap()
    decoder_layer(nc, *args, out)
    r = run_bass_kernel_spmd(nc, [arrays], core_ids=[0])
    return r.results[0]["y"].reshape(B, S, D)
```

```python
from contextlib import ExitStack

import numpy as np

import concourse.bass as bass
from concourse import mybir

F32 = mybir.dt.float32
F32R = mybir.dt.float32r
U8 = mybir.dt.uint8
I32 = mybir.dt.int32
U32 = mybir.dt.uint32
ALU = mybir.AluOpType
ACT = mybir.ActivationFunctionType
AX_X = mybir.AxisListType.X

P = 128
B, S, D = 16, 256, 256
TC = S // P
KC = D // P
EPS = 1e-5

HEADS = 16
DH_A = 32
D_EXP = HEADS * DH_A
EC = D_EXP // P
HPC = P // DH_A
W_COLS = 4 * D_EXP + HEADS
NEG_BIG = -1.0e10

DH_X = 64
INNER = HEADS * DH_X
XC = INNER // P
N_KEYS = 2 * S
NC = N_KEYS // P
PX_RING = KC * INNER // N_KEYS
X_SCALE = 1.0 / float(np.sqrt(DH_X))
MASKED = -1.0e30

E, F, TOP = 8, 1024, 2
T = B * S
FC = F // P
SLOTS = 256
N_TILES = (T * TOP + E * (SLOTS - 1)) // SLOTS
REGION = T
SPARE = E * REGION
JUNK = SPARE + (N_TILES + 1) * SLOTS
LIST = JUNK + E * REGION + S
SC = SLOTS // P
MAX_TILES = REGION // SLOTS
RING = 3
ROUNDS = N_TILES // RING
assert N_TILES % RING == 0



class Signal:

    def __init__(self, sem, per, start=None):
        self.sem, self.per = sem, per
        self.start = per if start is None else start

    def at(self, b, n):
        return b * self.per + (self.start + n)


def decoder_layer(nc, x, ctx_in, mask, w_in_t, w_out_t, wq, wkv, wout, cols, rows, heads_rows, y_bias, wr,
                  w1, b1, w2, b2, out):
    x1_dram = nc.dram_tensor("x1_rows", (T + S, D), F32).ap()
    x2_dram = nc.dram_tensor("x2_rows", (T + S, D), F32).ap()
    list_dram = nc.dram_tensor("expert_list", (LIST, 1), I32).ap()
    stack = ExitStack()
    with stack:
        def sem(name):
            return stack.enter_context(nc.semaphore(name))

        def sig(name, per, start=None):
            return Signal(sem(name), per, start)

        def keep(name, shape, dt=F32):
            return stack.enter_context(nc.sbuf_tensor(name, shape, dt))

        ident = keep("ident", [P, P])
        gates = keep("gates", [P, B + 1, TC, TOP])
        slots = keep("slots", [P, B + 1, TC, TOP])
        counts = keep("counts", [P, E])
        with ExitStack() as inner:
            def half(name, shape):
                return inner.enter_context(nc.sbuf_tensor(name, shape, F32))

            vx = half("x_vx", [P, NC, INNER])
            pt = half("x_pt", [P, PX_RING, N_KEYS])
            wkv_s = vx[:].rearrange("p (k h) n -> p k (h n)", k=KC)
            wq_s = pt[:].rearrange("p (k h) n -> p k (h n)", k=KC)
            wox = half("wox", [P, XC, D])
            wr_s = half("wr_s", [P, KC, E])
            col = half("col", [P, 28])
            row = half("row", [P, 2 * D + E])
            self_phase(nc, sem, sig, x, w_in_t, w_out_t, wq, wkv, wout, wr, cols, rows, heads_rows, y_bias, x1_dram,
                       list_dram, ident, wq_s, wkv_s, wox, wr_s, col, row)
            cross_phase(nc, sem, sig, ctx_in, mask, x1_dram, x2_dram, list_dram, ident, vx, pt, wq_s, wkv_s, wox, wr_s, col,
                        row, gates, slots, counts)
        expert_phase(nc, sem, w1, b1, w2, b2, x2_dram, list_dram, out, ident, gates, slots, counts)


def self_phase(nc, sem, sig, x, w_in_t, w_out_t, wq, wkv, wout, wr, cols, rows, heads_rows, y_bias, x1_dram, list_dram,
               ident, wq_s, wkv_s, wox, wr_s, col, row):
    FILLS = 12
    XT, YP, QP, WO, KP, PP, VP = 0, 1, 2, 4, 6, 8, 10
    LNS = LN_X, LN_OUT, LN_RES = range(3)
    PROB_RING, PT_RING = 6, 4
    with ExitStack() as stack:
        def sb(name, shape, dt=F32):
            return stack.enter_context(nc.sbuf_tensor(name, shape, dt))

        def bank(name):
            return stack.enter_context(nc.psum_tensor(name, [P, 512], F32))

        win_s = wkv_s
        win_hi = sb("win_hi", [P, KC, 4 * D_EXP], F32R)
        win_lo = sb("win_lo", [P, KC, 4 * D_EXP], F32R)
        win_y = sb("win_y", [P, KC, W_COLS - 4 * D_EXP])
        wo = sb("wo", [P, EC, D])
        smls = sb("smls", [P, 2 * EC])
        by = sb("by", [HEADS, 1])
        inw, inb, bq, bk, bp = (col[:, a:z] for a, z in ((0, 2), (2, 4), (4, 8), (8, 12), (12, 16)))
        bv, onw, onb = col[:, 24:28], row[:, 0:256], row[:, 256:512]
        smear = sb("smear", [P, EC])
        unsmear = sb("unsmear", [P, EC])
        q_scale = sb("q_scale", [P, EC])
        q_bias = sb("q_bias", [P, EC])
        half_bp = sb("half_bp", [P, EC])
        half_by = sb("half_by", [HEADS, 1])
        causal = sb("causal", [P, S])
        minus_half = sb("minus_half", [P, TC])
        zero_list = sb("zero_list", [P, JUNK // P], I32)
        zeros = sb("zeros", [P, 512])
        own_rows = sb("own_rows", [P, HPC, EC])
        x_raw = sb("x_raw", [P, TC, D])
        zx = sb("zx", [P, TC, D])
        xn_t = sb("xn_t", [P, KC, S])
        xn_hi = sb("xn_hi", [P, KC, S], F32R)
        xn_lo = sb("xn_lo", [P, KC, S], F32R)
        gate_tanh = sb("gate_tanh", [HEADS, S])
        one_keep = sb("one_keep", [HEADS, S])
        gate_sig = sb("gate_sig", [HEADS, S])
        pos = sb("pos", [HEADS, S])
        pos_parts = sb("pos_parts", [64, S], F32R)
        q_t = sb("q_t", [P, EC, S])
        k_t = sb("k_t", [P, EC, S])
        k_prev = sb("k_prev", [P, EC, S + 1])
        q_hi = sb("q_hi", [P, EC, S], F32R)
        q_lo = sb("q_lo", [P, EC, S], F32R)
        k_hi = sb("k_hi", [P, EC, S], F32R)
        k_lo = sb("k_lo", [P, EC, S], F32R)
        q_parts = sb("q_parts", [P, HPC, EC, S], F32R)
        k_parts = sb("k_parts", [P, HPC, EC, S], F32R)
        v_a = sb("v_a", [P, TC, D_EXP])
        p_tanh = sb("p_tanh", [P, EC, S])
        p_half = sb("p_half", [P, EC, S])
        silu_p = sb("silu_p", [P, EC, S])
        gated_t = sb("gated_t", [P, EC, S])
        prob = sb("prob", [P, PROB_RING, 3 * P])
        low = sb("low", [P, HEADS, TC])
        den = sb("den", [P, HEADS, TC])
        rden = sb("rden", [P, HEADS, TC])
        pt = sb("pt", [P, PT_RING, 3 * P])
        x_again = sb("x_again", [P, TC, D])
        x_res = sb("x_res", [P, TC, D])
        out_s = sb("out_s", [P, TC, D])
        centred = sb("centred", [P, TC, D])
        res1 = sb("res1", [P, TC, D])
        x1 = sb("x1", [P, TC, D])
        stat = sb("stat", [P, len(LNS), TC, 6])
        mv = sb("mv", [P, len(LNS), TC, 2])
        var_eps = sb("var_eps", [P, len(LNS), TC])
        rstd = sb("rstd", [P, len(LNS), TC])
        proj = [bank(f"proj{i}") for i in range(2)]
        score = [bank(f"score{i}") for i in range(2)]
        ptb = [bank(f"ptb{i}") for i in range(2)]
        av = [bank(f"av{i}") for i in range(2)]

        in_weights, late_weights = sem("in_weights"), sem("late_weights")
        consts, consts_v, consts_a = sem("consts"), sem("consts_v"), sem("consts_a")
        list_zeroed = sem("list_zeroed")
        passed = {e: sem(f"passed_{e}") for e in ("pool", "dve", "sp")}
        x_loaded, again_loaded = sig("x_loaded", 16), sig("again_loaded", 16, 0)
        parts_loaded = [sig(f"parts_loaded{g}", 16 * 8) for g in range(HPC)]
        x1_stored = sig("x1_stored", 16)
        residual_ready = sig("residual_ready", 1)

        NTH = (1, 1, 2)

        def norm_signals(name):
            apart_ = [sig(f"{name}{n}", max(k for k, g in zip(NTH, (0, 1, 1)) if g == n)) for n in range(2)]
            return [apart_[g] for g in (0, 1, 1)]

        half_stats, stats_ready, var_ready, rstd_ready = (
            norm_signals(name) for name in ("half_stats", "stats_ready", "var_ready", "rstd_ready"))
        zx_ready, x_res_ready, x1_ready = sig("zx_ready", 1), sig("x_res_ready", 1), sig("x1_ready", 1)
        proj_filled = sig("proj_filled", FILLS)
        proj_taken = [sig(f"proj_taken{i}", FILLS // 2) for i in range(2)]
        k_prev_ready, k_hi_ready = sig("k_prev_ready", 2), sig("k_hi_ready", 2)
        pos_steps, p_half_ready = sig("pos_steps", 4), sig("p_half_ready", 2)
        q_split, k_split = sig("q_split", 2), sig("k_split", 2)
        out_used = sig("out_used", 1)
        silu_ready = sig("silu_ready", 1, 0)
        score_filled, score_taken = sig("score_filled", HEADS), sig("score_taken", HEADS)
        exp_ready, rden_ready, prob_ready = sig("exp_ready", HEADS), sig("rden_ready", HEADS), sig("prob_ready", HEADS)
        pt_filled = sig("pt_filled", HEADS)
        pt_taken = [sig(f"pt_taken{i}", HEADS // 2) for i in range(2)]
        av_done, gated = sig("av_done", HEADS), sig("gated", 2, 0)
        N_CONSTS, N_VCONSTS, N_IN, N_LATE = 10, 6 + KC, 16 * 10, 16 * 4
        xn_hi_ready, xn_split = sig("xn_hi_ready", 1), sig("xn_split", 1)

        block = stack.enter_context(nc.Block())

        @block.sync
        def _(sp):
            def rows_of(nb):
                return x[nb].rearrange("(c p) d -> p c d", p=P)

            def pass_wait(s, value):
                sp.wait_ge(s.sem, value)
                sp.sem_inc(passed["sp"], 1)

            def spread_to(parts, g, sources):
                for place, src in enumerate(sources):
                    sp.dma_start(parts[DH_A * place:DH_A * (place + 1), g, :, :].bitcast(F32),
                                 src[DH_A * g:DH_A * (g + 1), :, :].bitcast(F32)).then_inc(parts_loaded[g].sem, 16)

            def spread_q_and_pos(b, g):
                sp.wait_ge(score_filled.sem, score_filled.at(b, EC * g + EC))
                spread_to(q_parts, g, (q_hi, q_lo, q_hi))
                for n in range(2):
                    sp.dma_start(k_parts[3 * DH_A + n * HEADS:3 * DH_A + (n + 1) * HEADS, g, :, :].bitcast(F32),
                                 pos_parts[32 * n:32 * n + HEADS, :].bitcast(F32).unsqueeze(1).broadcast_to([HEADS, EC, S])).then_inc(parts_loaded[g].sem, 16)

            def spread_early(b):
                sp.wait_ge(q_split.sem, q_split.at(b, 2))
                sp.wait_ge(pos_steps.sem, pos_steps.at(b, 4))
                for g in range(HPC - 1):
                    spread_q_and_pos(b, g)
                sp.wait_ge(k_split.sem, k_split.at(b, 2))
                for g in range(HPC - 1):
                    spread_to(k_parts, g, (k_hi, k_hi, k_lo))

            def spread_last(b):
                g = HPC - 1
                spread_q_and_pos(b, g)
                spread_to(k_parts, g, (k_hi, k_hi, k_lo))

            sp.dma_start(x_raw[:], rows_of(0)).then_inc(x_loaded.sem, 16)
            sp.dma_start(col[:], cols).then_inc(in_weights, 16)
            sp.dma_start(row[:], rows.broadcast_to([P, rows.shape[1]])).then_inc(in_weights, 16)
            w_in_rows = w_in_t.rearrange("(k p) n -> p k n", p=P)
            sp.dma_start(win_s, w_in_rows[:, :, 0:4 * D_EXP]).then_inc(in_weights, 16)
            sp.dma_start(win_y[:], w_in_rows[:, :, 4 * D_EXP:W_COLS]).then_inc(in_weights, 16)
            sp.dma_start(x_again[:], rows_of(0)).then_inc(again_loaded.sem, 16)
            sp.wait_ge(consts, N_CONSTS)
            sp.dma_start(list_dram[0:JUNK, :].rearrange("(p n) a -> p (n a)", p=P), zero_list[:]).then_inc(list_zeroed, 16)
            sp.wait_ge(zx_ready.sem, zx_ready.at(-1, 1))
            sp.dma_start(x_raw[:], rows_of(1)).then_inc(x_loaded.sem, 16)
            sp.wait_ge(consts_v, N_VCONSTS)
            spread_early(-1)
            spread_last(-1)
            sp.dma_start(wkv_s, wkv.rearrange("(k p) n -> p k n", p=P)).then_inc(late_weights, 16)
            sp.dma_start(wq_s, wq.rearrange("(k p) n -> p k n", p=P)).then_inc(late_weights, 16)
            sp.dma_start(wox[:], wout.rearrange("(m p) n -> p m n", p=P)).then_inc(late_weights, 16)
            sp.dma_start(wr_s[:], wr.rearrange("(k p) n -> p k n", p=P)).then_inc(late_weights, 16)
            with sp.Fori(0, B) as b:
                pass_wait(zx_ready, zx_ready.at(b, 1))
                sp.dma_start(x_raw[:], rows_of((b + 2) % B)).then_inc(x_loaded.sem, 16)
                pass_wait(x_res_ready, x_res_ready.at(b, 1))
                sp.dma_start(x_again[:], rows_of(b)).then_inc(again_loaded.sem, 16)
                spread_early(b)
                pass_wait(x1_ready, x1_ready.at(b, 1))
                sp.dma_start(x1_dram.rearrange("(b c p) d -> b p c d", c=TC, p=P)[b], x1[:]).then_inc(x1_stored.sem, 16)
                spread_last(b)
            sp.wait_ge(x1_ready.sem, x1_ready.at(B, 1))
            sp.dma_start(x1_dram.rearrange("(b c p) d -> b p c d", c=TC, p=P)[B], x1[:]).then_inc(x1_stored.sem, 16)
            sp.wait_ge(x1_stored.sem, x1_stored.at(B, 16))
            sp.wait_ge(list_zeroed, 16)
            sp.wait_ge(late_weights, N_LATE)
            sp.wait_ge(x_loaded.sem, x_loaded.at(B, 16))
            for g in range(HPC):
                sp.wait_ge(parts_loaded[g].sem, parts_loaded[g].at(B - 1, parts_loaded[g].per))

        @block.gpsimd
        def _(pool):
            pool.memset(ident[:], 0.0).then_inc(consts, 1)
            pool.memset(causal[:], 0.0).then_inc(consts, 1)
            pool.memset(minus_half[:], -0.5).then_inc(consts, 1)
            pool.memset(zero_list[:], 0).then_inc(consts, 1)
            pool.memset(zeros[:], 0.0).then_inc(consts, 1)
            pool.memset(own_rows[:], 0.0).then_inc(consts, 1)
            pool.wait_ge(consts, 6)
            pool.affine_select(out=own_rows[:], in_=own_rows[:], compare_op=ALU.not_equal, fill=1.0, base=-3 * DH_A,
                               pattern=[[-1, HPC], [-HPC, EC]], channel_multiplier=1).then_inc(consts, 1)
            pool.wait_ge(consts, 7)
            pool.affine_select(out=own_rows[:], in_=own_rows[:], compare_op=ALU.not_equal, fill=1.0, base=-3 * DH_A - HEADS,
                               pattern=[[-1, HPC], [-HPC, EC]], channel_multiplier=1).then_inc(consts, 1)
            pool.affine_select(out=ident[:], in_=ident[:], compare_op=ALU.not_equal, fill=1.0, base=0,
                               pattern=[[-1, P]], channel_multiplier=1).then_inc(consts, 1)
            pool.affine_select(out=causal[:], in_=causal[:], compare_op=ALU.is_ge, fill=NEG_BIG, base=P,
                               pattern=[[-1, S]], channel_multiplier=1).then_inc(consts, 1)
            pool.wait_ge(consts, N_CONSTS)

            def reciprocal_root(b, ln):
                pool.wait_ge(stats_ready[ln].sem, stats_ready[ln].at(b, NTH[ln]))
                pool.sem_inc(passed["pool"], 1)
                pool.tensor_scalar(var_eps[:, ln, :], mv[:, ln, :, 1], EPS, None, ALU.add).then_inc(var_ready[ln].sem, 1)
                pool.wait_ge(var_ready[ln].sem, var_ready[ln].at(b, NTH[ln]))
                pool.tensor_tensor(rstd[:, ln, :], var_eps[:, ln, :], minus_half[:], ALU.pow).then_inc(rstd_ready[ln].sem, 1)

            def low_q(b):
                for n in range(2):
                    m = slice(2 * n, 2 * n + 2)
                    f = QP + n
                    pool.wait_ge(proj_taken[f % 2].sem, proj_taken[f % 2].at(b, f // 2 + 1))
                    pool.tensor_tensor(q_lo[:, m, :], q_t[:, m, :], q_hi[:, m, :].bitcast(F32), ALU.subtract).then_inc(q_split.sem, 1)

            def low_k(b):
                for n in range(2):
                    m = slice(2 * n, 2 * n + 2)
                    pool.wait_ge(k_hi_ready.sem, k_hi_ready.at(b, n + 1))
                    pool.tensor_tensor(k_lo[:, m, :], k_t[:, m, :], k_hi[:, m, :].bitcast(F32), ALU.subtract).then_inc(k_split.sem, 1)

            def residual(b):
                pool.wait_ge(again_loaded.sem, again_loaded.at(b, 16))
                pool.wait_ge(residual_ready.sem, residual_ready.at(b - 1, 1))
                pool.tensor_tensor(x_res[:], x_again[:], onb.unsqueeze(1).broadcast_to([P, TC, D]), ALU.add).then_inc(x_res_ready.sem, 1)

            pool.sem_inc(x_res_ready.sem, 1)
            for s in (var_ready, rstd_ready):
                for ln in (LN_OUT, LN_RES):
                    pool.sem_inc(s[ln].sem, 1)
            reciprocal_root(-1, LN_X)
            pool.wait_ge(in_weights, N_IN)
            low_q(-1)
            low_k(-1)
            reciprocal_root(0, LN_X)
            with pool.Fori(0, B) as b:
                residual(b)
                low_q(b)
                for ln in (LN_OUT, LN_RES):
                    reciprocal_root(b, ln)
                low_k(b)
                reciprocal_root(b + 1, LN_X)
            residual(B)
            for ln in (LN_OUT, LN_RES):
                reciprocal_root(B, ln)

        @block.scalar
        def _(act):
            act.dma_start(by[:], y_bias).then_inc(in_weights, 16)
            for hh in range(HPC):
                act.dma_start(smls[DH_A * hh:DH_A * (hh + 1), :],
                              heads_rows[hh:hh + 1, 0:2 * EC].broadcast_to([DH_A, 2 * EC])).then_inc(in_weights, 16)
            act.dma_start(wo[:], w_out_t.rearrange("(m p) n -> p m n", p=P)).then_inc(in_weights, 16)
            act.wait_ge(in_weights, N_IN)
            nc.scalar.activation(smear[:], smls[:, 0:EC], ACT.Tanh, scale=0.5).then_inc(consts_a, 1)
            nc.scalar.activation(q_scale[:], smls[:, EC:2 * EC], ACT.Exp, scale=-2.0).then_inc(consts_a, 1)
            for k in range(KC):
                nc.scalar.copy(win_hi[:, k, :], win_s[:, k, :]).then_inc(consts_a, 1)
            act.wait_ge(consts_v, N_VCONSTS)

            def taken(ins, f):
                ins.then_inc(proj_taken[f % 2].sem, 1)

            def filled(b, f):
                act.wait_ge(proj_filled.sem, proj_filled.at(b, f + 1))

            def exps(b, u):
                act.wait_ge(score_taken.sem, score_taken.at(b, u + 1))
                slot = prob[:, u % PROB_RING, :]
                for c in range(TC):
                    s = slot[:, 0:P] if c == 0 else slot[:, P:P + S]
                    ins = nc.scalar.activation(s, s, ACT.Exp, bias=low[:, u, c:c + 1], scale=-1.0, accum_out=den[:, u, c:c + 1])
                ins.then_inc(exp_ready.sem, 1)

            def take_transposed(b, u):
                act.wait_ge(pt_filled.sem, pt_filled.at(b, u + 1))
                act.wait_ge(av_done.sem, av_done.at(b, u - PT_RING + 1))
                nc.scalar.copy(pt[:, u % PT_RING, :], ptb[u % 2][:, 0:3 * P]).then_inc(pt_taken[u % 2].sem, 1)

            def take_xt(b):
                filled(b, XT)
                for k in range(KC):
                    ins = nc.scalar.activation(xn_t[:, k, :], proj[XT % 2][:, k * S:(k + 1) * S], ACT.Identity,
                                               bias=inb[:, k:k + 1], scale=inw[:, k:k + 1])
                taken(ins, XT)
                act.wait_ge(proj_taken[XT % 2].sem, proj_taken[XT % 2].at(b, XT // 2 + 1))
                nc.scalar.copy(xn_hi[:], xn_t[:]).then_inc(xn_hi_ready.sem, 1)

            def take_y(b):
                filled(b, YP)
                taken(nc.scalar.activation(gate_tanh[:], proj[YP % 2][0:HEADS, 0:S], ACT.Tanh, bias=half_by[:, 0:1], scale=0.5), YP)

            def take_q(b, n):
                f = QP + n
                if n == 0:
                    act.wait_ge(q_split.sem, q_split.at(b - 1, 2))
                    for g in range(HPC):
                        act.wait_ge(parts_loaded[g].sem, parts_loaded[g].at(b - 1, parts_loaded[g].per))
                filled(b, f)
                for dst in (q_t, q_hi):
                    for i in range(2):
                        m = 2 * n + i
                        ins = nc.scalar.activation(dst[:, m, :], proj[f % 2][:, i * S:(i + 1) * S], ACT.Identity,
                                                   bias=q_bias[:, m:m + 1], scale=q_scale[:, m:m + 1])
                taken(ins, f)

            def smear_k(b, n):
                f = KP + n
                filled(b, f)
                for i in range(2):
                    m = 2 * n + i
                    ins = nc.scalar.activation(k_prev[:, m, 1:S + 1], proj[f % 2][:, i * S:(i + 1) * S], ACT.Identity,
                                               bias=bk[:, m:m + 1], scale=smear[:, m:m + 1])
                ins.then_inc(k_prev_ready.sem, 1)

            def high_k(b, n):
                f = KP + n
                act.wait_ge(proj_taken[f % 2].sem, proj_taken[f % 2].at(b, f // 2 + 1))
                nc.scalar.copy(k_hi[:, 2 * n:2 * n + 2, :], k_t[:, 2 * n:2 * n + 2, :]).then_inc(k_hi_ready.sem, 1)

            def tanh_p(b, n):
                f = PP + n
                act.wait_ge(p_half_ready.sem, p_half_ready.at(b, n + 1))
                act.wait_ge(silu_ready.sem, silu_ready.at(b, 1))
                for i in range(2):
                    m = 2 * n + i
                    ins = nc.scalar.activation(p_tanh[:, m, :], proj[f % 2][:, i * S:(i + 1) * S], ACT.Tanh,
                                               bias=half_bp[:, m:m + 1], scale=0.5)
                taken(ins, f)

            def take_v(b):
                act.wait_ge(av_done.sem, av_done.at(b - 1, HEADS))
                for f in (VP, VP + 1):
                    filled(b - 1, f)
                    taken(nc.scalar.copy(v_a[:, f - VP, :], proj[f % 2][:, :]), f)

            def take_output(c):
                def part(b):
                    filled(b, WO + c)
                    act.wait_ge(out_used.sem, out_used.at(b - 1, 1))
                    taken(nc.scalar.copy(out_s[:, c, :], proj[(WO + c) % 2][:, 0:D]), WO + c)
                return part

            def projections(b):
                take_xt(b)
                take_y(b)
                for n in range(2):
                    take_q(b, n)
                for n in range(2):
                    smear_k(b, n)
                    high_k(b, n)
                for n in range(2):
                    tanh_p(b, n)

            for s in (exp_ready, *pt_taken):
                act.sem_inc(s.sem, s.per)
            projections(-1)
            steps = {0: [take_v], 1: [take_xt], 2: [take_y], 3: [lambda b: take_q(b, 0)], 4: [lambda b: take_q(b, 1)],
                     5: [take_output(0)], 6: [take_output(1)], 7: [lambda b: smear_k(b, 0)], 9: [lambda b: smear_k(b, 1), lambda b: high_k(b, 0)],
                     11: [lambda b: high_k(b, 1)], 12: [lambda b: tanh_p(b, 0)],
                     14: [lambda b: tanh_p(b, 1)]}
            with act.Fori(0, B) as b:
                for i in range(HEADS + 3):
                    if i < HEADS:
                        exps(b, i)
                    if i >= 3:
                        take_transposed(b, i - 3)
                    for part in steps.get(i, ()):
                        part(b)
            take_v(B)
            for c in range(TC):
                take_output(c)(B)

        @block.vector
        def _(dve):
            def apart(signal, value):
                dve.wait_ge(signal.sem, value)
                dve.sem_inc(passed["dve"], 1)

            def filled(b, f):
                dve.wait_ge(proj_filled.sem, proj_filled.at(b, f + 1))

            def taken(ins, f):
                ins.then_inc(proj_taken[f % 2].sem, 1)

            dve.memset(silu_p[:], 0.0)
            dve.memset(one_keep[:], 1.0).then_inc(consts_v, 1)
            dve.wait_ge(consts, N_CONSTS)
            for g in range(HPC):
                ins = dve.tensor_copy(q_parts[3 * DH_A:P, g, :, :],
                                      own_rows[3 * DH_A:P, g, :].unsqueeze(2).broadcast_to([P - 3 * DH_A, EC, S]))
            ins.then_inc(consts_v, 1)
            dve.wait_ge(consts_a, 2)
            dve.wait_ge(in_weights, N_IN)
            dve.tensor_scalar(unsmear[:], smear[:], -0.5, 0.5, ALU.mult, ALU.add).then_inc(consts_v, 1)
            dve.tensor_scalar(q_scale[:], q_scale[:], 1.0 / float(np.sqrt(DH_A)), None, ALU.mult).then_inc(consts_v, 1)
            dve.tensor_scalar(half_bp[:], bp, 0.5, None, ALU.mult)
            dve.tensor_scalar(half_by[:], by[:], 0.5, None, ALU.mult).then_inc(consts_v, 1)
            dve.wait_ge(consts_v, 5)
            dve.tensor_scalar(smear[:], smear[:], 0.5, 0.5, ALU.mult, ALU.add)
            dve.tensor_tensor(q_bias[:], bq, q_scale[:], ALU.mult)
            dve.tensor_tensor(k_prev[:, :, 0], unsmear[:], bk, ALU.mult).then_inc(consts_v, 1)
            for k in range(KC):
                dve.wait_ge(consts_a, 2 + k + 1)
                dve.tensor_tensor(win_lo[:, k, :], win_s[:, k, :], win_hi[:, k, :].bitcast(F32), ALU.subtract).then_inc(consts_v, 1)
            for s in (half_stats, stats_ready):
                for ln in (LN_OUT, LN_RES):
                    dve.sem_inc(s[ln].sem, 1)
            for s in (residual_ready, x1_ready, x1_stored, out_used, score_taken, rden_ready, prob_ready):
                dve.sem_inc(s.sem, s.per)

            def stats(b, ln, sources):
                for c in range(TC):
                    ins = dve.bn_stats(stat[:, ln, c, :], sources[c])
                ins.then_inc(half_stats[ln].sem, 1)
                apart(half_stats[ln], half_stats[ln].at(b, NTH[ln]))
                for c in range(TC):
                    ins = dve.bn_aggr(mv[:, ln, c, :], stat[:, ln, c, :])
                ins.then_inc(stats_ready[ln].sem, 1)

            def normalise(ln, out, src, c):
                return dve.tensor_scalar(out, src, mv[:, ln, c, 0:1], rstd[:, ln, c:c + 1], ALU.subtract, ALU.mult)

            def x_stats(b):
                dve.wait_ge(x_loaded.sem, x_loaded.at(b, 16))
                stats(b, LN_X, [x_raw[:, c, :] for c in range(TC)])

            def x_normalised(b):
                dve.wait_ge(rstd_ready[LN_X].sem, rstd_ready[LN_X].at(b, NTH[LN_X]))
                for c in range(TC):
                    ins = normalise(LN_X, zx[:, c, :], x_raw[:, c, :], c)
                ins.then_inc(zx_ready.sem, 1)

            def low_x(b):
                dve.wait_ge(xn_hi_ready.sem, xn_hi_ready.at(b, 1))
                dve.tensor_tensor(xn_lo[:], xn_t[:], xn_hi[:].bitcast(F32), ALU.subtract).then_inc(xn_split.sem, 1)

            def forget_gates(b):
                dve.wait_ge(proj_taken[YP % 2].sem, proj_taken[YP % 2].at(b, YP // 2 + 1))
                dve.tensor_scalar(gate_sig[:], gate_tanh[:], 0.5, 0.5, ALU.mult, ALU.add).then_inc(pos_steps.sem, 1)
                dve.wait_ge(pos_steps.sem, pos_steps.at(b, 1))
                dve.tensor_tensor_scan(pos[:], one_keep[:], gate_sig[:], 0.0, ALU.mult, ALU.add).then_inc(pos_steps.sem, 1)
                dve.wait_ge(pos_steps.sem, pos_steps.at(b, 2))
                for g in range(HPC):
                    dve.wait_ge(parts_loaded[g].sem, parts_loaded[g].at(b - 1, parts_loaded[g].per))
                dve.tensor_copy(pos_parts[0:HEADS, :], pos[:]).then_inc(pos_steps.sem, 1)
                dve.wait_ge(pos_steps.sem, pos_steps.at(b, 3))
                dve.tensor_tensor(pos_parts[32:32 + HEADS, :], pos[:], pos_parts[0:HEADS, :].bitcast(F32),
                                  ALU.subtract).then_inc(pos_steps.sem, 1)

            def take_k(b, n):
                f = KP + n
                if n == 0:
                    dve.wait_ge(k_split.sem, k_split.at(b - 1, 2))
                dve.wait_ge(k_prev_ready.sem, k_prev_ready.at(b, n + 1))
                for i in range(2):
                    m = 2 * n + i
                    ins = dve.scalar_tensor_tensor(out=k_t[:, m, :], in0=proj[f % 2][:, i * S:(i + 1) * S],
                                                   scalar=unsmear[:, m:m + 1], in1=k_prev[:, m, 0:S],
                                                   op0=ALU.mult, op1=ALU.add)
                taken(ins, f)

            def half_p(b, n):
                f = PP + n
                filled(b, f)
                for i in range(2):
                    m = 2 * n + i
                    ins = dve.tensor_scalar(p_half[:, m, :], proj[f % 2][:, i * S:(i + 1) * S],
                                            bp[:, m:m + 1], 0.5, ALU.add, ALU.mult)
                ins.then_inc(p_half_ready.sem, 1)

            def gate(b):
                dve.wait_ge(av_done.sem, av_done.at(b - 1, HEADS))
                for m in range(EC):
                    ins = dve.scalar_tensor_tensor(out=gated_t[:, m, :], in0=av[m // 2][:, (m % 2) * S:(m % 2 + 1) * S],
                                                   scalar=bv[:, m:m + 1], in1=silu_p[:, m, :], op0=ALU.add, op1=ALU.mult)
                    if m % 2 == 1:
                        ins.then_inc(gated.sem, 1)

            def silu(b):
                dve.wait_ge(gated.sem, gated.at(b, 2))
                f = PP + 1
                dve.wait_ge(proj_taken[f % 2].sem, proj_taken[f % 2].at(b - 1, f // 2 + 1))
                dve.scalar_tensor_tensor(out=silu_p[:], in0=p_tanh[:], scalar=1.0, in1=p_half[:],
                                         op0=ALU.add, op1=ALU.mult).then_inc(silu_ready.sem, 1)

            def masked_scores(b, u):
                apart(pt_filled, pt_filled.at(b, u - PROB_RING + 1))
                apart(score_filled, score_filled.at(b, u + 1))
                slot, bank = prob[:, u % PROB_RING, :], score[u % 2]
                dve.tensor_tensor_reduce(slot[:, 0:P], bank[:, 0:P], causal[:, P:S], -1.0, 3.0e38,
                                         ALU.add, ALU.min, low[:, u, 0:1])
                dve.tensor_tensor_reduce(slot[:, P:P + S], bank[:, S:2 * S], causal[:, :], -1.0, 3.0e38,
                                         ALU.add, ALU.min, low[:, u, 1:2]).then_inc(score_taken.sem, 1)

            def one_over_sum(b, u):
                dve.wait_ge(exp_ready.sem, exp_ready.at(b, u + 1))
                dve.reciprocal(rden[:, u, :], den[:, u, :]).then_inc(rden_ready.sem, 1)

            def probabilities(b, u):
                dve.wait_ge(rden_ready.sem, rden_ready.at(b, u + 1))
                slot = prob[:, u % PROB_RING, :]
                for c in range(TC):
                    s = slot[:, 0:P] if c == 0 else slot[:, P:P + S]
                    ins = dve.tensor_scalar(s, s, rden[:, u, c:c + 1], None, ALU.mult)
                ins.then_inc(prob_ready.sem, 1)

            def out_stats(b):
                f = WO + 1
                dve.wait_ge(proj_taken[f % 2].sem, proj_taken[f % 2].at(b, f // 2 + 1))
                stats(b, LN_OUT, [out_s[:, c, :] for c in range(TC)])

            def residual_sum(b):
                dve.wait_ge(rstd_ready[LN_OUT].sem, rstd_ready[LN_OUT].at(b, NTH[LN_OUT]))
                for c in range(TC):
                    ins = dve.scalar_tensor_tensor(out=centred[:, c, :], in0=out_s[:, c, :],
                                                   scalar=mv[:, LN_OUT, c, 0:1], in1=onw,
                                                   op0=ALU.subtract, op1=ALU.mult)
                ins.then_inc(out_used.sem, 1)
                dve.wait_ge(x_res_ready.sem, x_res_ready.at(b, 1))
                dve.wait_ge(out_used.sem, out_used.at(b, 1))
                for c in range(TC):
                    ins = dve.scalar_tensor_tensor(out=res1[:, c, :], in0=centred[:, c, :], scalar=rstd[:, LN_OUT, c:c + 1],
                                                   in1=x_res[:, c, :], op0=ALU.mult, op1=ALU.add)
                ins.then_inc(residual_ready.sem, 1)

            def residual_stats(b):
                dve.wait_ge(residual_ready.sem, residual_ready.at(b, 1))
                stats(b, LN_RES, [res1[:, c, :] for c in range(TC)])

            def x1_of(b):
                dve.wait_ge(x1_stored.sem, x1_stored.at(b, 0))
                dve.wait_ge(rstd_ready[LN_RES].sem, rstd_ready[LN_RES].at(b, NTH[LN_RES]))
                for c in range(TC):
                    ins = normalise(LN_RES, x1[:, c, :], res1[:, c, :], c)
                ins.then_inc(x1_ready.sem, 1)

            x_stats(-1)
            x_normalised(-1)
            low_x(-1)
            forget_gates(-1)
            for n in range(2):
                take_k(-1, n)
            for n in range(2):
                half_p(-1, n)
            x_stats(0)
            x_normalised(0)
            steps = {1: [gate], 2: [low_x, silu], 3: [forget_gates], 7: [out_stats], 8: [residual_sum, lambda b: take_k(b, 0)], 9: [residual_stats],
                     10: [lambda b: take_k(b, 1)], 11: [lambda b: half_p(b, 0)], 12: [x1_of], 13: [lambda b: half_p(b, 1)],
                     14: [lambda b: x_stats(b + 1)], 16: [lambda b: x_normalised(b + 1)]}
            with dve.Fori(0, B) as b:
                for i in range(HEADS + 2):
                    if i < HEADS:
                        masked_scores(b, i)
                    if 1 <= i <= HEADS:
                        one_over_sum(b, i - 1)
                    if i >= 2:
                        probabilities(b, i - 2)
                    for part in steps.get(i, ()):
                        part(b)
            gate(B)
            for part in (out_stats, residual_sum, residual_stats, x1_of):
                part(B)

        @block.tensor
        def _(pe):
            pe.wait_ge(consts, N_CONSTS)
            pe.wait_ge(in_weights, N_IN)
            for s, n in ((score_filled, HEADS), (pt_filled, HEADS),
                         (av_done, HEADS - 1)):
                pe.sem_inc(s.sem, n)
            matmul, transpose = nc.tensor.matmul, nc.tensor.transpose

            def free(b, f):
                pe.wait_ge(proj_taken[f % 2].sem, proj_taken[f % 2].at(b, f // 2))
                return proj[f % 2]

            def in_sbuf(b, f):
                pe.wait_ge(proj_taken[f % 2].sem, proj_taken[f % 2].at(b, f // 2 + 1))

            def full(ins):
                ins.then_inc(proj_filled.sem, 1)

            def project(out, lhs, rhs, chunks):
                for k in range(chunks):
                    ins = matmul(out, lhs(k), rhs(k), start=(k == 0), stop=(k == chunks - 1))
                return ins

            win_parts, xn_parts = (win_hi, win_lo), (xn_hi, xn_lo)

            def project_parts(out, lhs, rhs):
                for k in range(KC):
                    for i, j in ((0, 0), (0, 1), (1, 0)):
                        ins = matmul(out, lhs(i, k), rhs(j, k), start=(k == 0 and i + j == 0), stop=(k == KC - 1 and i == 1))
                return ins

            def x_transposed(b):
                bk_ = free(b, XT)
                pe.wait_ge(zx_ready.sem, zx_ready.at(b, 1))
                for k in range(KC):
                    for c in range(TC):
                        ins = transpose(bk_[:, k * S + c * P:k * S + (c + 1) * P], zx[:, c, k * P:(k + 1) * P], ident[:])
                full(ins)

            def project_y(b):
                bk_ = free(b, YP)
                in_sbuf(b, XT)
                full(project(bk_[0:HEADS, 0:S], lambda k: win_y[:, k, :], lambda k: xn_t[:, k, :], KC))

            def chunk(b, f, i, col0):
                bk_ = free(b, f) if i == 0 else proj[f % 2]
                if f == QP and i == 0:
                    pe.wait_ge(xn_split.sem, xn_split.at(b, 1))
                ins = project_parts(bk_[:, i * S:(i + 1) * S], lambda a, k: win_parts[a][:, k, col0:col0 + P],
                                    lambda a, k: xn_parts[a][:, k, :])
                if i == 1:
                    full(ins)

            def chunks_of(f0, col0):
                return [lambda b, m=m: chunk(b, f0 + m // 2, m % 2, col0 + m * P) for m in range(EC)]

            def project_v(b, c):
                bk_ = free(b, VP + c)
                full(project_parts(bk_[:, :], lambda a, k: xn_parts[a][:, k, c * P:(c + 1) * P],
                                   lambda a, k: win_parts[a][:, k, 2 * D_EXP:3 * D_EXP]))

            def scores(b, u):
                g, m = divmod(u, EC)
                pe.wait_ge(score_taken.sem, score_taken.at(b, u - 1))
                if m == 0:
                    pe.wait_ge(parts_loaded[g].sem, parts_loaded[g].at(b - 1, parts_loaded[g].per))
                for c in range(TC):
                    ins = matmul(score[u % 2][:, c * S:(c + 1) * S], q_parts[:, g, m, c * P:(c + 1) * P], k_parts[:, g, m, :],
                                 start=True, stop=True)
                ins.then_inc(score_filled.sem, 1)

            def transposes(b, u):
                pe.wait_ge(pt_taken[u % 2].sem, pt_taken[u % 2].at(b, u // 2))
                pe.wait_ge(prob_ready.sem, prob_ready.at(b, u + 1))
                for i in range(3):
                    ins = transpose(ptb[u % 2][:, i * P:(i + 1) * P], prob[:, u % PROB_RING, i * P:(i + 1) * P], ident[:])
                ins.then_inc(pt_filled.sem, 1)

            def values(b, u):
                g, m = divmod(u, EC)
                h = HPC * m + g
                if u == 0:
                    in_sbuf(b - 1, VP)
                    in_sbuf(b - 1, VP + 1)
                if u in (0, 2):
                    pe.wait_ge(gated.sem, gated.at(b, u // 2 + 1))
                pe.wait_ge(pt_taken[u % 2].sem, pt_taken[u % 2].at(b, u // 2 + 1))
                o = av[m // 2][DH_A * g:DH_A * (g + 1), (m % 2) * S:(m % 2 + 1) * S]
                dims = slice(DH_A * h, DH_A * (h + 1))
                matmul(o, v_a[:, 0, dims], pt[:, u % PT_RING, 0:S], start=True, stop=False)
                matmul(o[:, P:S], v_a[:, 1, dims], pt[:, u % PT_RING, S:S + P], start=False, stop=True).then_inc(av_done.sem, 1)

            def output(c):
                def part(b):
                    pe.wait_ge(gated.sem, gated.at(b, 2))
                    bk_ = free(b, WO + c)
                    full(project(bk_[:, 0:D], lambda k: gated_t[:, k, c * P:(c + 1) * P], lambda k: wo[:, k, :], EC))
                return part

            for j in range(2):
                ins = matmul(av[j][:, :], zeros[:, 0:P], zeros[:, :], start=True, stop=True)
            ins.then_inc(av_done.sem, 1)
            pe.wait_ge(consts_v, N_VCONSTS)
            outputs = [output(c) for c in range(TC)]
            inputs = [x_transposed, project_y, *chunks_of(QP, 0), *chunks_of(KP, D_EXP), *chunks_of(PP, 3 * D_EXP),
                      lambda b: project_v(b, 0), lambda b: project_v(b, 1)]

            def skip(b, f):
                free(b, f)
                in_sbuf(b, f - 1) if f > 0 else in_sbuf(b - 1, FILLS - 1)
                pe.sem_inc(proj_taken[f % 2].sem, 1)
                pe.sem_inc(proj_filled.sem, 1)

            n_first = 2 + EC
            for part in inputs[:n_first]:
                part(-1)
            for c in range(TC):
                skip(-1, WO + c)
            for part in inputs[n_first:]:
                part(-1)
            before_ = {2: inputs[1], 3: inputs[3], 4: inputs[5]}
            before_.update({6 + n: part for n, part in enumerate(inputs[n_first:])})
            after_ = {0: inputs[0], 2: inputs[2], 3: inputs[4], 4: outputs[0], 5: outputs[1]}
            scores(0, 0)
            with pe.Fori(0, B) as b:
                for i in range(HEADS + 4):
                    if i in before_:
                        before_[i](b)
                    if 3 <= i < HEADS + 3:
                        transposes(b, i - 3)
                    if i + 1 < HEADS:
                        scores(b, i + 1)
                    elif i == HEADS + 2:
                        scores(b + 1, 0)
                    if i >= 4:
                        values(b, i - 4)
                    if i in after_:
                        after_[i](b)
            for f in range(WO):
                skip(B, f)
            for part in outputs:
                part(B)


def cross_phase(nc, sem, sig, ctx_in, mask, x1_dram, x2_dram, list_dram, ident, vx, pt, wq_s, wkv_s, wox, wr_s, col, row,
                gates, slots, counts):
    FILLS = 26
    V1 = (0, 1, 3, 4)
    WOX, CT, LT, X2T, LOGITS, PREFIX = 2, 5, 6, 7, 9, 12
    KQ = (8, 10, 11, 13, 14, 15, 16, 17, 19, 20, 22, 23)
    V0 = (18, 21, 24, 25)
    WHOLES = 4
    LNS = LN_LAT, LN_CTX, LN_X2 = range(3)
    UNITS = 2 * HEADS
    PROB_RING = 6
    QUADS = HEADS // 4
    with ExitStack() as stack:
        def sb(name, shape, dt=F32):
            return stack.enter_context(nc.sbuf_tensor("x_" + name, shape, dt))

        def bank(name):
            return stack.enter_context(nc.psum_tensor("x_" + name, [P, 512], F32))

        def signal(name, per, start=None):
            return sig("x_" + name, per, start)

        g1, be1, g2, be2 = (col[:, a:z] for a, z in ((16, 18), (18, 20), (20, 22), (22, 24)))
        br_row = row[:, 2 * D:2 * D + E]
        before = sb("before", [P, P])
        ones = sb("ones", [P, P])
        minus_half = sb("minus_half", [P, TC])
        expert_no = sb("expert_no", [P, E])
        expert_i = sb("expert_i", [P, E], I32)
        expert_base = sb("expert_base", [P, E])
        down = sb("down", [P, E])
        ctx_raw = sb("ctx_raw", [P, TC, D])
        x1_raw = sb("x1_raw", [P, TC, D])
        mask_raw = sb("mask_raw", [P, S // 4], I32)
        mask_add = sb("mask_add", [P, N_KEYS])
        zctx = sb("zctx", [P, TC, D])
        zlat = sb("zlat", [P, TC, D])
        keys_hi = sb("keys_hi", [P, KC, N_KEYS], F32R)
        keys_lo = sb("keys_lo", [P, KC, N_KEYS], F32R)
        keys_t = [z[:].rearrange("p c d -> p (c d)").rearrange("p (k s) -> p k s", k=KC) for z in (zctx, zlat)]
        wkv_hi = sb("wkv_hi", [P, KC, 2 * INNER], F32R)
        wkv_lo = sb("wkv_lo", [P, KC, 2 * INNER], F32R)
        wq_hi = sb("wq_hi", [P, KC, INNER], F32R)
        wq_lo = sb("wq_lo", [P, KC, INNER], F32R)
        q_parts = sb("q_parts", [P, HEADS, S], F32R)
        q_lo = sb("q_lo", [P, 2, 2, S], F32R)
        whole = sb("whole", [P, WHOLES, 2 * S])
        k_twice = sb("k_twice", [P, HEADS, N_KEYS], F32R)
        k_lo = sb("k_lo", [P, XC, N_KEYS], F32R)
        prob = sb("prob", [P, PROB_RING, N_KEYS])
        low = sb("low", [P, UNITS])
        den = sb("den", [P, UNITS])
        rden = sb("rden", [P, UNITS])
        ox_t = sb("ox_t", [P, XC, S])
        x1_again = sb("x1_again", [P, TC, D])
        x2 = sb("x2", [P, TC, D])
        x2_t = sb("x2_t", [P, KC, S])
        stat = sb("stat", [P, len(LNS), TC, 6])
        mv = sb("mv", [P, len(LNS), TC, 2])
        var_eps = sb("var_eps", [P, len(LNS), TC])
        rstd = sb("rstd", [P, len(LNS), TC])
        logit = sb("logit", [P, TC, E])
        others = sb("others", [P, TC, E])
        best = sb("best", [P, TC, TOP])
        is_best = sb("is_best", [P, TC, E])
        rank = sb("rank", [P, TC, E])
        best_rank = sb("best_rank", [P, TC])
        margin = sb("margin", [P, TC])
        margin_tanh = sb("margin_tanh", [P, TC])
        chosen = sb("chosen", [P, TC, TOP, E])
        either = sb("either", [P, TC, E])
        place = sb("place", [P, TC, E])
        own_place = sb("own_place", [P, TC, TOP, E])
        slot_f = sb("slot_f", [P, TC, TOP])
        slot_i = sb("slot_i", [P, TC * TOP], I32)
        next_free = sb("next_free", [P, E])
        real = sb("real", [P, 1])
        junk_off = sb("junk_off", [P, 1])
        token_f = sb("token_f", [P, TC])
        token_i = sb("token_i", [P, TC], I32)
        proj = [bank(f"proj{i}") for i in range(2)]
        score = [bank(f"score{i}") for i in range(2)]
        ptb = [bank(f"ptb{i}") for i in range(2)]
        av = [bank(f"av{i}") for i in range(2)]

        consts, consts_v = sem("x_consts"), sem("x_consts_v")
        passed = {e: sem(f"x_passed_{e}") for e in ("pool", "dve", "sp")}
        x1_loaded, ctx_loaded, mask_loaded = signal("x1_loaded", 16), signal("ctx_loaded", 16), signal("mask_loaded", 16)
        again_loaded, x2_stored = signal("again_loaded", 16, 0), signal("x2_stored", 16)
        spread = [signal(f"spread{f}", 16 * 6) for f in range(QUADS)]
        scattered, scatter_over = signal("scattered", 16 * TC * TOP, 0), signal("scatter_over", 1)
        mask_ready = signal("mask_ready", 1)
        residual_ready = signal("residual_ready", 1)

        NTH = (1, 2, 1)

        def norm_signals(name):
            apart_ = [signal(f"{name}{n}", max(k for k, g in zip(NTH, (0, 0, 1)) if g == n)) for n in range(2)]
            return [apart_[g] for g in (0, 0, 1)]

        half_stats, stats_ready, var_ready, rstd_ready = (
            norm_signals(name) for name in ("half_stats", "stats_ready", "var_ready", "rstd_ready"))
        zlat_ready, zctx_ready, x2_ready = signal("zlat_ready", 1), signal("zctx_ready", 1), signal("x2_ready", 1)
        proj_filled = signal("proj_filled", FILLS)
        proj_taken = [signal(f"proj_taken{i}", FILLS // 2) for i in range(2)]
        keys_hi_ready, keys_split = signal("keys_hi_ready", 2), signal("keys_split", 2)
        weights_hi, weights_split = sem("x_weights_hi"), sem("x_weights_split")
        high_ready, low_ready = signal("high_ready", 3 * QUADS), signal("low_ready", 6 * QUADS)
        score_filled, score_taken = signal("score_filled", UNITS), signal("score_taken", UNITS)
        exp_ready, prob_ready = signal("exp_ready", UNITS), signal("prob_ready", HEADS)
        rden_ready = signal("rden_ready", HEADS)
        pt_filled = signal("pt_filled", UNITS)
        pt_taken = [signal(f"pt_taken{i}", HEADS) for i in range(2)]
        av_done = signal("av_done", UNITS)
        av_taken = [signal(f"av_taken{i}", XC // 2) for i in range(2)]
        route_steps, margin_steps = signal("route_steps", 14), signal("margin_steps", 1)
        margin_ready, margin_tanh_ready = signal("margin_ready", 1), signal("margin_tanh_ready", 1)
        either_ready, slot_ready = signal("either_ready", 1), signal("slot_ready", 1)
        token_steps = signal("token_steps", 2)
        counts_ready = sem("counts_ready")
        N_CONSTS, N_VCONSTS = 9, 3

        weights = [(wkv_hi[:, k, :], wkv_s[:, k, :]) for k in range(KC)] + [(wq_hi[:], wq_s)]
        weights_lo = [wkv_lo[:, k, :] for k in range(KC)] + [wq_lo[:]]

        def halves(f):
            return [(slice(DH_X * o, DH_X * (o + 1)), slice(4 * f + o, 4 * f + 4, 2)) for o in range(2)]

        def whole_of(n, rows):
            return whole[rows, n % WHOLES, :].rearrange("p (i s) -> p i s", i=2)

        def high_of(rows, heads, kind):
            return q_parts[rows, heads, :] if kind == 2 else k_twice[rows, heads, kind * S:(kind + 1) * S]

        block = stack.enter_context(nc.Block())

        @block.sync
        def _(sp):
            x1_rows, x2_rows = (a.rearrange("(b c p) d -> b p c d", c=TC, p=P) for a in (x1_dram, x2_dram))

            def pass_wait(s, value):
                sp.wait_ge(s.sem, value)
                sp.sem_inc(passed["sp"], 1)

            def context_of(nb):
                return ctx_in[nb].rearrange("(c p) d -> p c d", p=P)

            def spread_heads(b):
                for f in range(QUADS):
                    (lo_rows, even), (hi_rows, odd) = halves(f)
                    for n in range(2):
                        keys = slice(n * S, (n + 1) * S)
                        sp.wait_ge(high_ready.sem, high_ready.at(b, 3 * f + n + 1))
                        for dst, src, heads in ((hi_rows, lo_rows, even), (lo_rows, hi_rows, odd)):
                            sp.dma_start(k_twice[dst, heads, keys].bitcast(F32),
                                         k_twice[src, heads, keys].bitcast(F32)).then_inc(spread[f].sem, 16)
                    sp.wait_ge(low_ready.sem, low_ready.at(b, 6 * f + 6))
                    for dst, src, heads in ((hi_rows, lo_rows, even), (lo_rows, hi_rows, odd)):
                        sp.dma_start(q_parts[dst, heads, :].bitcast(F32),
                                     q_lo[src, f % 2, :, :].bitcast(F32)).then_inc(spread[f].sem, 16)

            sp.dma_start(x1_raw[:], x1_rows[1]).then_inc(x1_loaded.sem, 16)
            sp.dma_start(ctx_raw[:], context_of(0)).then_inc(ctx_loaded.sem, 16)
            sp.dma_start(mask_raw[:], mask[0].broadcast_to([P, S // 4])).then_inc(mask_loaded.sem, 16)
            sp.dma_start(x1_again[:], x1_rows[0]).then_inc(again_loaded.sem, 16)
            sp.wait_ge(zlat_ready.sem, zlat_ready.at(-1, 1))
            sp.dma_start(x1_raw[:], x1_rows[2]).then_inc(x1_loaded.sem, 16)
            sp.wait_ge(zctx_ready.sem, zctx_ready.at(-1, 1))
            sp.dma_start(ctx_raw[:], context_of(1)).then_inc(ctx_loaded.sem, 16)
            spread_heads(-1)
            with sp.Fori(0, B) as b:
                pass_wait(mask_ready, mask_ready.at(b - 1, 1))
                sp.dma_start(mask_raw[:], mask[(b + 1) % B].broadcast_to([P, S // 4])).then_inc(mask_loaded.sem, 16)
                pass_wait(zlat_ready, zlat_ready.at(b, 1))
                sp.dma_start(x1_raw[:], x1_rows[(b + 3) % (B + 1)]).then_inc(x1_loaded.sem, 16)
                pass_wait(zctx_ready, zctx_ready.at(b, 1))
                sp.dma_start(ctx_raw[:], context_of((b + 2) % B)).then_inc(ctx_loaded.sem, 16)
                pass_wait(x2_ready, x2_ready.at(b, 1))
                sp.dma_start(x1_again[:], x1_rows[b + 1]).then_inc(again_loaded.sem, 16)
                sp.dma_start(x2_rows[b], x2[:]).then_inc(x2_stored.sem, 16)
                spread_heads(b)
            sp.wait_ge(x2_ready.sem, x2_ready.at(B, 1))
            sp.dma_start(x2_rows[B], x2[:]).then_inc(x2_stored.sem, 16)
            sp.wait_ge(x2_stored.sem, x2_stored.at(B, 16))
            sp.wait_ge(mask_loaded.sem, mask_loaded.at(B - 1, 16))
            sp.wait_ge(x1_loaded.sem, x1_loaded.at(B, 16))
            sp.wait_ge(ctx_loaded.sem, ctx_loaded.at(B, 16))
            for f in range(QUADS):
                sp.wait_ge(spread[f].sem, spread[f].at(B - 1, spread[f].per))

        @block.gpsimd
        def _(pool):
            pool.memset(ones[:], 1.0).then_inc(consts, 1)
            pool.memset(minus_half[:], -0.5).then_inc(consts, 1)
            pool.memset(mask_add[:], 0.0).then_inc(consts, 1)
            pool.memset(ox_t[:], 0.0).then_inc(consts, 1)
            pool.iota(expert_i[:], pattern=[[1, E]], base=0, channel_multiplier=0).then_inc(consts, 1)
            pool.iota(token_i[:], pattern=[[P, TC]], base=-S, channel_multiplier=1).then_inc(consts, 1)
            pool.wait_ge(consts, 6)
            pool.affine_select(out=before[:], in_=ones[:], compare_op=ALU.is_ge, fill=0.0, base=-1,
                               pattern=[[1, P]], channel_multiplier=-1).then_inc(consts, 1)
            pool.tensor_copy(token_f[:], token_i[:]).then_inc(consts, 1)
            pool.tensor_copy(expert_no[:], expert_i[:]).then_inc(consts, 1)
            pool.wait_ge(consts, N_CONSTS)

            def reciprocal_root(b, ln):
                pool.wait_ge(stats_ready[ln].sem, stats_ready[ln].at(b, NTH[ln]))
                pool.sem_inc(passed["pool"], 1)
                pool.tensor_scalar(var_eps[:, ln, :], mv[:, ln, :, 1], EPS, None, ALU.add).then_inc(var_ready[ln].sem, 1)
                pool.wait_ge(var_ready[ln].sem, var_ready[ln].at(b, NTH[ln]))
                pool.tensor_tensor(rstd[:, ln, :], var_eps[:, ln, :], minus_half[:], ALU.pow).then_inc(rstd_ready[ln].sem, 1)

            def low_keys(b):
                for n in range(2):
                    keys = slice(n * S, (n + 1) * S)
                    pool.wait_ge(keys_hi_ready.sem, keys_hi_ready.at(b, n + 1))
                    pool.tensor_tensor(keys_lo[:, :, keys], keys_t[n], keys_hi[:, :, keys].bitcast(F32),
                                       ALU.subtract).then_inc(keys_split.sem, 1)

            def lows_over(b, n):
                if not (isinstance(b, int) and b < 0 and n == 0):
                    pool.wait_ge(low_ready.sem, low_ready.at(b, n))
                    pool.sem_inc(passed["pool"], 1)

            def low_part(b, n):
                f, kind = n // 3, n % 3
                if kind == 2:
                    pool.wait_ge(spread[(f + 2) % QUADS].sem, spread[(f + 2) % QUADS].at(b - (f < 2), spread[f].per))
                pool.wait_ge(high_ready.sem, high_ready.at(b, n + 1))
                for o, (rows, heads) in enumerate(halves(f)):
                    lows_over(b, 2 * n + o)
                    low = q_lo[rows, f % 2, :, :] if kind == 2 else k_lo[rows, 2 * f:2 * f + 2, kind * S:(kind + 1) * S]
                    pool.tensor_tensor(low, whole_of(n, rows), high_of(rows, heads, kind).bitcast(F32), ALU.subtract).then_inc(low_ready.sem, 1)

            def scatter(b):
                pool.tensor_scalar(token_f[:], token_f[:], float(S), None, ALU.add).then_inc(token_steps.sem, 1)
                pool.wait_ge(token_steps.sem, token_steps.at(b, 1))
                pool.sem_inc(passed["pool"], 1)
                pool.tensor_copy(token_i[:], token_f[:]).then_inc(token_steps.sem, 1)
                pool.wait_ge(token_steps.sem, token_steps.at(b, 2))
                pool.wait_ge(slot_ready.sem, slot_ready.at(b, 1))
                pool.sem_inc(passed["pool"], 1)
                for c in range(TC):
                    for j in range(TOP):
                        n = c * TOP + j
                        pool.indirect_dma_start(
                            list_dram, bass.IndirectOffsetOnAxis(ap=slot_i[:, n:n + 1].bitcast(U32), axis=0),
                            token_i[:, c:c + 1], None).then_inc(scattered.sem, 16)
                pool.wait_ge(scattered.sem, scattered.at(b, scattered.per))
                pool.sem_inc(scatter_over.sem, 1)

            for s in (scatter_over, token_steps):
                pool.sem_inc(s.sem, s.per)
            for s in (var_ready, rstd_ready):
                pool.sem_inc(s[LN_X2].sem, 1)
            for ln in (LN_LAT, LN_CTX):
                reciprocal_root(-1, ln)
            low_keys(-1)
            pool.wait_ge(keys_split.sem, keys_split.at(-1, 2))
            for n in range(3 * QUADS):
                low_part(-1, n)
            with pool.Fori(0, B) as b:
                lows_over(b, 0)
                for ln in LNS:
                    reciprocal_root(b, ln)
                low_keys(b)
                pool.wait_ge(keys_split.sem, keys_split.at(b, 2))
                for n in range(2):
                    low_part(b, n)
                lows_over(b, 4)
                scatter(b)
                for n in range(2, 3 * QUADS):
                    low_part(b, n)
            lows_over(B, 0)
            reciprocal_root(B, LN_X2)
            scatter(B)

        @block.scalar
        def _(act):
            def taken(ins, f):
                ins.then_inc(proj_taken[f % 2].sem, 1)

            def filled(b, f):
                act.wait_ge(proj_filled.sem, proj_filled.at(b, f + 1))

            def exps(b, u):
                act.wait_ge(score_taken.sem, score_taken.at(b, u + 1))
                slot = prob[:, u % PROB_RING, :]
                nc.scalar.activation(slot, slot, ACT.Exp, bias=low[:, u:u + 1], scale=-1.0,
                                     accum_out=den[:, u:u + 1]).then_inc(exp_ready.sem, 1)

            def take_transposed(b, w):
                act.wait_ge(pt_filled.sem, pt_filled.at(b, w + 1))
                act.wait_ge(av_done.sem, av_done.at(b, w - PX_RING + 1))
                nc.scalar.copy(pt[:, w % PX_RING, :], ptb[w % 2][:, :]).then_inc(pt_taken[w % 2].sem, 1)

            def take_values(b, m):
                if m == 0:
                    filled(b, WOX)
                act.wait_ge(av_done.sem, av_done.at(b, 4 * m + 4))
                nc.scalar.copy(ox_t[:, m, :], av[m % 2][:, 0:S]).then_inc(av_taken[m % 2].sem, 1)

            def take_x2_t(b):
                filled(b, X2T)
                taken(nc.scalar.copy(x2_t[:].rearrange("p k s -> p (k s)"), proj[X2T % 2][:, :]), X2T)

            def gate_margin(b):
                act.wait_ge(margin_ready.sem, margin_ready.at(b, 1))
                nc.scalar.activation(margin_tanh[:], margin[:], ACT.Tanh, scale=0.5).then_inc(margin_tanh_ready.sem, 1)

            def take_keys_t(b, f, w, bias, n):
                keys = slice(n * S, (n + 1) * S)
                filled(b, f)
                for k in range(KC):
                    ins = nc.scalar.activation(keys_t[n][:, k, :], proj[f % 2][:, k * S:(k + 1) * S], ACT.Identity,
                                               bias=bias[:, k:k + 1], scale=w[:, k:k + 1])
                taken(ins, f)
                act.wait_ge(proj_taken[f % 2].sem, proj_taken[f % 2].at(b, f // 2 + 1))
                nc.scalar.copy(keys_hi[:, :, keys], keys_t[n]).then_inc(keys_hi_ready.sem, 1)

            def take_context(b):
                take_keys_t(b, CT, g1, be1, 0)

            def take_latents(b):
                take_keys_t(b, LT, g2, be2, 1)

            def high_part(b, n):
                f, kind = n // 3, n % 3
                fill = KQ[n]
                act.wait_ge(proj_taken[fill % 2].sem, proj_taken[fill % 2].at(b, fill // 2 + 1))
                act.wait_ge(score_filled.sem, score_filled.at(b, 8 * f + 8))
                for rows, heads in halves(f):
                    ins = nc.scalar.copy(high_of(rows, heads, kind), whole_of(n, rows))
                ins.then_inc(high_ready.sem, 1)

            def take_v(b, f, n, half):
                filled(b, f)
                last = (b, 2 * 8) if half == 0 else (b - 1, UNITS)
                act.wait_ge(av_done.sem, av_done.at(*last))
                taken(nc.scalar.copy(vx[:, n, 512 * half:512 * (half + 1)], proj[f % 2][:, :]), f)

            def part(n):
                return lambda b: high_part(b, n)

            def v_part(fills, n, half):
                return lambda b: take_v(b, fills[n], n, half)

            for s in (exp_ready, margin_tanh_ready, *pt_taken, *av_taken):
                act.sem_inc(s.sem, s.per)
            act.wait_ge(consts, N_CONSTS)
            for hi, w in weights:
                nc.scalar.copy(hi, w).then_inc(weights_hi, 1)
            take_context(-1)
            take_latents(-1)
            for f in range(LT + 1, FILLS):
                if f in KQ:
                    high_part(-1, KQ.index(f))
                elif f in V0[0::2]:
                    take_v(-1, f, V0.index(f), 0)
            steps = {}
            for n, i in enumerate((8, 9, 10, 11, 12, 13, 13, 14, 15, 16, 17, 18)):
                steps.setdefault(i, []).append(part(n))
            for i, more in ((0, v_part(V1, 0, 1)), (2, v_part(V1, 2, 1)), (4, take_context), (5, take_latents), (6, take_x2_t),
                            (9, gate_margin), (14, v_part(V0, 0, 0)), (18, v_part(V0, 2, 0))):
                steps.setdefault(i, []).insert(0, more)
            with act.Fori(0, B) as b:
                for i in range(HEADS + 4):
                    if i < HEADS:
                        for c in range(TC):
                            exps(b, 2 * i + c)
                    if 2 <= i < HEADS + 2:
                        for half in range(2):
                            take_transposed(b, 2 * (i - 2) + half)
                    if i >= 5 and i % 2 == 1:
                        take_values(b, (i - 5) // 2)
                    for part in steps.get(i, ()):
                        part(b)
            take_x2_t(B)
            gate_margin(B)

        @block.vector
        def _(dve):
            def apart(signal, value):
                dve.wait_ge(signal.sem, value)
                dve.sem_inc(passed["dve"], 1)

            def filled(b, f):
                dve.wait_ge(proj_filled.sem, proj_filled.at(b, f + 1))

            def taken(ins, f):
                ins.then_inc(proj_taken[f % 2].sem, 1)

            dve.memset(real[:], 0.0)
            dve.memset(junk_off[:], float(JUNK)).then_inc(consts_v, 1)
            dve.wait_ge(consts, N_CONSTS)
            dve.tensor_scalar(down[:], expert_no[:], -1.0, float(E), ALU.mult, ALU.add)
            dve.tensor_scalar(expert_base[:], expert_no[:], float(REGION), None, ALU.mult).then_inc(consts_v, 1)
            dve.tensor_scalar(next_free[:], expert_no[:], float(REGION), float(JUNK), ALU.mult, ALU.add).then_inc(consts_v, 1)
            dve.wait_ge(consts_v, N_VCONSTS)
            for s in (half_stats, stats_ready):
                dve.sem_inc(s[LN_X2].sem, 1)
            for s in (residual_ready, x2_ready, x2_stored, score_taken, prob_ready, rden_ready, route_steps, margin_steps,
                      margin_ready, either_ready, slot_ready):
                dve.sem_inc(s.sem, s.per)

            def stats(b, ln, sources):
                for c in range(TC):
                    ins = dve.bn_stats(stat[:, ln, c, :], sources[c])
                ins.then_inc(half_stats[ln].sem, 1)
                apart(half_stats[ln], half_stats[ln].at(b, NTH[ln]))
                for c in range(TC):
                    ins = dve.bn_aggr(mv[:, ln, c, :], stat[:, ln, c, :])
                ins.then_inc(stats_ready[ln].sem, 1)

            def normalise(ln, out, src, c):
                return dve.tensor_scalar(out, src, mv[:, ln, c, 0:1], rstd[:, ln, c:c + 1], ALU.subtract, ALU.mult)

            def input_stats(b):
                dve.wait_ge(x1_loaded.sem, x1_loaded.at(b, 16))
                stats(b, LN_LAT, [x1_raw[:, c, :] for c in range(TC)])
                dve.wait_ge(ctx_loaded.sem, ctx_loaded.at(b, 16))
                stats(b, LN_CTX, [ctx_raw[:, c, :] for c in range(TC)])

            def input_normalised(b):
                for ln, n, z, raw, ready in ((LN_LAT, 1, zlat, x1_raw, zlat_ready), (LN_CTX, 0, zctx, ctx_raw, zctx_ready)):
                    dve.wait_ge(rstd_ready[ln].sem, rstd_ready[ln].at(b, NTH[ln]))
                    if not isinstance(b, int):
                        dve.wait_ge(keys_split.sem, keys_split.at(b - 1, n + 1))
                    for c in range(TC):
                        ins = normalise(ln, z[:, c, :], raw[:, c, :], c)
                    ins.then_inc(ready.sem, 1)

            def residual_sum(b):
                dve.wait_ge(again_loaded.sem, again_loaded.at(b, 16))
                filled(b, WOX)
                ins = dve.tensor_tensor(x1_again[:], proj[WOX % 2][:, :].rearrange("p (c d) -> p c d", c=TC), x1_again[:], ALU.add)
                ins.then_inc(residual_ready.sem, 1)
                dve.wait_ge(residual_ready.sem, residual_ready.at(b, 1))
                dve.sem_inc(proj_taken[WOX % 2].sem, 1)
                stats(b, LN_X2, [x1_again[:, c, :] for c in range(TC)])

            def x2_of(b):
                dve.wait_ge(x2_stored.sem, x2_stored.at(b, 0))
                dve.wait_ge(rstd_ready[LN_X2].sem, rstd_ready[LN_X2].at(b, NTH[LN_X2]))
                for c in range(TC):
                    ins = normalise(LN_X2, x2[:, c, :], x1_again[:, c, :], c)
                ins.then_inc(x2_ready.sem, 1)

            def take_part(b, n):
                f = KQ[n]
                if not (isinstance(b, int) and n < WHOLES):
                    dve.wait_ge(low_ready.sem, low_ready.at(b, 2 * (n + 1 - WHOLES)))
                filled(b, f)
                taken(dve.tensor_copy(whole[:, n % WHOLES, :], proj[f % 2][:, :]), f)

            def take_v(b, f, n, half):
                filled(b, f)
                last = (b, 2 * 8) if half == 0 else (b - 1, UNITS)
                dve.wait_ge(av_done.sem, av_done.at(*last))
                taken(dve.tensor_copy(vx[:, n, 512 * half:512 * (half + 1)], proj[f % 2][:, :]), f)

            def spread_mask(b):
                dve.wait_ge(mask_loaded.sem, mask_loaded.at(b, 16))
                dve.wait_ge(score_taken.sem, score_taken.at(b, UNITS))
                dve.tensor_scalar(mask_add[:, 0:S], mask_raw[:].bitcast(U8), 1.0, -MASKED, ALU.subtract, ALU.mult).then_inc(mask_ready.sem, 1)

            def masked_scores(b, u):
                if u == 0:
                    apart(mask_ready, mask_ready.at(b - 1, 1))
                apart(pt_filled, pt_filled.at(b, 2 * ((u - PROB_RING) // 2) + 2))
                apart(score_filled, score_filled.at(b, u + 1))
                dve.tensor_tensor_reduce(prob[:, u % PROB_RING, :], score[u % 2][:, :], mask_add[:, :], -X_SCALE, 3.0e38,
                                         ALU.add, ALU.min, low[:, u:u + 1]).then_inc(score_taken.sem, 1)

            def one_over_sum(b, h):
                dve.wait_ge(exp_ready.sem, exp_ready.at(b, 2 * h + 2))
                dve.reciprocal(rden[:, 2 * h:2 * h + 2], den[:, 2 * h:2 * h + 2]).then_inc(rden_ready.sem, 1)

            def probabilities(b, h):
                dve.wait_ge(rden_ready.sem, rden_ready.at(b, h + 1))
                for u in (2 * h, 2 * h + 1):
                    slot = prob[:, u % PROB_RING, :]
                    ins = dve.tensor_scalar(slot, slot, rden[:, u:u + 1], None, ALU.mult)
                ins.then_inc(prob_ready.sem, 1)

            def best_two(b):
                filled(b, LOGITS)
                taken(dve.tensor_tensor(logit[:], proj[LOGITS % 2][:, 0:TC * E].rearrange("p (c e) -> p c e", c=TC),
                                        br_row.unsqueeze(1).broadcast_to([P, TC, E]), ALU.add), LOGITS)
                apart(proj_taken[LOGITS % 2], proj_taken[LOGITS % 2].at(b, LOGITS // 2 + 1))
                every = [P, TC, E]
                rest = logit
                for j in range(TOP):
                    n = 5 * j
                    dve.tensor_reduce(best[:, :, j], rest[:], AX_X, ALU.max).then_inc(route_steps.sem, 1)
                    dve.wait_ge(route_steps.sem, route_steps.at(b, n + 1))
                    dve.tensor_tensor(is_best[:], rest[:], best[:, :, j].unsqueeze(2).broadcast_to(every), ALU.is_equal).then_inc(route_steps.sem, 1)
                    dve.wait_ge(route_steps.sem, route_steps.at(b, n + 2))
                    dve.tensor_tensor(rank[:], is_best[:], down[:].unsqueeze(1).broadcast_to(every), ALU.mult).then_inc(route_steps.sem, 1)
                    dve.wait_ge(route_steps.sem, route_steps.at(b, n + 3))
                    dve.tensor_reduce(best_rank[:], rank[:], AX_X, ALU.max).then_inc(route_steps.sem, 1)
                    dve.wait_ge(route_steps.sem, route_steps.at(b, n + 4))
                    dve.tensor_tensor(chosen[:, :, j, :], down[:].unsqueeze(1).broadcast_to(every),
                                      best_rank[:].unsqueeze(2).broadcast_to(every), ALU.is_equal).then_inc(route_steps.sem, 1)
                    dve.wait_ge(route_steps.sem, route_steps.at(b, n + 5))
                    if j == 0:
                        dve.scalar_tensor_tensor(out=others[:], in0=chosen[:, :, 0, :], scalar=MASKED, in1=logit[:],
                                                 op0=ALU.mult, op1=ALU.add).then_inc(margin_steps.sem, 1)
                        dve.wait_ge(margin_steps.sem, margin_steps.at(b, 1))
                        rest = others
                dve.tensor_tensor(margin[:], best[:, :, 0], best[:, :, 1], ALU.subtract).then_inc(margin_ready.sem, 1)
                dve.tensor_tensor(either[:], chosen[:, :, 0, :], chosen[:, :, 1, :], ALU.add).then_inc(either_ready.sem, 1)

            def list_places(b):
                dve.wait_ge(margin_tanh_ready.sem, margin_tanh_ready.at(b, 1))
                dve.tensor_scalar(gates[:, b, :, 0], margin_tanh[:], 0.5, 0.5, ALU.mult, ALU.add)
                dve.tensor_scalar(gates[:, b, :, 1], margin_tanh[:], -0.5, 0.5, ALU.mult, ALU.add)
                filled(b, PREFIX)
                dve.tensor_tensor(place[:], proj[PREFIX % 2][:, 0:TC * E].rearrange("p (c e) -> p c e", c=TC),
                                  next_free[:].unsqueeze(1).broadcast_to([P, TC, E]), ALU.add).then_inc(route_steps.sem, 1)
                dve.wait_ge(route_steps.sem, route_steps.at(b, 11))
                taken(dve.scalar_tensor_tensor(out=next_free[:], in0=proj[PREFIX % 2][:, TC * E:(TC + 1) * E],
                                               scalar=real[:, 0:1], in1=next_free[:], op0=ALU.mult, op1=ALU.add), PREFIX)
                dve.tensor_tensor(own_place[:], chosen[:], place[:].unsqueeze(2).broadcast_to([P, TC, TOP, E]),
                                  ALU.mult).then_inc(route_steps.sem, 1)
                dve.wait_ge(route_steps.sem, route_steps.at(b, 12))
                dve.tensor_scalar(next_free[:], next_free[:], junk_off[:, 0:1], None, ALU.subtract)
                dve.tensor_reduce(slot_f[:], own_place[:], AX_X, ALU.add).then_inc(route_steps.sem, 1)
                dve.wait_ge(route_steps.sem, route_steps.at(b, 13))
                dve.wait_ge(scatter_over.sem, scatter_over.at(b, 0))
                dve.tensor_copy(slots[:, b, :, :], slot_f[:])
                dve.tensor_copy(slot_i[:], slot_f[:].rearrange("p c j -> p (c j)")).then_inc(slot_ready.sem, 1)
                dve.memset(real[:], 1.0)
                dve.memset(junk_off[:], 0.0).then_inc(route_steps.sem, 1)

            def part(n):
                return lambda b: take_part(b, n)

            def v_part(fills, n, half):
                return lambda b: take_v(b, fills[n], n, half)

            def last_values(b):
                take_v(b - 1, V0[3], 3, 0)

            spread_mask(-1)
            input_stats(-1)
            input_normalised(-1)
            for n, ((hi, w), lo) in enumerate(zip(weights, weights_lo)):
                dve.wait_ge(weights_hi, n + 1)
                dve.tensor_tensor(lo, w, hi.bitcast(F32), ALU.subtract).then_inc(weights_split, 1)
            for f in range(LT + 1, FILLS):
                if f in KQ:
                    take_part(-1, KQ.index(f))
                elif f == V0[1]:
                    take_v(-1, f, 1, 0)
            steps = {0: [last_values], 1: [v_part(V1, 1, 1), input_stats], 2: [input_normalised], 3: [residual_sum], 4: [v_part(V1, 3, 1), x2_of],
                     7: [part(0)], 8: [part(1), best_two], 9: [part(2)], 10: [part(3), list_places], 11: [part(4)],
                     12: [part(5), part(6)], 13: [part(7)], 14: [part(8)], 15: [part(9)], 16: [v_part(V0, 1, 0), part(10), spread_mask],
                     17: [part(11)]}
            with dve.Fori(0, B) as b:
                for i in range(HEADS + 4):
                    if i < HEADS:
                        masked_scores(b, 2 * i)
                    if 1 <= i <= HEADS:
                        one_over_sum(b, i - 1)
                    if i < HEADS:
                        masked_scores(b, 2 * i + 1)
                    if 1 <= i <= HEADS:
                        probabilities(b, i - 1)
                    for part in steps.get(i, ()):
                        part(b)
            for part in (last_values, residual_sum, x2_of, best_two, list_places):
                part(B)
            dve.wait_ge(route_steps.sem, route_steps.at(B, 14))
            dve.tensor_tensor(counts[:], next_free[:], expert_base[:], ALU.subtract).then_inc(counts_ready, 1)

        @block.tensor
        def _(pe):
            pe.wait_ge(consts, N_CONSTS)
            for s, n in ((proj_filled, CT), (proj_taken[0], (CT + 1) // 2), (proj_taken[1], CT // 2), (score_filled, UNITS),
                         (pt_filled, UNITS), (av_done, UNITS)):
                pe.sem_inc(s.sem, n)
            matmul, transpose = nc.tensor.matmul, nc.tensor.transpose

            def free(b, f):
                pe.wait_ge(proj_taken[f % 2].sem, proj_taken[f % 2].at(b, f // 2))
                return proj[f % 2]

            def in_sbuf(b, f):
                pe.wait_ge(proj_taken[f % 2].sem, proj_taken[f % 2].at(b, f // 2 + 1))

            def full(ins):
                ins.then_inc(proj_filled.sem, 1)

            def project(out, lhs, rhs, chunks):
                for k in range(chunks):
                    ins = matmul(out, lhs(k), rhs(k), start=(k == 0), stop=(k == chunks - 1))
                return ins

            def transposed(b, f, z, ready, value):
                bk_ = free(b, f)
                pe.wait_ge(ready.sem, value)
                for k in range(KC):
                    for c in range(TC):
                        ins = transpose(bk_[:, k * S + c * P:k * S + (c + 1) * P], z[:, c, k * P:(k + 1) * P], ident[:])
                full(ins)

            def context_transposed(b):
                transposed(b, CT, zctx, zctx_ready, zctx_ready.at(b, 1))

            def latents_transposed(b):
                transposed(b, LT, zlat, zlat_ready, zlat_ready.at(b, 1))

            def x2_transposed(b):
                transposed(b, X2T, x2, x2_ready, x2_ready.at(b, 1))

            def project_parts(out, lhs, rhs):
                for k in range(KC):
                    for i, j in ((0, 0), (0, 1), (1, 0)):
                        ins = matmul(out, lhs(i, k), rhs(j, k), start=(k == 0 and i + j == 0), stop=(k == KC - 1 and i == 1))
                return ins

            keys_parts = (keys_hi, keys_lo)

            def chunk_pair(b, f, parts, col0, keys):
                bk_ = free(b, f)
                for i in range(2):
                    m0 = col0 + i * P
                    ins = project_parts(bk_[:, i * S:(i + 1) * S], lambda n, k: parts[n][:, k, m0:m0 + P],
                                        lambda n, k: keys_parts[n][:, k, keys])
                full(ins)

            def keys_of(b, f, n):
                if f == 0:
                    pe.wait_ge(keys_split.sem, keys_split.at(b, n + 1))
                chunk_pair(b, KQ[3 * f + n], (wkv_hi, wkv_lo), 2 * f * P, slice(n * S, (n + 1) * S))

            def queries(b, f):
                chunk_pair(b, KQ[3 * f + 2], (wq_hi, wq_lo), 2 * f * P, slice(S, N_KEYS))

            def values_of(b, fills, n, half):
                bk_ = free(b, fills[n])
                cols = slice(INNER + 512 * half, INNER + 512 * (half + 1))
                full(project_parts(bk_[:, :], lambda i, k: keys_parts[i][:, k, n * P:(n + 1) * P],
                                   lambda i, k: (wkv_hi, wkv_lo)[i][:, k, cols]))

            def output(b):
                bk_ = free(b, WOX)
                for i in range(2):
                    pe.wait_ge(av_taken[i].sem, av_taken[i].at(b - 1, XC // 2))
                for c in range(TC):
                    ins = project(bk_[:, c * D:(c + 1) * D], lambda k: ox_t[:, k, c * P:(c + 1) * P], lambda k: wox[:, k, :], XC)
                full(ins)

            def logits(b):
                bk_ = free(b, LOGITS)
                in_sbuf(b, X2T)
                for c in range(TC):
                    ins = project(bk_[:, c * E:(c + 1) * E], lambda k: x2_t[:, k, c * P:(c + 1) * P],
                                  lambda k: wr_s[:, k, :], KC)
                full(ins)

            def prefixes(b):
                bk_ = free(b, PREFIX)
                pe.wait_ge(either_ready.sem, either_ready.at(b, 1))
                matmul(bk_[:, 0:E], before[:], either[:, 0, :], start=True, stop=True)
                matmul(bk_[:, E:2 * E], ones[:], either[:, 0, :], start=True, stop=False)
                matmul(bk_[:, E:2 * E], before[:], either[:, 1, :], start=False, stop=True)
                matmul(bk_[:, 2 * E:3 * E], ones[:], either[:, 0, :], start=True, stop=False)
                full(matmul(bk_[:, 2 * E:3 * E], ones[:], either[:, 1, :], start=False, stop=True))

            def scores(b, h, c):
                u, m, r = 2 * h + c, h // 2, slice(DH_X * (h % 2), DH_X * (h % 2 + 1))
                pe.wait_ge(score_taken.sem, score_taken.at(b, u - 1))
                if h % 4 == 0 and c == 0:
                    f = h // 4
                    pe.wait_ge(low_ready.sem, low_ready.at(b - 1, 6 * f + 6))
                    pe.wait_ge(spread[f].sem, spread[f].at(b - 1, spread[f].per))
                tokens = slice(c * P, (c + 1) * P)
                matmul(score[u % 2][:, :], q_parts[:, h, tokens], k_twice[:, h, :], start=True, stop=False)
                matmul(score[u % 2][:, :], q_parts[r, h, tokens], k_lo[r, m, :], start=False, stop=True).then_inc(score_filled.sem, 1)

            def transposes(b, h):
                for half in range(2):
                    w = 2 * h + half
                    pe.wait_ge(pt_taken[w % 2].sem, pt_taken[w % 2].at(b, w // 2))
                    if half == 0:
                        pe.wait_ge(prob_ready.sem, prob_ready.at(b, h + 1))
                    for nn in range(2):
                        n = 2 * half + nn
                        for c in range(TC):
                            ins = transpose(ptb[w % 2][:, nn * S + c * P:nn * S + (c + 1) * P],
                                            prob[:, (2 * h + c) % PROB_RING, n * P:(n + 1) * P], ident[:])
                    ins.then_inc(pt_filled.sem, 1)

            def values(b, h):
                m, r = h // 2, slice(DH_X * (h % 2), DH_X * (h % 2 + 1))
                if h == 0:
                    in_sbuf(b - 1, V0[2])
                    in_sbuf(b - 1, V0[3])
                if h == HEADS // 2:
                    in_sbuf(b, V1[2])
                    in_sbuf(b, V1[3])
                if h % 2 == 0:
                    pe.wait_ge(av_taken[m % 2].sem, av_taken[m % 2].at(b, m // 2))
                for half in range(2):
                    w = 2 * h + half
                    pe.wait_ge(pt_taken[w % 2].sem, pt_taken[w % 2].at(b, w // 2 + 1))
                    for nn in range(2):
                        n = 2 * half + nn
                        ins = matmul(av[m % 2][r, 0:S], vx[:, n, DH_X * h:DH_X * (h + 1)],
                                     pt[:, w % PX_RING, nn * S:(nn + 1) * S], start=(n == 0), stop=(n == NC - 1))
                    ins.then_inc(av_done.sem, 1)

            def quad(f):
                return [lambda b: keys_of(b, f, 0), lambda b: keys_of(b, f, 1), lambda b: queries(b, f)]

            def v_parts(fills, half):
                return [lambda b, n=n: values_of(b, fills, n, half) for n in range(NC)]

            def skip(b, f):
                free(b, f)
                in_sbuf(b, f - 1) if f > 0 else in_sbuf(b - 1, FILLS - 1)
                pe.sem_inc(proj_taken[f % 2].sem, 1)
                pe.sem_inc(proj_filled.sem, 1)

            first, second = v_parts(V0, 0), v_parts(V1, 1)
            kq = [part for f in range(QUADS) for part in quad(f)]
            context_transposed(-1)
            latents_transposed(-1)
            pe.wait_ge(weights_split, len(weights))
            for f in range(LT + 1, FILLS):
                if f in KQ:
                    kq[KQ.index(f)](-1)
                elif f in V0:
                    first[V0.index(f)](-1)
                else:
                    skip(-1, f)

            def last_values_and_context(b):
                second[3](b)
                context_transposed(b)

            before_ = {1: second[1], 2: second[2], 4: last_values_and_context, 5: latents_transposed, 6: x2_transposed,
                       8: kq[1], 9: kq[2], 10: kq[3], 11: kq[4], 12: kq[6], 13: kq[7], 14: kq[8], 15: kq[9], 16: kq[10],
                       17: kq[11], 18: first[3]}
            after_ = {0: second[0], 1: output, 6: kq[0], 7: logits, 9: prefixes, 11: kq[5], 13: first[0], 15: first[1],
                      17: first[2]}
            for c in range(TC):
                scores(0, 0, c)
            with pe.Fori(0, B) as b:
                for i in range(HEADS + 3):
                    if i in before_:
                        before_[i](b)
                    if 2 <= i < HEADS + 2:
                        transposes(b, i - 2)
                    if i + 1 < HEADS:
                        for c in range(TC):
                            scores(b, i + 1, c)
                    elif i == HEADS + 1:
                        for c in range(TC):
                            scores(b + 1, 0, c)
                    if i >= 3:
                        values(b, i - 3)
                    if i in after_:
                        after_[i](b)

            rest = {WOX: output, X2T: x2_transposed, LOGITS: logits, PREFIX: prefixes}
            for f in range(PREFIX + 1):
                if f in rest:
                    rest[f](B)
                else:
                    skip(B, f)


def expert_phase(nc, sem, w1, b1, w2, b2, x2_dram, list_dram, out, ident, gates, slots, counts):
    y_dram = nc.dram_tensor("expert_rows", (N_TILES * SLOTS, D), F32).ap()
    HALVES = 2
    with ExitStack() as stack:
        def sb(name, shape, dt=F32):
            return stack.enter_context(nc.sbuf_tensor(name, shape, dt))

        def bank(name):
            return stack.enter_context(nc.psum_tensor(name, [P, 512], F32))

        def sig(name, per, start=None):
            return Signal(sem(name), per, RING * per if start is None else start)

        tile_i = sb("tile_i", [P, N_TILES], I32)
        tile_no = sb("tile_no", [P, N_TILES])
        bound_i = sb("bound_i", [P, MAX_TILES], I32)
        bound = sb("bound", [P, MAX_TILES])
        has_tile = sb("has_tile", [P, E, MAX_TILES])
        tiles_of = sb("tiles_of", [P, E])
        one_e = sb("one_e", [P, E])
        last_tile = sb("last_tile", [P, E])
        is_past = sb("is_past", [P, N_TILES, E])
        past_tiles = sb("past_tiles", [P, N_TILES, E])
        expert_f = sb("expert_f", [P, N_TILES])
        first_f = sb("first_f", [P, N_TILES])
        expert_rows_f = sb("expert_rows_f", [P, N_TILES])
        tile_base = sb("tile_base", [P, N_TILES], I32)
        tile_expert = sb("tile_expert", [P, N_TILES], I32)
        half_e = sb("half_e", [P, TC])
        region_i = sb("region_i", [P, E], I32)
        region = sb("region", [P, E])
        closing = sb("closing", [P, E])
        in_region = sb("in_region", [P, B * TC * TOP, E])
        gaps = sb("gaps", [P, B * TC * TOP, E])
        gap = sb("gap", [P, B * TC * TOP])
        row_no = sb("row_no", [P, B, TC, TOP], I32)
        w1_half, w2_half = ([slice(n * size // HALVES, (n + 1) * size // HALVES) for n in range(HALVES)] for size in (KC, FC))
        w1_s = sb("w1_s", [P, KC, F])
        w2_s = sb("w2_s", [P, FC, D])
        w1_lo = [sb(f"w1_lo{i}", [P, KC, F], F32R) for i in range(RING)]
        w2_lo = [sb(f"w2_lo{i}", [P, FC, D], F32R) for i in range(RING)]
        b1_s = [sb(f"b1_s{i}", [P, FC]) for i in range(RING)]
        b2_s = [sb(f"b2_s{i}", [P, D]) for i in range(RING)]
        w1_hi = [sb(f"w1_hi{i}", [P, KC, F], F32R) for i in range(RING)]
        w2_hi = [sb(f"w2_hi{i}", [P, FC, D], F32R) for i in range(RING)]
        tokens = [sb(f"tokens{i}", [P, SC], I32) for i in range(RING)]
        xg = [sb(f"xg{i}", [P, SC, D]) for i in range(RING)]
        xg_hi = [sb(f"xg_hi{i}", [P, KC, SLOTS], F32R) for i in range(RING)]
        xg_lo = [sb(f"xg_lo{i}", [P, KC, SLOTS], F32R) for i in range(RING)]
        h_lo = sb("h_lo", [P, FC, SLOTS], F32R)
        h_t = sb("h_t", [P, FC, SLOTS])
        h_hi = sb("h_hi", [P, FC, SLOTS], F32R)
        y_s = [sb(f"y_s{i}", [P, SC, D]) for i in range(RING)]
        own_slots = [sb(f"own_slots{q}", [P, TC, TOP], I32) for q in range(2)]
        yb = [sb(f"yb{q}", [P, TC, TOP, D]) for q in range(2)]
        xb = [sb(f"xb{q}", [P, TC, D]) for q in range(2)]
        half_sum = sb("half_sum", [P, TC, D])
        res3 = sb("res3", [P, TC, D])
        stat3 = sb("stat3", [P, TC, 6])
        mv3 = sb("mv3", [P, TC, 2])
        var3 = sb("var3", [P, TC])
        rstd3 = sb("rstd3", [P, TC])
        ob = [sb(f"ob{q}", [P, TC, D]) for q in range(2)]
        xt_bank = bank("xt_bank")
        h_bank = [bank(f"h_bank{i}") for i in range(FC // 2)]
        y_bank = [bank(f"y_bank{i}") for i in range(RING)]

        consts = sem("tile_consts")
        plan = sem("tile_plan")
        passed = {e: sem(f"passed3_{e}") for e in ("pool", "dve", "sp")}
        w1_loaded = [sig(f"w1_loaded{n}", 16, 0) for n in range(HALVES)]
        w2_loaded = [sig(f"w2_loaded{n}", 16, 0) for n in range(HALVES)]
        b1_loaded = [sig(f"b1_loaded{i}", 16, 0) for i in range(RING)]
        b2_loaded = [sig(f"b2_loaded{i}", 16, 0) for i in range(RING)]
        tokens_loaded = [sig(f"tokens_loaded{i}", 16, 0) for i in range(RING)]
        gathered = [sig(f"gathered{i}", 16 * SC, 0) for i in range(RING)]
        y_stored = [Signal(sem(f"y_stored{i}"), 16, 16) for i in range(RING)]
        xt_filled, xt_taken = sig("xt_filled", 1), sig("xt_taken", 1)
        h_filled, h_taken = sig("h_filled", FC // 2), sig("h_taken", FC // 2)
        y_filled, y_taken = sig("y_filled", 1), sig("y_taken", 1)
        xg_hi_ready, w1_hi_ready, w2_hi_ready = sig("xg_hi_ready", 1, 0), sig("w1_hi_ready", HALVES, 0), sig("w2_hi_ready", HALVES, 0)
        w1_split, w2_split = sig("w1_split", HALVES, 0), sig("w2_split", HALVES, 0)
        h_hi_ready, h_split = sig("h_hi_ready", FC // 2, 0), sig("h_split", FC // 2, 0)
        slots_ready = Signal(sem("slots_ready"), 1, 2)
        rows_back = [sig(f"rows_back{q}", 16 * TC * TOP, 0) for q in range(2)]
        xb_loaded = [sig(f"xb_loaded{q}", 16, 0) for q in range(2)]
        out_stored = [Signal(sem(f"out_stored{q}"), 16, 16) for q in range(2)]
        sum_steps = Signal(sem("sum_steps"), 3, 6)
        stats3 = Signal(sem("stats3"), 1, 2)
        var3_ready, rstd3_ready = Signal(sem("var3_ready"), 1, 2), Signal(sem("rstd3_ready"), 1, 2)
        ob_ready = Signal(sem("ob_ready"), 1, 2)
        N_PLAN = 10

        block = stack.enter_context(nc.Block())

        @block.sync
        def _(sp):
            def pass_wait(s, value):
                if not (isinstance(value, int) and value <= 0):
                    sp.wait_ge(s.sem, value)
                    sp.sem_inc(passed["sp"], 1)

            def load_tokens(r, i):
                base = sp.value_load(tile_base[0:1, bass.ds(r * RING + i, 1)], min_val=0, max_val=JUNK - SLOTS)
                pass_wait(gathered[i], gathered[i].at(r, 0))
                sp.dma_start(tokens[i][:], list_dram[bass.ds(base, SLOTS), :].rearrange("(p c) a -> p (c a)", p=P)).then_inc(tokens_loaded[i].sem, 16)

            def load_w1(r, i):
                t = r * RING + i
                e = sp.value_load(tile_expert[0:1, bass.ds(t, 1)], min_val=0, max_val=E - 1)
                for n, part in enumerate(w1_half):
                    pass_wait(w1_split, w1_split.at(t - 1, n + 1))
                    sp.dma_start(w1_s[:, part, :], w1[e].rearrange("(k p) f -> p k f", p=P)[:, part, :]).then_inc(w1_loaded[n].sem, 16)
                sp.dma_start(b1_s[i][:], b1[e]).then_inc(b1_loaded[i].sem, 16)

            def load_w2(r, i):
                t = r * RING + i
                e = sp.value_load(tile_expert[0:1, bass.ds(t, 1)], min_val=0, max_val=E - 1)
                for n, part in enumerate(w2_half):
                    pass_wait(w2_split, w2_split.at(t - 1, n + 1))
                    sp.dma_start(w2_s[:, part, :], w2[e].rearrange("(k p) d -> p k d", p=P)[:, part, :]).then_inc(w2_loaded[n].sem, 16)
                pass_wait(y_taken, y_taken.at(t - RING, 1))
                sp.dma_start(b2_s[i][:], b2[e].broadcast_to([P, D])).then_inc(b2_loaded[i].sem, 16)

            def load(r, i):
                if not (isinstance(r, int) and r * RING + i == N_TILES - 1):
                    load_tokens(r + (i + 1) // RING, (i + 1) % RING)
                    load_w1(r + (i + 1) // RING, (i + 1) % RING)
                load_w2(r, i)

            def store(r, i):
                t = r * RING + i
                pass_wait(y_taken, y_taken.at(t, 1))
                sp.dma_start(y_dram.rearrange("(t p c) d -> t p c d", p=P, c=SC)[t], y_s[i][:]).then_inc(y_stored[i].sem, 16)

            sp.wait_ge(plan, N_PLAN)
            load_tokens(0, 0)
            load_w1(0, 0)
            for i in range(RING):
                load(0, i)
            store(0, 0)

            def load_and_store(r):
                for i in range(RING):
                    load(r, i)
                    store(r - 1 + (i + 1) // RING, (i + 1) % RING)

            with sp.Fori(1, ROUNDS - 1) as r:
                load_and_store(r)
            load_and_store(ROUNDS - 1)
            for i in range(1, RING):
                store(ROUNDS - 1, i)

            x2_rows, out_rows = (a.rearrange("(b c p) d -> b p c d", c=TC, p=P) for a in (x2_dram, out))

            def load_x2(r, q):
                b = 2 * r + q
                if not isinstance(r, int):
                    pass_wait(sum_steps, sum_steps.at(b - 2, 2))
                sp.dma_start(xb[q][:], x2_rows[b + 1]).then_inc(xb_loaded[q].sem, 16)

            def store_out(r, q):
                b = 2 * r + q
                pass_wait(ob_ready, ob_ready.at(b, 1))
                sp.dma_start(out_rows[b], ob[q][:]).then_inc(out_stored[q].sem, 16)

            load_x2(0, 0)
            load_x2(0, 1)
            with sp.Fori(1, B // 2) as r:
                for q in range(2):
                    store_out(r - 1, q)
                    load_x2(r, q)
            for q in range(2):
                store_out(B // 2 - 1, q)
            for q in range(2):
                sp.wait_ge(out_stored[q].sem, out_stored[q].at(B // 2, 0))

        @block.gpsimd
        def _(pool):
            pool.iota(tile_i[:], pattern=[[1, N_TILES]], base=0, channel_multiplier=0).then_inc(consts, 1)
            pool.iota(bound_i[:], pattern=[[SLOTS, MAX_TILES]], base=0, channel_multiplier=0).then_inc(consts, 1)
            pool.memset(half_e[:], -0.5).then_inc(consts, 1)
            pool.iota(region_i[:], pattern=[[REGION, E]], base=0, channel_multiplier=0).then_inc(consts, 1)
            pool.wait_ge(consts, 4)
            pool.tensor_copy(region[:], region_i[:]).then_inc(consts, 1)
            pool.tensor_copy(tile_no[:], tile_i[:]).then_inc(consts, 1)
            pool.tensor_copy(bound[:], bound_i[:]).then_inc(consts, 1)
            pool.sem_inc(var3_ready.sem, var3_ready.start)
            pool.sem_inc(rstd3_ready.sem, rstd3_ready.start)

            def gather(r, i):
                t = r * RING + i
                pool.wait_ge(tokens_loaded[i].sem, tokens_loaded[i].at(r, 16))
                pool.sem_inc(passed["pool"], 1)
                pool.wait_ge(xt_filled.sem, xt_filled.at(t - RING, 1))
                pool.sem_inc(passed["pool"], 1)
                for c in range(SC):
                    pool.indirect_dma_start(xg[i][:, c, :], None, x2_dram, bass.IndirectOffsetOnAxis(
                        ap=tokens[i][:, c:c + 1].bitcast(U32), axis=0)).then_inc(gathered[i].sem, 16)

            def low_w2(r, i):
                t = r * RING + i
                for n, part in enumerate(w2_half):
                    pool.wait_ge(w2_hi_ready.sem, w2_hi_ready.at(t, n + 1))
                    pool.tensor_tensor(w2_lo[i][:, part, :], w2_s[:, part, :], w2_hi[i][:, part, :].bitcast(F32),
                                       ALU.subtract).then_inc(w2_split.sem, 1)

            def ahead(part, r, i, n):
                part(r + (i + n) // RING, (i + n) % RING)

            gather(0, 0)
            gather(0, 1)
            low_w2(0, 0)
            with pool.Fori(0, ROUNDS - 1) as r:
                for i in range(RING):
                    ahead(gather, r, i, 2)
                    ahead(low_w2, r, i, 1)
            gather(ROUNDS - 1, 2)
            low_w2(ROUNDS - 1, 1)
            low_w2(ROUNDS - 1, 2)
            for i in range(RING):
                pool.wait_ge(y_stored[i].sem, y_stored[i].at(ROUNDS, 0))

            def rows(r, q):
                b = 2 * r + q
                pool.wait_ge(slots_ready.sem, slots_ready.at(b, 1))
                pool.sem_inc(passed["pool"], 1)
                pool.wait_ge(sum_steps.sem, sum_steps.at(b - 2, 2))
                pool.sem_inc(passed["pool"], 1)
                for c in range(TC):
                    for j in range(TOP):
                        pool.indirect_dma_start(yb[q][:, c, j, :], None, y_dram, bass.IndirectOffsetOnAxis(
                            ap=own_slots[q][:, c, j:j + 1].bitcast(U32), axis=0)).then_inc(rows_back[q].sem, 16)

            def reciprocal_root(b):
                pool.wait_ge(stats3.sem, stats3.at(b, 1))
                pool.sem_inc(passed["pool"], 1)
                pool.tensor_scalar(var3[:], mv3[:, :, 1], EPS, None, ALU.add).then_inc(var3_ready.sem, 1)
                pool.wait_ge(var3_ready.sem, var3_ready.at(b, 1))
                pool.tensor_tensor(rstd3[:], var3[:], half_e[:], ALU.pow).then_inc(rstd3_ready.sem, 1)

            rows(0, 0)
            with pool.Fori(0, B // 2 - 1) as r:
                rows(r, 1)
                reciprocal_root(2 * r)
                rows(r + 1, 0)
                reciprocal_root(2 * r + 1)
            rows(B // 2 - 1, 1)
            reciprocal_root(B - 2)
            reciprocal_root(B - 1)

        @block.scalar
        def _(act):
            act.sem_inc(h_taken.sem, h_taken.start)

            def gelus(r, i):
                t = r * RING + i
                act.wait_ge(b1_loaded[i].sem, b1_loaded[i].at(r, 16))
                act.wait_ge(y_filled.sem, y_filled.at(t - 1, 1))
                for m in range(FC // 2):
                    act.wait_ge(h_filled.sem, h_filled.at(t, m + 1))
                    for n in range(2):
                        f = 2 * m + n
                        ins = nc.scalar.activation(h_t[:, f, :], h_bank[m][:, n * SLOTS:(n + 1) * SLOTS], ACT.Gelu,
                                                   bias=b1_s[i][:, f:f + 1])
                    ins.then_inc(h_taken.sem, 1)
                    act.wait_ge(h_taken.sem, h_taken.at(t, m + 1))
                    nc.scalar.copy(h_hi[:, 2 * m:2 * m + 2, :], h_t[:, 2 * m:2 * m + 2, :]).then_inc(h_hi_ready.sem, 1)

            def high_rows(r, i):
                t = r * RING + i
                act.wait_ge(xt_filled.sem, xt_filled.at(t, 1))
                act.wait_ge(h_filled.sem, h_filled.at(t - RING, FC // 2))
                nc.scalar.copy(xg_hi[i][:].rearrange("p k s -> p (k s)"), xt_bank[:, :]).then_inc(xg_hi_ready.sem, 1)

            def high_w1(r, i):
                t = r * RING + i
                act.wait_ge(h_filled.sem, h_filled.at(t - RING, FC // 2))
                for n, part in enumerate(w1_half):
                    act.wait_ge(w1_loaded[n].sem, w1_loaded[n].at(t, 16))
                    nc.scalar.copy(w1_hi[i][:, part, :], w1_s[:, part, :]).then_inc(w1_hi_ready.sem, 1)

            def ahead(part, r, i, n):
                part(r + (i + n) // RING, (i + n) % RING)

            high_rows(0, 0)
            high_w1(0, 0)
            high_w1(0, 1)
            with act.Fori(0, ROUNDS - 1) as r:
                for i in range(RING):
                    gelus(r, i)
                    ahead(high_rows, r, i, 1)
                    ahead(high_w1, r, i, 2)
            gelus(ROUNDS - 1, 0)
            high_rows(ROUNDS - 1, 1)
            high_w1(ROUNDS - 1, 2)
            gelus(ROUNDS - 1, 1)
            high_rows(ROUNDS - 1, 2)
            gelus(ROUNDS - 1, 2)

        @block.vector
        def _(dve):
            def apart(s, value):
                dve.wait_ge(s.sem, value)
                dve.sem_inc(passed["dve"], 1)

            def step(ins, n):
                ins.then_inc(plan, 1)
                dve.wait_ge(plan, n)

            dve.wait_ge(consts, 7)
            dve.memset(one_e[:], 1.0)
            step(dve.tensor_tensor(has_tile[:], counts[:].unsqueeze(2).broadcast_to([P, E, MAX_TILES]),
                                   bound[:].unsqueeze(1).broadcast_to([P, E, MAX_TILES]), ALU.is_gt), 1)
            step(dve.tensor_reduce(tiles_of[:], has_tile[:], AX_X, ALU.add), 2)
            step(dve.tensor_tensor_scan(last_tile[:], one_e[:], tiles_of[:], 0.0, ALU.mult, ALU.add), 3)
            step(dve.tensor_tensor(is_past[:], tile_no[:].unsqueeze(2).broadcast_to([P, N_TILES, E]),
                                   last_tile[:].unsqueeze(1).broadcast_to([P, N_TILES, E]), ALU.is_ge), 4)
            step(dve.tensor_tensor(past_tiles[:], is_past[:], tiles_of[:].unsqueeze(1).broadcast_to([P, N_TILES, E]),
                                   ALU.mult), 5)
            step(dve.tensor_reduce(expert_f[:], is_past[:], AX_X, ALU.add), 6)
            step(dve.tensor_reduce(first_f[:], past_tiles[:], AX_X, ALU.add), 7)
            dve.tensor_scalar(expert_rows_f[:], expert_f[:], float(REGION), None, ALU.mult)
            step(dve.tensor_tensor(first_f[:], tile_no[:], first_f[:], ALU.subtract), 8)
            dve.tensor_scalar(tile_expert[:], expert_f[:], float(E - 1), None, ALU.min)
            step(dve.scalar_tensor_tensor(out=expert_rows_f[:], in0=first_f[:], scalar=float(SLOTS), in1=expert_rows_f[:],
                                          op0=ALU.mult, op1=ALU.add), 9)
            dve.tensor_copy(tile_base[:], expert_rows_f[:]).then_inc(plan, 1)
            own = slots[:, 1:B + 1, :, :].rearrange("p b c j -> p (b c j)")
            dve.memset(closing[:, 0:1], 0.0)
            dve.tensor_scalar(closing[:, 1:E], tiles_of[:, 0:E - 1], float(SLOTS), float(REGION), ALU.mult, ALU.subtract)
            step(dve.tensor_tensor(in_region[:], own.unsqueeze(2).broadcast_to([P, B * TC * TOP, E]),
                                   region[:].unsqueeze(1).broadcast_to([P, B * TC * TOP, E]), ALU.is_ge), 11)
            step(dve.tensor_tensor(gaps[:], in_region[:], closing[:].unsqueeze(1).broadcast_to([P, B * TC * TOP, E]),
                                   ALU.mult), 12)
            step(dve.tensor_reduce(gap[:], gaps[:], AX_X, ALU.add), 13)
            step(dve.tensor_tensor(row_no[:].rearrange("p b c j -> p (b c j)"), own, gap[:], ALU.add), 14)
            for s in (xt_taken, y_taken, slots_ready, sum_steps, stats3, ob_ready, *y_stored, *out_stored):
                dve.sem_inc(s.sem, s.start)

            def low_rows(r, i):
                t = r * RING + i
                dve.wait_ge(xg_hi_ready.sem, xg_hi_ready.at(t, 1))
                dve.tensor_tensor(xg_lo[i][:].rearrange("p k s -> p (k s)"), xt_bank[:, :],
                                  xg_hi[i][:].bitcast(F32).rearrange("p k s -> p (k s)"), ALU.subtract).then_inc(xt_taken.sem, 1)

            def high_w2(r, i):
                t = r * RING + i
                dve.wait_ge(y_filled.sem, y_filled.at(t - RING, 1))
                for n, part in enumerate(w2_half):
                    dve.wait_ge(w2_loaded[n].sem, w2_loaded[n].at(t, 16))
                    dve.tensor_copy(w2_hi[i][:, part, :], w2_s[:, part, :]).then_inc(w2_hi_ready.sem, 1)

            def low_w1(r, i):
                t = r * RING + i
                for n, part in enumerate(w1_half):
                    dve.wait_ge(w1_hi_ready.sem, w1_hi_ready.at(t, n + 1))
                    dve.tensor_tensor(w1_lo[i][:, part, :], w1_s[:, part, :], w1_hi[i][:, part, :].bitcast(F32),
                                      ALU.subtract).then_inc(w1_split.sem, 1)

            def low_hidden(r, i):
                t = r * RING + i
                for m in range(FC // 2):
                    f = slice(2 * m, 2 * m + 2)
                    dve.wait_ge(h_hi_ready.sem, h_hi_ready.at(t, m + 1))
                    dve.tensor_tensor(h_lo[:, f, :], h_t[:, f, :], h_hi[:, f, :].bitcast(F32), ALU.subtract).then_inc(h_split.sem, 1)

            def take_y(r, i):
                t = r * RING + i
                dve.wait_ge(b2_loaded[i].sem, b2_loaded[i].at(r, 16))
                dve.wait_ge(y_stored[i].sem, y_stored[i].at(r, 0))
                dve.wait_ge(y_filled.sem, y_filled.at(t, 1))
                dve.tensor_tensor(y_s[i][:], y_bank[i][:, :].rearrange("p (c d) -> p c d", c=SC),
                                  b2_s[i][:].unsqueeze(1).broadcast_to([P, SC, D]), ALU.add).then_inc(y_taken.sem, 1)

            def ahead(part, r, i, n):
                part(r + (i + n) // RING, (i + n) % RING)

            low_w1(0, 0)
            low_rows(0, 0)
            high_w2(0, 0)
            low_w1(0, 1)
            with dve.Fori(0, ROUNDS - 1) as r:
                for i in range(RING):
                    low_hidden(r, i)
                    ahead(low_rows, r, i, 1)
                    ahead(high_w2, r, i, 1)
                    ahead(low_w1, r, i, 2)
                    take_y(r, i)
            for i in range(RING):
                low_hidden(ROUNDS - 1, i)
                if i + 1 < RING:
                    low_rows(ROUNDS - 1, i + 1)
                    high_w2(ROUNDS - 1, i + 1)
                if i + 2 < RING:
                    low_w1(ROUNDS - 1, i + 2)
                take_y(ROUNDS - 1, i)

            def places(r, q):
                b = 2 * r + q
                dve.tensor_copy(own_slots[q][:], row_no[:, b, :, :] if isinstance(b, int) else
                                row_no[:, bass.ds(b, 1), :, :].rearrange("p o c j -> p (o c) j")).then_inc(slots_ready.sem, 1)

            def combine(r, q, last=False):
                b = 2 * r + q
                g = gates[:, b + 1, :, :] if isinstance(b, int) else gates[:, bass.ds(b + 1, 1), :, :].rearrange("p o c j -> p (o c) j")
                dve.wait_ge(xb_loaded[q].sem, xb_loaded[q].at(r, 16))
                dve.wait_ge(rows_back[q].sem, rows_back[q].at(r, rows_back[q].per))
                for c in range(TC):
                    ins = dve.scalar_tensor_tensor(out=half_sum[:, c, :], in0=yb[q][:, c, 0, :], scalar=g[:, c, 0:1],
                                                   in1=xb[q][:, c, :], op0=ALU.mult, op1=ALU.add)
                ins.then_inc(sum_steps.sem, 1)
                dve.wait_ge(sum_steps.sem, sum_steps.at(b, 1))
                for c in range(TC):
                    ins = dve.scalar_tensor_tensor(out=res3[:, c, :], in0=yb[q][:, c, 1, :], scalar=g[:, c, 1:2],
                                                   in1=half_sum[:, c, :], op0=ALU.mult, op1=ALU.add)
                ins.then_inc(sum_steps.sem, 1)
                if not last:
                    places(r + 1, q)
                dve.wait_ge(sum_steps.sem, sum_steps.at(b, 2))
                for c in range(TC):
                    ins = dve.bn_stats(stat3[:, c, :], res3[:, c, :])
                ins.then_inc(sum_steps.sem, 1)
                apart(sum_steps, sum_steps.at(b, 3))
                for c in range(TC):
                    ins = dve.bn_aggr(mv3[:, c, :], stat3[:, c, :])
                ins.then_inc(stats3.sem, 1)
                dve.wait_ge(out_stored[q].sem, out_stored[q].at(r, 0))
                dve.wait_ge(rstd3_ready.sem, rstd3_ready.at(b, 1))
                for c in range(TC):
                    ins = dve.tensor_scalar(ob[q][:, c, :], res3[:, c, :], mv3[:, c, 0:1], rstd3[:, c:c + 1],
                                            ALU.subtract, ALU.mult)
                ins.then_inc(ob_ready.sem, 1)

            for q in range(2):
                places(0, q)
            with dve.Fori(0, B // 2 - 1) as r:
                for q in range(2):
                    combine(r, q)
            for q in range(2):
                combine(B // 2 - 1, q, last=True)

        @block.tensor
        def _(pe):
            for s in (xt_filled, h_filled, y_filled):
                pe.sem_inc(s.sem, s.start)
            matmul, transpose = nc.tensor.matmul, nc.tensor.transpose

            def rows_transposed(r, i):
                t = r * RING + i
                pe.wait_ge(gathered[i].sem, gathered[i].at(r, gathered[i].per))
                pe.wait_ge(xt_taken.sem, xt_taken.at(t - 1, 1))
                for k in range(KC):
                    for c in range(SC):
                        ins = transpose(xt_bank[:, k * SLOTS + c * P:k * SLOTS + (c + 1) * P],
                                        xg[i][:, c, k * P:(k + 1) * P], ident[:])
                ins.then_inc(xt_filled.sem, 1)

            part_pairs = ((0, 0), (0, 1), (1, 0))

            def first_product(r, i):
                t = r * RING + i
                w, xs = (w1_hi[i], w1_lo[i]), (xg_hi[i], xg_lo[i])
                pe.wait_ge(w1_split.sem, w1_split.at(t, HALVES))
                pe.wait_ge(xt_taken.sem, xt_taken.at(t, 1))
                for m in range(FC // 2):
                    pe.wait_ge(h_taken.sem, h_taken.at(t - 1, m + 1))
                    for n in range(2):
                        f = 2 * m + n
                        for k in range(KC):
                            for a, z in part_pairs:
                                ins = matmul(h_bank[m][:, n * SLOTS:(n + 1) * SLOTS], w[a][:, k, f * P:(f + 1) * P],
                                             xs[z][:, k, :], start=(k == 0 and a + z == 0), stop=(k == KC - 1 and a == 1))
                    ins.then_inc(h_filled.sem, 1)

            def second_product(r, i):
                t = r * RING + i
                h, w = (h_hi, h_lo), (w2_hi[i], w2_lo[i])
                pe.wait_ge(w2_split.sem, w2_split.at(t, HALVES))
                pe.wait_ge(y_taken.sem, y_taken.at(t - RING, 1))
                for c in range(SC):
                    for f in range(FC):
                        if c == 0 and f % 2 == 0:
                            pe.wait_ge(h_split.sem, h_split.at(t, f // 2 + 1))
                        for a, z in part_pairs:
                            ins = matmul(y_bank[i][:, c * D:(c + 1) * D], h[a][:, f, c * P:(c + 1) * P], w[z][:, f, :],
                                         start=(f == 0 and a + z == 0), stop=(f == FC - 1 and a == 1))
                ins.then_inc(y_filled.sem, 1)

            rows_transposed(0, 0)
            with pe.Fori(0, ROUNDS - 1) as r:
                for i in range(RING):
                    first_product(r, i)
                    rows_transposed(r + (i + 1) // RING, (i + 1) % RING)
                    second_product(r, i)
            for i in range(RING):
                first_product(ROUNDS - 1, i)
                if i + 1 < RING:
                    rows_transposed(ROUNDS - 1, i + 1)
                second_product(ROUNDS - 1, i)


def kernel(**inputs):
    from concourse import bacc
    from concourse.bass_utils import run_bass_kernel_spmd

    def a(name):
        return np.asarray(inputs[name])

    def by_partition(v):
        return np.ascontiguousarray(v.reshape(-1, P).T)

    b_in = a("L0_attn_b_in")
    smear, scale = a("L0_attn_smear_factor"), a("L0_attn_log_scale")
    heads_rows = np.concatenate([smear.reshape(EC, HPC).T, scale.reshape(EC, HPC).T], axis=1)
    arrays = {
        "x": a("x"),
        "ctx": a("ctx_1024"),
        "mask": np.ascontiguousarray(a("mask_BxS2_bk0")).reshape(B, 1, S).view(np.int32),
        "w_in_t": a("L0_attn_W_in").T,
        "w_out_t": a("L0_attn_W_out").T,
        "wq": a("L0_xattn_Wq"),
        "wkv": a("L0_xattn_Wkv"),
        "wout": a("L0_xattn_Wout"),
        "cols": np.concatenate([by_partition(v) for v in (
            a("L0_attn_in_ln_w"), a("L0_attn_in_ln_b"), b_in[0:D_EXP], b_in[D_EXP:2 * D_EXP],
            b_in[3 * D_EXP:4 * D_EXP], a("L0_xattn_g1"), a("L0_xattn_b1"), a("L0_xattn_g2"), a("L0_xattn_b2"),
            b_in[2 * D_EXP:3 * D_EXP])], axis=1),
        "rows": np.concatenate([a("L0_attn_out_ln_w"), a("L0_attn_out_ln_b"),
                                a("L0_ffn_br")])[None, :],
        "heads_rows": heads_rows,
        "y_bias": b_in[4 * D_EXP:][:, None],
        "wr": a("L0_ffn_Wr"),
        "w1": a("L0_ffn_W1"),
        "b1": a("L0_ffn_b1").reshape(E, FC, P).transpose(0, 2, 1),
        "w2": a("L0_ffn_W2"),
        "b2": a("L0_ffn_b2").reshape(E, 1, D),
    }
    arrays = {k: np.ascontiguousarray(v) for k, v in arrays.items()}
    nc = bacc.Bacc("TRN2", target_bir_lowering=False, num_devices=1)
    args = [nc.dram_tensor(k, v.shape, mybir.dt.from_np(v.dtype), kind="ExternalInput").ap() for k, v in arrays.items()]
    out = nc.dram_tensor("y", (T, D), F32, kind="ExternalOutput").ap()
    decoder_layer(nc, *args, out)
    r = run_bass_kernel_spmd(nc, [arrays], core_ids=[0])
    return r.results[0]["y"].reshape(B, S, D)
```
